# Optimizing a Trainium2 kernel written in Bass

```python
import numpy as np
import jax
import jax.numpy as jnp

def _softmax(x, axis=-1):
    return jax.nn.softmax(x, axis=axis)

def _gelu(x):
    return jax.nn.gelu(x, approximate=True)

def _silu(x):
    return jax.nn.silu(x)

def _sigmoid(x):
    return jax.nn.sigmoid(x)

def _layernorm(x, axis=-1, eps=1e-05):
    m = jnp.mean(x, axis=axis, keepdims=True)
    v = jnp.var(x, axis=axis, keepdims=True)
    return (x - m) / jnp.sqrt(v + eps)

def _scatter_add(tgt, idx, src, axis=0):
    return tgt.at[idx].add(src)

def _segment_sum(src, seg, n):
    return jax.ops.segment_sum(src, seg, n)
kernel_name = 'mk_adj_resnorm_d4_adj_r2_b270b2'

def setup_inputs(seed: int=0):
    np.random.seed(seed)
    _w = jnp.asarray

    def _rec_inputs():
        import jax
        import jax.numpy as jnp
        _gk = jax.random.key(seed)
        x = -0.000125 + 0.9999 * jax.random.normal(jax.random.fold_in(_gk, 1), (32, 256, 256), jnp.float32)
        _a = jax.random.bernoulli(jax.random.fold_in(_gk, 2), 0.015625, (256, 256))
        _a = jnp.logical_or(_a, jnp.swapaxes(_a, -1, -2))
        _a = jnp.logical_or(_a, jnp.eye(256, dtype=bool))
        _af = _a.astype(jnp.float32)
        adj = _af
        return (x, adj)
    x, adj = _rec_inputs()

    def _L0_gnn_setup():
        import jax, jax.numpy as jnp
        import numpy as np
        ALPHA = 0.2
        key = jax.random.key(seed)
        k0, k1, k2, k3 = jax.random.split(key, 4)
        B, N, C, F = (64, 512, 256, 256)
        x = jax.random.normal(k0, (B, N, C), dtype=jnp.float32)
        W = jax.random.normal(k1, (C, F), dtype=jnp.float32) * (1.414 / np.sqrt(C + F))
        a = jax.random.normal(k2, (2 * F, 1), dtype=jnp.float32) * (1.414 / np.sqrt(2 * F + 1))
        beta = jnp.ones((1,), dtype=jnp.float32)
        mask = (jax.random.uniform(k3, (N, N)) < 0.3).astype(jnp.float32)
        return {'x': x, 'W': W, 'a': a, 'beta': beta, 'mask': mask}
    _L0_gnn_all = _L0_gnn_setup()
    _L0_gnn_in = {k: v for k, v in _L0_gnn_all.items() if k in ('W', 'a', 'beta')}
    del _L0_gnn_all

    def _L1_gnn_setup():
        import jax, jax.numpy as jnp
        import numpy as np
        B, N, D = (8, 1024, 256)
        key = jax.random.key(seed)
        k1, k2, k3, k4, k5 = jax.random.split(key, 5)
        neuron_states = jax.random.normal(k1, (B, N, D), dtype=jnp.float32)
        adjacency = jax.random.randint(k2, (N, N), 0, 2).astype(jnp.float32)
        scale = 1.0 / np.sqrt(D)
        Wq = jax.random.normal(k3, (D, D), dtype=jnp.float32) * scale
        Wk = jax.random.normal(k4, (D, D), dtype=jnp.float32) * scale
        Wv = jax.random.normal(k5, (D, D), dtype=jnp.float32) * scale
        return {'neuron_states': neuron_states, 'adjacency': adjacency, 'Wq': Wq, 'Wk': Wk, 'Wv': Wv}
    _L1_gnn_all = _L1_gnn_setup()
    _L1_gnn_in = {k: v for k, v in _L1_gnn_all.items() if k in ('Wq', 'Wk', 'Wv')}
    del _L1_gnn_all

    def _L2_gnn_setup():
        import jax, jax.numpy as jnp
        import numpy as np
        B, N, F_IN, F_OUT = (16, 1024, 256, 256)
        key = jax.random.key(seed)
        k1, k2, k3 = jax.random.split(key, 3)
        x = jax.random.normal(k1, (B, N, F_IN), dtype=jnp.float32)
        adj = jax.random.uniform(k2, (N, N), dtype=jnp.float32)
        bound = np.sqrt(6.0 / F_OUT)
        weight = jax.random.uniform(k3, (F_IN, F_OUT), dtype=jnp.float32, minval=-bound, maxval=bound)
        bias = jnp.zeros((F_OUT,), dtype=jnp.float32)
        return {'x': x, 'adj': adj, 'weight': weight, 'bias': bias}
    _L2_gnn_all = _L2_gnn_setup()
    _L2_gnn_in = {k: v for k, v in _L2_gnn_all.items() if k in ('weight', 'bias')}
    del _L2_gnn_all

    def _L3_gnn_setup():
        import jax, jax.numpy as jnp
        import numpy as np
        B, N, D, T = (64, 128, 256, 3)

        def _lin(v, W, b):
            return jnp.einsum('...i,oi->...o', v, W) + b
        key = jax.random.key(seed)
        ks = jax.random.split(key, 12)
        s2 = 1.0 / np.sqrt(2 * D)
        s1 = 1.0 / np.sqrt(D)
        return {'x': jax.random.normal(ks[0], (B, N, D), jnp.float32), 'in_mat': jax.random.uniform(ks[1], (N, N), jnp.float32) / N, 'out_mat': jax.random.uniform(ks[2], (N, N), jnp.float32) / N, 'w3_w': jax.random.normal(ks[3], (D, 2 * D), jnp.float32) * s2, 'w3_b': jnp.zeros((D,), jnp.float32), 'u3_w': jax.random.normal(ks[4], (D, D), jnp.float32) * s1, 'u3_b': jnp.zeros((D,), jnp.float32), 'w4_w': jax.random.normal(ks[5], (D, 2 * D), jnp.float32) * s2, 'w4_b': jnp.zeros((D,), jnp.float32), 'w5_w': jax.random.normal(ks[6], (D, 2 * D), jnp.float32) * s2, 'w5_b': jnp.zeros((D,), jnp.float32), 'u5_w': jax.random.normal(ks[7], (D, D), jnp.float32) * s1, 'u5_b': jnp.zeros((D,), jnp.float32)}
    _L3_gnn_all = _L3_gnn_setup()
    _L3_gnn_in = {k: v for k, v in _L3_gnn_all.items() if k in ('w3_w', 'w3_b', 'u3_w', 'u3_b', 'w4_w', 'w4_b', 'w5_w', 'w5_b', 'u5_w', 'u5_b')}
    del _L3_gnn_all
    return {'x': x, 'adj': adj, 'L0_gnn_W': _L0_gnn_in['W'], 'L0_gnn_a': _L0_gnn_in['a'], 'L0_gnn_beta': _L0_gnn_in['beta'], 'L1_gnn_Wq': _L1_gnn_in['Wq'], 'L1_gnn_Wk': _L1_gnn_in['Wk'], 'L1_gnn_Wv': _L1_gnn_in['Wv'], 'L2_gnn_weight': _L2_gnn_in['weight'], 'L2_gnn_bias': _L2_gnn_in['bias'], 'L3_gnn_w3_w': _L3_gnn_in['w3_w'], 'L3_gnn_w3_b': _L3_gnn_in['w3_b'], 'L3_gnn_u3_w': _L3_gnn_in['u3_w'], 'L3_gnn_u3_b': _L3_gnn_in['u3_b'], 'L3_gnn_w4_w': _L3_gnn_in['w4_w'], 'L3_gnn_w4_b': _L3_gnn_in['w4_b'], 'L3_gnn_w5_w': _L3_gnn_in['w5_w'], 'L3_gnn_w5_b': _L3_gnn_in['w5_b'], 'L3_gnn_u5_w': _L3_gnn_in['u5_w'], 'L3_gnn_u5_b': _L3_gnn_in['u5_b']}

def reference(x, adj, L0_gnn_W, L0_gnn_a, L0_gnn_beta, L1_gnn_Wq, L1_gnn_Wk, L1_gnn_Wv, L2_gnn_weight, L2_gnn_bias, L3_gnn_w3_w, L3_gnn_w3_b, L3_gnn_u3_w, L3_gnn_u3_b, L3_gnn_w4_w, L3_gnn_w4_b, L3_gnn_w5_w, L3_gnn_w5_b, L3_gnn_u5_w, L3_gnn_u5_b):
    import jax
    import jax.numpy as jnp

    def _L0_gnn_ref(x, W, a, beta, mask):
        import jax, jax.numpy as jnp
        import numpy as np
        ALPHA = 0.2
        F_ = W.shape[1]
        h = jnp.einsum('bnc,cf->bnf', x, W)
        a1, a2 = (a[:F_, 0], a[F_:, 0])
        s1 = jnp.einsum('bnf,f->bn', h, a1)
        s2 = jnp.einsum('bnf,f->bn', h, a2)
        e = jax.nn.leaky_relu(s1[:, :, None] + s2[:, None, :], negative_slope=ALPHA)
        e = e * mask[None, :, :]
        att = jax.nn.softmax(e, axis=2)
        h_prime = jnp.einsum('bij,bjf->bif', att, h)
        return jax.nn.elu(h_prime + beta * h)

    def _L1_gnn_ref(neuron_states, adjacency, Wq, Wk, Wv):
        import jax, jax.numpy as jnp
        import numpy as np
        B, N, D = (8, 1024, 256)
        q = jnp.einsum('bnd,ed->bne', neuron_states, Wq)
        k = jnp.einsum('bnd,ed->bne', neuron_states, Wk)
        v = jnp.einsum('bnd,ed->bne', neuron_states, Wv)
        rel = jnp.einsum('bnd,bmd->bnm', q, k)
        rel = adjacency.T[None, :, :] * rel
        rel = rel / jnp.linalg.norm(rel, axis=2, keepdims=True)
        return jnp.einsum('bnm,bmd->bnd', rel, v)

    def _L2_gnn_ref(x, adj, weight, bias):
        import jax, jax.numpy as jnp
        import numpy as np
        B, N, F_IN, F_OUT = (16, 1024, 256, 256)
        deg = adj.sum(axis=1)
        deg_inv_sqrt = jnp.where(deg > 0, jax.lax.rsqrt(deg), 0.0)
        norm_adj = adj * deg_inv_sqrt[:, None] * deg_inv_sqrt[None, :]
        support = jnp.einsum('bni,io->bno', x, weight)
        output = jnp.einsum('nm,bmo->bno', norm_adj, support)
        return output + bias

    def _L3_gnn_ref(x, in_mat, out_mat, w3_w, w3_b, u3_w, u3_b, w4_w, w4_b, w5_w, w5_b, u5_w, u5_b):
        import jax, jax.numpy as jnp
        import numpy as np
        B, N, D, T = (64, 128, 256, 3)

        def _lin(v, W, b):
            return jnp.einsum('...i,oi->...o', v, W) + b
        h = x
        for _ in range(T):
            a_in = jnp.einsum('nm,bmd->bnd', in_mat, h)
            a_out = jnp.einsum('nm,bmd->bnd', out_mat, h)
            av = jnp.concatenate([a_in, a_out], axis=-1)
            z = jax.nn.sigmoid(_lin(av, w3_w, w3_b) + _lin(h, u3_w, u3_b))
            r = jax.nn.sigmoid(_lin(av, w4_w, w4_b) + _lin(h, u3_w, u3_b))
            hv = jnp.tanh(_lin(av, w5_w, w5_b) + _lin(r * h, u5_w, u5_b))
            h = (1.0 - z) * h + z * hv
        return h
    x = _layernorm(x + _L0_gnn_ref(x, L0_gnn_W, L0_gnn_a, L0_gnn_beta, adj), axis=-1)
    x = _layernorm(x + _L1_gnn_ref(x, adj, L1_gnn_Wq, L1_gnn_Wk, L1_gnn_Wv), axis=-1)
    x = _layernorm(x + _L2_gnn_ref(x, adj, L2_gnn_weight, L2_gnn_bias), axis=-1)
    x = _layernorm(x + _L3_gnn_ref(x, adj, adj, L3_gnn_w3_w, L3_gnn_w3_b, L3_gnn_u3_w, L3_gnn_u3_b, L3_gnn_w4_w, L3_gnn_w4_b, L3_gnn_w5_w, L3_gnn_w5_b, L3_gnn_u5_w, L3_gnn_u5_b), axis=-1)
    return x

_drawn_inputs = setup_inputs


def setup_inputs(seed=0):
    import zlib

    import numpy as np

    out = dict(_drawn_inputs(seed))
    spreads = {'L2_gnn_bias': (0.0, 0.1),
     'L3_gnn_w3_b': (0.0, 0.284),
     'L3_gnn_u3_b': (0.0, 0.285),
     'L3_gnn_w4_b': (0.0, 2.0),
     'L3_gnn_w5_b': (0.0, 0.1),
     'L3_gnn_u5_b': (0.0, 0.1)}
    factors = {}
    for name, (base, spread) in spreads.items():
        noise = np.random.default_rng([zlib.crc32(name.encode()), seed]).standard_normal(out[name].shape)
        drawn = base * np.exp(spread * noise) if base else spread * noise
        out[name] = jnp.asarray(drawn.astype(out[name].dtype))
    for name, factor in factors.items():
        out[name] = (out[name] * factor).astype(out[name].dtype)
    return out
```

```python
from contextlib import ExitStack

import concourse.bass as bass
from concourse import mybir

P = 128
ALU = mybir.AluOpType
ACT = mybir.ActivationFunctionType
F32 = mybir.dt.float32
F32R = mybir.dt.float32r

B, N, D = 32, 256, 256
BG = 2
G = B // BG
T = 3
NT, DT = N // P, D // P
SLOPE = 0.2
EPS = 1e-5



def four_layer_gnn_kernel(
    nc: bass.Bass,
    x: bass.AP,
    adj: bass.AP,
    W0: bass.AP,
    a0: bass.AP,
    beta: bass.AP,
    Wq: bass.AP,
    Wk: bass.AP,
    Wv: bass.AP,
    W2: bass.AP,
    bias2: bass.AP,
    w3_w: bass.AP,
    w3_b: bass.AP,
    u3_w: bass.AP,
    u3_b: bass.AP,
    w4_w: bass.AP,
    w4_b: bass.AP,
    w5_w: bass.AP,
    w5_b: bass.AP,
    u5_w: bass.AP,
    u5_b: bass.AP,
    out: bass.AP,
):
    ctx = ExitStack()
    with ctx:
        def sb(name, shape, dt=F32):
            return ctx.enter_context(nc.sbuf_tensor(name, shape, dt))

        def split(name, shape):
            return sb(name + "_hi", shape, F32R), sb(name + "_lo", shape, F32R)

        def both(name, shape, dt=F32):
            return [sb(f"{name}{b}", shape, dt) for b in range(BG)]

        def both_split(name, shape):
            return [split(f"{name}{b}", shape) for b in range(BG)]

        def sem(name):
            return ctx.enter_context(nc.semaphore(name))

        def sems(*names):
            return {n: sem(n) for n in names}

        def sems_b(*names):
            return [{n: sem(f"{n}{b}") for n in names} for b in range(BG)]

        pF = [ctx.enter_context(nc.psum_tensor(f"front{b}", [P, 512], F32)) for b in range(BG)]
        pA = ctx.enter_context(nc.psum_tensor("agg", [P, 2, 512], F32))
        pR = ctx.enter_context(nc.psum_tensor("gates", [P, 2, 512], F32))
        pH = ctx.enter_context(nc.psum_tensor("candidate", [P, 2, 512], F32))

        ident = sb("ident", [P, P])
        ones = sb("ones", [P, 2])
        minus_half = sb("minus_half", [P, BG * NT])
        eps = sb("eps", [P, BG * NT])
        scratch = sb("scratch", [P, 1])
        pscratch = sb("pscratch", [P, 1])
        adjN = sb("adjN", [P, NT, N])
        adjT = split("adjT", [P, NT, N])
        dinv = sb("dinv", [P, NT])
        deg = sb("deg", [P, 4 * NT])
        w0 = split("w0", [P, DT, D])
        wa = split("wa", [P, DT, 2])
        wa2 = split("wa2", [P, DT, P])
        gqk = split("gqk", [P, DT, D])
        wv = split("wv", [P, DT, D])
        w2 = split("w2", [P, DT, D])
        u3 = split("u3", [P, DT, D])
        w4 = split("w4", [P, DT, D])
        w34 = split("w34", [P, DT, D])
        w5 = split("w5", [P, DT, D])
        u5 = split("u5", [P, DT, D])
        beta_c = sb("beta_c", [P, 1])
        bias2_r = sb("bias2_r", [P, BG * 128 * 2])
        braw = sb("braw", [P, 5, DT])
        bz = sb("bz", [P, DT])
        br = sb("br", [P, DT])
        bh = sb("bh", [P, DT])
        arow = sb("arow", [P, 2, D])
        wsum = sb("wsum", [P, 8])

        X0 = both("X0", [P, NT, D])
        X1 = both("X1", [P, NT, D])
        X2 = both("X2", [P, NT, D])
        xT = both_split("xT", [P, DT, N])
        W02 = both("W02", [P, NT, N])
        E = both("E", [P, NT, N])
        E2 = both("E2", [P, NT, N])
        s1 = both("s1", [P, 2 * NT])
        nmx = both("nmx", [P, 2 * NT])
        rs = both("rs", [P, 2 * NT])
        hs = both_split("hs", [P, NT, D])
        HB = both("HB", [P, NT, D])
        pt = both_split("pt", [P, NT, N])
        V = both("V", [P, NT, D])
        Y = both("Y", [P, NT, D])
        yT = both_split("yT", [P, DT, N])
        rn = both("rn", [P, 2 * NT])
        st = both("st", [P, NT, 6])
        mv = both("mv", [P, NT, 2])
        rstd = both("rstd", [P, 2 * NT])
        R, SQ = E, E2
        XB = HB

        X3 = sb("X3", [P, BG, NT, D])
        XR = sb("XR", [P, BG, NT, D])
        hN = split("hN", [P, BG, NT, D])
        hT = sb("hT", [P, DT, BG * N])
        hTs = split("hTs", [P, DT, BG * N])
        aT = split("aT", [P, DT, BG * N])
        tr = sb("tr", [P, DT, BG * N])
        tz = sb("tz", [P, DT, BG * N])
        rh = sb("rh", [P, DT, BG * N])
        rhs = split("rhs", [P, DT, BG * N])
        hv = sb("hv", [P, DT, BG * N])
        dl = rh
        YO = sb("YO", [P, BG, NT, D])
        st3 = sb("st3", [P, BG * NT, 6])
        mv3 = sb("mv3", [P, BG * NT, 2])
        rstd3 = sb("rstd3", [P, 2 * BG * NT])

        stage3 = [tr[:, :, :], tz[:, :, :], rh[:, :, :]]
        stage2 = [hv[:, 0, :], hv[:, 1, :], YO[:, 0, :, :].rearrange("p t d -> p (t d)"),
                  YO[:, 1, :, :].rearrange("p t d -> p (t d)"), XR[:, 0, :, :].rearrange("p t d -> p (t d)"),
                  XR[:, 1, :, :].rearrange("p t d -> p (t d)"), X3[:, 0, :, :].rearrange("p t d -> p (t d)")]
        w3_s, w4_s, w5_s = [s.rearrange("p t (h d) -> p t h d", h=2) for s in stage3]
        w0_s, wq_s, wk_s, wv_s, w2_s, u3_s, u5_s = [s.rearrange("p (t d) -> p t d", t=DT) for s in stage2]
        w4_sum, w34_sum, w5_sum = [hT[:, :, 0:D], hT[:, :, D:2 * D], X3[:, 1, :, :]]

        c = sems("loaded", "ident_zero", "ident_ready", "const_ready", "matrix_in_psum", "matrix_hi", "matrix_lo",
                 "w_prep", "direct_hi", "wa_sum", "wa_ready", "deg_step", "deg_pow", "setup_done")
        f = sems_b("x_loaded", "xT_psum", "xT_hi", "xT_lo",
                   "s_psum", "s1_copied", "w02_ready", "lrelu_ready", "masked_ready", "max_ready", "exp_ready",
                   "rinv_ready",
                   "h_psum", "h_hi", "h_lo", "hb_ready",
                   "p_psum", "p_hi", "p_lo", "att_psum", "v_ready", "neg_ready", "elu_exp", "elu_ready", "y_ready",
                   "stats_ready", "mean_ready", "var_eps", "rstd_ready", "x1_ready", "x2_ready", "x3_ready",
                   "yT_psum", "yT_hi", "yT_lo", "rel_psum", "rel_masked", "rel_hi", "rel_lo", "rel_sq",
                   "vv_psum", "vv_hi", "vv_lo", "norm_psum", "norm_copied", "rn_ready", "out1_psum",
                   "sup_psum", "sup_hi", "sup_lo", "xb_ready", "out2_psum")
        g3 = sems("x3T_psum", "hT_copied", "xr_copied", "hT_hi", "hT_lo", "hN_psum", "hN_hi", "hN_lo",
                  "a_psum", "a_hi", "a_lo", "r_psum", "r_ready", "rh_ready", "rh_hi", "rh_lo",
                  "w5_psum", "z_psum", "z_ready", "hv_psum", "hv_ready", "diff_ready", "gated_ready", "h_new",
                  "yo_ready", "stats3", "mean3", "var_eps3", "rstd3_ready", "normed3", "stored")

        def flat(t):
            return t[:, :, :].rearrange("p a b -> p (a b)")

        def f32(t):
            return t.bitcast(F32)

        x_rows = x.rearrange("b (t p) d -> b p t d", p=P)
        out_rows = out.rearrange("(g b) (t p) d -> g p b t d", b=BG, p=P)
        LOADS = 21

        def once(eng, semaphore, uses):
            if not isinstance(uses, int) or uses > 0:
                eng.wait_ge(semaphore, uses)

        block = ctx.enter_context(nc.Block())

        @block.sync
        def _(sp):
            def rows(w):
                return w.rearrange("(t p) d -> p t d", p=P)

            loads = [(adjN[:, :, :], rows(adj)), (w0_s, rows(W0)), (wq_s, rows(Wq)), (wk_s, rows(Wk)),
                     (wv_s, rows(Wv)), (w2_s, rows(W2)), (u3_s, rows(u3_w)), (u5_s, rows(u5_w)),
                     (stage3[0], rows(w3_w)), (stage3[1], rows(w4_w)), (stage3[2], rows(w5_w)),
                     (arow[:, 0, :], a0[0:D, :].rearrange("f o -> o f").broadcast_to([P, D])),
                     (arow[:, 1, :], a0[D:2 * D, :].rearrange("f o -> o f").broadcast_to([P, D])),
                     (beta_c[:, :], beta.rearrange("(a o) -> a o", a=1).broadcast_to([P, 1])),
                     (bias2_r[:, 0:D], bias2.rearrange("(a o) -> a o", a=1).broadcast_to([P, D])),
                     (bias2_r[:, D:2 * D], bias2.rearrange("(a o) -> a o", a=1).broadcast_to([P, D]))]
            for k, bvec in enumerate((w3_b, u3_b, w4_b, w5_b, u5_b)):
                loads.append((braw[:, k, :], bvec.rearrange("(t p) -> p t", p=P)))
            assert len(loads) == LOADS
            for dst, src in loads:
                sp.dma_start(dst, src, allow_slow_non_contiguous=True).then_inc(c["loaded"], 16)

            for b in range(BG):
                sp.dma_start(X0[b][:, :, :], x_rows[b]).then_inc(f[b]["x_loaded"], 16)
            with sp.Fori(0, G - 1) as i:
                for b in range(BG):
                    sp.wait_ge(f[b]["y_ready"], 3 * i + 1)
                    sp.dma_start(X0[b][:, :, :], x_rows[bass.ds(i * BG + BG + b, 1)].rearrange("o p t d -> p (o t) d")
                                 ).then_inc(f[b]["x_loaded"], 16)
                sp.wait_ge(g3["normed3"], 4 * i + 4)
                sp.dma_start(out_rows[bass.ds(i, 1)].rearrange("o p b t d -> p (o b) t d"), YO[:, :, :, :]
                             ).then_inc(g3["stored"], 16)
            sp.wait_ge(g3["normed3"], 4 * G)
            sp.dma_start(out_rows[G - 1], YO[:, :, :, :]).then_inc(g3["stored"], 16)
            sp.wait_ge(g3["stored"], 16 * G)

        @block.tensor
        def _(pe):
            def passes(o, ls, rs_, start, stop):
                terms = []
                for (lh, ll), (rh_, rl) in zip(ls, rs_):
                    terms += [(lh, rh_), (lh, rl), (ll, rh_)]
                for j, (l, r) in enumerate(terms):
                    mm = pe.matmul(o, l, r, start=start and j == 0, stop=stop and j == len(terms) - 1,
                                   skip_group_check=True)
                return mm

            def cut(s, k, a, b):
                return s[0][:, k, a:b], s[1][:, k, a:b]

            def product(outs, left, right, n_right, start=True, stop=True):
                for i, o in enumerate(outs):
                    mm = passes(o, [cut(left, k, i * P, i * P + P) for k in range(2)],
                                [cut(right, k, 0, n_right) for k in range(2)], start, stop)
                return mm

            def halves(b):
                return [pF[b][:, 0:256], pF[b][:, 256:512]]

            def transpose_tiles(dst, src, start=True):
                for i in range(2):
                    for k in range(2):
                        mm = pe.transpose(dst[:, i * 256 + k * P:i * 256 + k * P + P], src[:, k, i * P:i * P + P],
                                          ident[:, :])
                return mm

            pe.wait_ge(c["loaded"], 16 * LOADS)
            pe.wait_ge(c["ident_ready"], 1)
            order = [(adjN, 0), (wv_s, 0), (u3_s, 0), (w4_sum, 3), (w34_sum, 3), (w5_sum, 3), (u5_s, 0)]
            for n, (src, need) in enumerate(order):
                if need:
                    pe.wait_ge(c["w_prep"], need)
                if n >= 2:
                    pe.wait_ge(c["matrix_lo"], n - 1)
                transpose_tiles(pF[n % 2], src).then_inc(c["matrix_in_psum"], 1)
            n = len(order)
            pe.wait_ge(c["matrix_lo"], n - 1)
            for i in range(2):
                for k in range(2):
                    mm = pe.matmul(pF[n % 2][:, i * 256:i * 256 + 256], wq_s[:, k, i * P:i * P + P], wk_s[:, k, :],
                                   start=(k == 0), stop=(k == 1))
            mm.then_inc(c["matrix_in_psum"], 1)
            pe.wait_ge(c["setup_done"], 1)
            pe.wait_ge(c["matrix_lo"], n + 1)

            def x_to_T(g, b, layer):
                s = f[b]
                if layer == 0:
                    pe.wait_ge(s["x_loaded"], 16 * g + 16)
                    once(pe, s["y_ready"], 3 * g)
                elif layer == 1:
                    pe.wait_ge(s["x1_ready"], 2 * g + 2)
                else:
                    pe.wait_ge(s["x2_ready"], 2 * g + 2)
                transpose_tiles(pF[b], (X0, X1, X2)[layer][b]).then_inc(s["xT_psum"], 1)

            def l0_scores(g, b):
                s = f[b]
                pe.wait_ge(s["xT_hi"], 3 * g + 1)
                pe.wait_ge(s["xT_lo"], 3 * g + 1)
                passes(pF[b][:, 0:N], [cut(wa2, k, 0, P) for k in range(2)], [cut(xT[b], k, 0, N) for k in range(2)],
                       True, True)
                for i in range(NT):
                    mm = passes(pF[b][:, N + 2 * i:N + 2 * i + 2], [cut(xT[b], k, i * P, i * P + P) for k in range(2)],
                                [cut(wa, k, 0, 2) for k in range(2)], True, True)
                mm.then_inc(s["s_psum"], 1)

            def l0_project(g, b):
                s = f[b]
                pe.wait_ge(s["w02_ready"], 2 * g + 2)
                pe.wait_ge(s["lrelu_ready"], 2 * g + 2)
                product(halves(b), xT[b], w0, D).then_inc(s["h_psum"], 1)

            def l0_turn(g, b):
                s = f[b]
                pe.wait_ge(s["h_hi"], g + 1)
                pe.wait_ge(s["h_lo"], g + 1)
                pe.wait_ge(s["hb_ready"], g + 1)
                pe.wait_ge(s["exp_ready"], 2 * g + 2)
                transpose_tiles(pF[b], W02[b]).then_inc(s["p_psum"], 1)

            def l0_attend(g, b):
                s = f[b]
                pe.wait_ge(s["p_hi"], g + 1)
                pe.wait_ge(s["p_lo"], g + 1)
                product(halves(b), pt[b], hs[b], D).then_inc(s["att_psum"], 1)

            def l1_y(g, b):
                s = f[b]
                pe.wait_ge(s["xT_hi"], 3 * g + 2)
                pe.wait_ge(s["xT_lo"], 3 * g + 2)
                product(halves(b), gqk, xT[b], N).then_inc(s["yT_psum"], 1)

            def l1_rel(g, b):
                s = f[b]
                pe.wait_ge(s["yT_hi"], g + 1)
                pe.wait_ge(s["yT_lo"], g + 1)
                product(halves(b), xT[b], yT[b], N).then_inc(s["rel_psum"], 1)

            def l1_v(g, b):
                s = f[b]
                pe.wait_ge(s["rel_masked"], g + 1)
                product(halves(b), xT[b], wv, D).then_inc(s["vv_psum"], 1)

            def l1_norm(g, b):
                s = f[b]
                pe.wait_ge(s["vv_hi"], g + 1)
                pe.wait_ge(s["vv_lo"], g + 1)
                pe.wait_ge(s["rel_sq"], g + 1)
                for i in range(NT):
                    for k in range(NT):
                        mm = pe.matmul(pF[b][:, i:i + 1], SQ[b][:, k, i * P:i * P + P], ones[:, 0:1],
                                       start=(k == 0), stop=(k == NT - 1), skip_group_check=True)
                mm.then_inc(s["norm_psum"], 1)

            def l1_out(g, b):
                s = f[b]
                pe.wait_ge(s["norm_copied"], g + 1)
                pe.wait_ge(s["rel_hi"], g + 1)
                pe.wait_ge(s["rel_lo"], g + 1)
                product(halves(b), pt[b], hs[b], D).then_inc(s["out1_psum"], 1)

            def l2_support(g, b):
                s = f[b]
                pe.wait_ge(s["xT_hi"], 3 * g + 3)
                pe.wait_ge(s["xT_lo"], 3 * g + 3)
                product(halves(b), xT[b], w2, D).then_inc(s["sup_psum"], 1)

            def l2_out(g, b):
                s = f[b]
                pe.wait_ge(s["sup_hi"], 2 * g + 2)
                pe.wait_ge(s["sup_lo"], 2 * g + 2)
                product(halves(b), adjT, hs[b], D).then_inc(s["out2_psum"], 1)

            def x3_to_T(g):
                for b in range(BG):
                    pe.wait_ge(f[b]["x3_ready"], 2 * g + 2)
                once(pe, g3["yo_ready"], g)
                for b in range(BG):
                    for i in range(DT):
                        for k in range(NT):
                            mm = pe.transpose(pA[:, i, b * N + k * P:b * N + k * P + P],
                                              X3[:, b, k, i * P:i * P + P], ident[:, :])
                mm.then_inc(g3["x3T_psum"], 1)

            def aggregate(g, t):
                pe.wait_ge(g3["hN_hi"], 3 * g + t + 1)
                pe.wait_ge(g3["hN_lo"], 3 * g + t + 1)
                pe.wait_ge(g3["hT_copied"], g + 1)
                for i in range(DT):
                    for b in range(BG):
                        mm = passes(pA[:, i, b * N:b * N + N],
                                    [(hN[0][:, b, k, i * P:i * P + P], hN[1][:, b, k, i * P:i * P + P])
                                     for k in range(NT)],
                                    [cut(adjT, k, 0, N) for k in range(NT)], True, True)
                mm.then_inc(g3["a_psum"], 1)

            def gate_u3(g, t):
                pe.wait_ge(g3["hT_hi"], 3 * g + t + 1)
                pe.wait_ge(g3["hT_lo"], 3 * g + t + 1)
                once(pe, g3["z_ready"], 2 * (3 * g + t))
                product([pR[:, 0, :], pR[:, 1, :]], u3, hTs, BG * N, True, False)

            def gate_r(g, t):
                pe.wait_ge(g3["a_hi"], 3 * g + t + 1)
                pe.wait_ge(g3["a_lo"], 3 * g + t + 1)
                product([pR[:, 0, :], pR[:, 1, :]], w4, aT, BG * N, False, True).then_inc(g3["r_psum"], 1)

            def candidate_a(g, t):
                once(pe, g3["hv_ready"], 2 * (3 * g + t))
                product([pH[:, 0, :], pH[:, 1, :]], w5, aT, BG * N, True, False)

            def gate_z(g, t):
                pe.wait_ge(g3["r_ready"], 2 * (3 * g + t + 1))
                product([pR[:, 0, :], pR[:, 1, :]], w34, aT, BG * N, False, True).then_inc(g3["z_psum"], 1)

            def candidate_rh(g, t):
                pe.wait_ge(g3["rh_hi"], 3 * g + t + 1)
                pe.wait_ge(g3["rh_lo"], 3 * g + t + 1)
                product([pH[:, 0, :], pH[:, 1, :]], u5, rhs, BG * N, False, True).then_inc(g3["hv_psum"], 1)

            def h_to_N(g, t):
                pe.wait_ge(g3["h_new"], 3 * g + t + 1)
                pe.wait_ge(g3["a_lo"], 3 * g + t + 1)
                for b in range(BG):
                    for k in range(NT):
                        for i in range(DT):
                            mm = pe.transpose(pA[:, b, k * D + i * P:k * D + i * P + P],
                                              hT[:, i, b * N + k * P:b * N + k * P + P], ident[:, :])
                mm.then_inc(g3["hN_psum"], 1)

            def merged(front, gf, back, gb):
                def fr(*steps):
                    if front:
                        for step in steps:
                            for b in range(BG):
                                step(gf, b)

                def step_a(t):
                    if back:
                        aggregate(gb, t)
                        gate_u3(gb, t)

                if back:
                    x3_to_T(gb)
                fr(lambda g, b: x_to_T(g, b, 0))
                step_a(0)
                fr(l0_scores)
                if back:
                    gate_r(gb, 0)
                    candidate_a(gb, 0)
                fr(l0_project)
                if back:
                    gate_z(gb, 0)
                fr(l0_turn)
                if back:
                    candidate_rh(gb, 0)
                fr(l0_attend)
                if back:
                    h_to_N(gb, 0)
                    step_a(1)
                    gate_r(gb, 1)
                fr(lambda g, b: x_to_T(g, b, 1))
                if back:
                    candidate_a(gb, 1)
                fr(l1_y)
                if back:
                    gate_z(gb, 1)
                fr(l1_rel)
                if back:
                    candidate_rh(gb, 1)
                fr(l1_v, l1_norm)
                fr(l1_out)
                if back:
                    h_to_N(gb, 1)
                    step_a(2)
                    gate_r(gb, 2)
                    candidate_a(gb, 2)
                fr(lambda g, b: x_to_T(g, b, 2))
                if back:
                    gate_z(gb, 2)
                fr(l2_support)
                if back:
                    candidate_rh(gb, 2)
                fr(l2_out)
                if back:
                    h_to_N(gb, 2)

            merged(True, 0, False, None)
            merged(True, 1, True, 0)
            with pe.Fori(1, G - 1) as i:
                merged(True, i + 1, True, i)
            merged(False, None, True, G - 1)

        @block.scalar
        def _(act):
            def copy(o, i):
                return act.activation(o, i, ACT.Copy)

            targets = [adjT, wv, u3, w4, w34, w5, u5, gqk]
            for n, t in enumerate(targets):
                act.wait_ge(c["matrix_in_psum"], n + 1)
                act.activation(flat(t[0]), pF[n % 2][:, :], ACT.Copy,
                               scale=0.5 if t is u5 else 1.0).then_inc(c["matrix_hi"], 1)
            act.wait_ge(c["loaded"], 16 * LOADS)
            copy(w0[0][:, :, :], w0_s).then_inc(c["direct_hi"], 1)
            copy(w2[0][:, :, :], w2_s).then_inc(c["direct_hi"], 1)
            act.wait_ge(c["setup_done"], 1)

            def xT_hi(g, b, layer):
                s = f[b]
                act.wait_ge(s["xT_psum"], 3 * g + layer + 1)
                copy(flat(xT[b][0]), pF[b][:, :]).then_inc(s["xT_hi"], 1)

            def l0_w02(g, b):
                s = f[b]
                act.wait_ge(s["s1_copied"], 2 * g + 2)
                for k in range(NT):
                    act.activation(W02[b][:, k, :], pF[b][:, 0:N], ACT.Identity,
                                   bias=s1[b][:, NT + k:NT + k + 1], scale=SLOPE).then_inc(s["w02_ready"], 1)

            def l0_exp(g, b):
                s = f[b]
                act.wait_ge(s["max_ready"], g + 1)
                for k in range(NT):
                    act.activation(W02[b][:, k, :], E2[b][:, k, :], ACT.Exp, bias=nmx[b][:, NT + k:NT + k + 1],
                                   accum_out=rs[b][:, k:k + 1]).then_inc(s["exp_ready"], 1)

            def l0_h_hi(g, b):
                act.wait_ge(f[b]["h_psum"], g + 1)
                copy(flat(hs[b][0]), pF[b][:, :]).then_inc(f[b]["h_hi"], 1)

            def l0_p_hi(g, b):
                act.wait_ge(f[b]["p_psum"], g + 1)
                copy(flat(pt[b][0]), pF[b][:, :]).then_inc(f[b]["p_hi"], 1)

            def l0_elu(g, b):
                act.wait_ge(f[b]["neg_ready"], g + 1)
                act.activation(flat(E[b]), flat(HB[b]), ACT.Exp).then_inc(f[b]["elu_exp"], 1)

            def l1_y_hi(g, b):
                act.wait_ge(f[b]["yT_psum"], g + 1)
                copy(flat(yT[b][0]), pF[b][:, :]).then_inc(f[b]["yT_hi"], 1)

            def l1_rel_hi(g, b):
                s = f[b]
                act.wait_ge(s["rel_masked"], g + 1)
                copy(flat(pt[b][0]), flat(R[b])).then_inc(s["rel_hi"], 1)
                act.activation(flat(SQ[b]), flat(R[b]), ACT.Square).then_inc(s["rel_sq"], 1)

            def l1_v_hi(g, b):
                act.wait_ge(f[b]["vv_psum"], g + 1)
                copy(flat(hs[b][0]), pF[b][:, :]).then_inc(f[b]["vv_hi"], 1)

            def l2_sup_hi(g, b):
                act.wait_ge(f[b]["sup_psum"], g + 1)
                for k in range(NT):
                    act.activation(hs[b][0][:, k, :], pF[b][:, k * D:k * D + D], ACT.Copy,
                                   scale=dinv[:, k:k + 1]).then_inc(f[b]["sup_hi"], 1)

            def take_x3(g):
                act.wait_ge(f[0]["x3_ready"], 2 * g + 2)
                act.wait_ge(f[1]["x3_ready"], 2 * g + 2)
                act.wait_ge(g3["x3T_psum"], g + 1)
                copy(hT[:, :, :], pA[:, :, :]).then_inc(g3["hT_copied"], 1)
                copy(hN[0][:, :, :, :], X3[:, :, :, :]).then_inc(g3["hN_hi"], 1)
                act.wait_ge(g3["hT_copied"], g + 1)
                copy(hTs[0][:, :, :], hT[:, :, :]).then_inc(g3["hT_hi"], 1)

            def a_hi(g, t):
                act.wait_ge(g3["a_psum"], 3 * g + t + 1)
                once(act, g3["z_psum"], 3 * g + t)
                copy(aT[0][:, :, :], pA[:, :, :]).then_inc(g3["a_hi"], 1)

            def gate_r(g, t):
                act.wait_ge(g3["r_psum"], 3 * g + t + 1)
                for i in range(DT):
                    act.activation(tr[:, i, :], pR[:, i, :], ACT.Tanh, bias=br[:, i:i + 1],
                                   scale=0.5).then_inc(g3["r_ready"], 1)

            def rh_hi(g, t):
                act.wait_ge(g3["rh_ready"], 3 * g + t + 1)
                copy(rhs[0][:, :, :], rh[:, :, :]).then_inc(g3["rh_hi"], 1)

            def gate_z(g, t):
                act.wait_ge(g3["z_psum"], 3 * g + t + 1)
                once(act, g3["gated_ready"], 3 * g + t)
                for i in range(DT):
                    act.activation(tz[:, i, :], pR[:, i, :], ACT.Tanh, bias=bz[:, i:i + 1],
                                   scale=0.5).then_inc(g3["z_ready"], 1)

            def cand(g, t):
                act.wait_ge(g3["hv_psum"], 3 * g + t + 1)
                once(act, g3["diff_ready"], 3 * g + t)
                for i in range(DT):
                    act.activation(hv[:, i, :], pH[:, i, :], ACT.Tanh, bias=bh[:, i:i + 1]).then_inc(g3["hv_ready"], 1)

            def h_hi(g, t):
                act.wait_ge(g3["h_new"], 3 * g + t + 1)
                copy(hTs[0][:, :, :], hT[:, :, :]).then_inc(g3["hT_hi"], 1)
                act.wait_ge(g3["hN_psum"], 3 * g + t + 1)
                copy(hN[0][:, :, :, :].rearrange("p b t d -> p b (t d)"), pA[:, :, :]).then_inc(g3["hN_hi"], 1)

            def merged(front, gf, back, gb):
                def fr(*steps):
                    if front:
                        for step in steps:
                            for b in range(BG):
                                step(gf, b)

                def bk(step, *t):
                    if back:
                        step(gb, *t)

                bk(take_x3)
                fr(lambda g, b: xT_hi(g, b, 0))
                bk(a_hi, 0)
                fr(l0_w02)
                bk(gate_r, 0)
                fr(l0_exp)
                bk(rh_hi, 0)
                fr(l0_h_hi)
                bk(gate_z, 0)
                fr(l0_p_hi)
                bk(cand, 0)
                fr(l0_elu)
                bk(h_hi, 0)
                bk(a_hi, 1)
                bk(gate_r, 1)
                fr(lambda g, b: xT_hi(g, b, 1))
                bk(rh_hi, 1)
                fr(l1_y_hi)
                bk(gate_z, 1)
                fr(l1_rel_hi)
                bk(cand, 1)
                fr(l1_v_hi)
                bk(h_hi, 1)
                bk(a_hi, 2)
                bk(gate_r, 2)
                bk(rh_hi, 2)
                fr(lambda g, b: xT_hi(g, b, 2))
                bk(gate_z, 2)
                fr(l2_sup_hi)
                bk(cand, 2)

            merged(True, 0, False, None)
            merged(True, 1, True, 0)
            with act.Fori(1, G - 1) as i:
                merged(True, i + 1, True, i)
            merged(False, None, True, G - 1)

        @block.vector
        def _(dve):
            dve.wait_ge(c["loaded"], 16 * LOADS)
            dve.tensor_tensor(w4_sum, w4_s[:, :, 0, :], w4_s[:, :, 1, :], ALU.add).then_inc(c["w_prep"], 1)
            dve.tensor_tensor(w5_sum, w5_s[:, :, 0, :], w5_s[:, :, 1, :], ALU.add).then_inc(c["w_prep"], 1)
            dve.tensor_tensor(w34_sum, w3_s[:, :, 0, :], w3_s[:, :, 1, :], ALU.add).then_inc(c["wa_sum"], 1)
            dve.wait_ge(c["wa_sum"], 1)
            dve.wait_ge(c["w_prep"], 2)
            dve.tensor_tensor(w34_sum, w34_sum, w4_sum, ALU.subtract).then_inc(c["w_prep"], 1)
            for k in range(DT):
                for j in range(2):
                    dve.tensor_tensor_reduce(V[j][:, k, :], w0_s[:, k, :], arow[:, j, :], 1.0, 0.0, ALU.mult, ALU.add,
                                             wsum[:, 2 * k + j:2 * k + j + 1]).then_inc(c["wa_sum"], 1)
            dve.tensor_reduce(deg[:, 0:NT], adjN[:, :, :], mybir.AxisListType.X, ALU.add).then_inc(c["deg_step"], 1)
            dve.wait_ge(c["deg_step"], 1)
            dve.tensor_scalar(deg[:, NT:2 * NT], deg[:, 0:NT], 1e-38, None, ALU.max).then_inc(c["deg_step"], 1)
            dve.tensor_scalar(deg[:, 2 * NT:3 * NT], deg[:, 0:NT], 0.0, None, ALU.is_gt).then_inc(c["deg_step"], 1)
            dve.wait_ge(c["deg_pow"], 1)
            dve.wait_ge(c["deg_step"], 3)
            dve.tensor_tensor(dinv[:, :], deg[:, 3 * NT:4 * NT], deg[:, 2 * NT:3 * NT], ALU.mult).then_inc(c["deg_step"], 1)
            dve.wait_ge(c["wa_sum"], 5)
            dve.wait_ge(c["const_ready"], 3)
            wsv = wsum[:, 0:4].rearrange("p (k j) -> p k j", k=DT)
            dve.tensor_copy(wa[0][:, :, :], wsv).then_inc(c["wa_ready"], 1)
            dve.memset(Y[0][:, 0, 0:P], 1.0).then_inc(c["wa_ready"], 1)
            dve.wait_ge(c["wa_ready"], 2)
            dve.tensor_tensor(wa[1][:, :, :], wsv, f32(wa[0][:, :, :]), ALU.subtract).then_inc(c["wa_ready"], 1)
            for k in range(DT):
                dve.tensor_scalar(V[0][:, k, 0:P], Y[0][:, 0, 0:P], wsum[:, 2 * k + 1:2 * k + 2], None,
                                  ALU.mult).then_inc(c["wa_ready"], 1)
            dve.wait_ge(c["wa_ready"], 5)
            dve.tensor_copy(wa2[0][:, :, :], V[0][:, :, 0:P]).then_inc(c["wa_ready"], 1)
            dve.wait_ge(c["wa_ready"], 6)
            dve.tensor_tensor(wa2[1][:, :, :], V[0][:, :, 0:P], f32(wa2[0][:, :, :]),
                              ALU.subtract).then_inc(c["wa_ready"], 1)
            dve.tensor_tensor(bz[:, :], braw[:, 0, :], braw[:, 1, :], ALU.add).then_inc(c["wa_ready"], 1)
            dve.tensor_tensor(br[:, :], braw[:, 2, :], braw[:, 1, :], ALU.add).then_inc(c["wa_ready"], 1)
            dve.tensor_tensor(bh[:, :], braw[:, 3, :], braw[:, 4, :], ALU.add).then_inc(c["wa_ready"], 1)
            dve.wait_ge(c["wa_ready"], 10)
            dve.tensor_scalar(bz[:, :], bz[:, :], 0.5, None, ALU.mult).then_inc(c["wa_ready"], 1)
            dve.tensor_scalar(br[:, :], br[:, :], 0.5, None, ALU.mult).then_inc(c["wa_ready"], 1)
            targets = [adjT, wv, u3, w4, w34, w5, u5, gqk]
            for n, t in enumerate(targets):
                dve.wait_ge(c["matrix_hi"], n + 1)
                if t is u5:
                    dve.scalar_tensor_tensor(flat(t[1]), pF[n % 2][:, :], 0.5, f32(flat(t[0])), ALU.mult,
                                             ALU.subtract).then_inc(c["matrix_lo"], 1)
                else:
                    dve.tensor_tensor(flat(t[1]), pF[n % 2][:, :], f32(flat(t[0])),
                                      ALU.subtract).then_inc(c["matrix_lo"], 1)
            dve.wait_ge(c["direct_hi"], 2)
            dve.tensor_tensor(w0[1][:, :, :], w0_s, f32(w0[0][:, :, :]), ALU.subtract).then_inc(c["wa_ready"], 1)
            dve.tensor_tensor(w2[1][:, :, :], w2_s, f32(w2[0][:, :, :]), ALU.subtract).then_inc(c["wa_ready"], 1)
            dve.wait_ge(c["wa_ready"], 14)
            dve.wait_ge(c["deg_step"], 4)
            dve.wait_ge(c["matrix_lo"], 8)
            dve.memset(deg[:, 0:1], 0.0).then_inc(c["setup_done"], 1)

            def lo(o, full, hi):
                return dve.tensor_tensor(o, full, f32(hi), ALU.subtract)

            def layernorm(s, b, o, n, ready):
                dve.wait_ge(s["y_ready"], n + 1)
                for k in range(NT):
                    dve.bn_stats(st[b][:, k, :], Y[b][:, k, :]).then_inc(s["stats_ready"], 1)
                dve.wait_ge(s["stats_ready"], 2 * n + 2)
                dve.memset(scratch[:, 0:1], 0.0)
                for k in range(NT):
                    dve.bn_aggr(mv[b][:, k, :], st[b][:, k, :]).then_inc(s["mean_ready"], 1)
                dve.wait_ge(s["rstd_ready"], n + 1)
                for k in range(NT):
                    dve.tensor_scalar(o[:, k, :], Y[b][:, k, :], mv[b][:, k, 0:1], rstd[b][:, NT + k:NT + k + 1],
                                      ALU.subtract, ALU.mult).then_inc(ready, 1)

            def xT_lo(g, b, layer):
                s = f[b]
                dve.wait_ge(s["xT_hi"], 3 * g + layer + 1)
                lo(flat(xT[b][1]), pF[b][:, :], flat(xT[b][0])).then_inc(s["xT_lo"], 1)

            def l0_s1(g, b):
                s = f[b]
                dve.wait_ge(s["s_psum"], g + 1)
                pv = pF[b][:, N:N + 2 * NT].rearrange("p (t j) -> p j t", j=2)[:, 0, :]
                dve.tensor_copy(s1[b][:, 0:NT], pv).then_inc(s["s1_copied"], 1)
                dve.tensor_scalar(s1[b][:, NT:2 * NT], pv, SLOPE, None, ALU.mult).then_inc(s["s1_copied"], 1)

            def l0_mask(g, b):
                s = f[b]
                dve.wait_ge(s["w02_ready"], 2 * g + 2)
                for k in range(NT):
                    dve.scalar_tensor_tensor(E[b][:, k, :], pF[b][:, 0:N], s1[b][:, k:k + 1], W02[b][:, k, :],
                                             ALU.add, ALU.max).then_inc(s["lrelu_ready"], 1)
                dve.wait_ge(c["setup_done"], 1)
                dve.wait_ge(s["lrelu_ready"], 2 * g + 2)
                for k in range(NT):
                    dve.tensor_tensor_reduce(E2[b][:, k, :], E[b][:, k, :], adjN[:, k, :], 1.0, -3e38, ALU.mult, ALU.max,
                                             nmx[b][:, k:k + 1]).then_inc(s["masked_ready"], 1)
                dve.wait_ge(s["masked_ready"], 2 * g + 2)
                dve.tensor_scalar(nmx[b][:, NT:2 * NT], nmx[b][:, 0:NT], -1.0, None, ALU.mult).then_inc(s["max_ready"], 1)

            def l0_h_lo(g, b):
                s = f[b]
                dve.wait_ge(s["h_hi"], g + 1)
                lo(flat(hs[b][1]), pF[b][:, :], flat(hs[b][0])).then_inc(s["h_lo"], 1)
                dve.tensor_scalar(flat(HB[b]), pF[b][:, :], beta_c[:, 0:1], None, ALU.mult).then_inc(s["hb_ready"], 1)

            def l0_p_lo(g, b):
                s = f[b]
                dve.wait_ge(s["p_hi"], g + 1)
                lo(flat(pt[b][1]), pF[b][:, :], flat(pt[b][0])).then_inc(s["p_lo"], 1)
                dve.wait_ge(s["exp_ready"], 2 * g + 2)
                dve.reciprocal(rs[b][:, NT:2 * NT], rs[b][:, 0:NT]).then_inc(s["rinv_ready"], 1)

            def l0_elu_in(g, b):
                s = f[b]
                dve.wait_ge(s["att_psum"], g + 1)
                dve.wait_ge(s["rinv_ready"], g + 1)
                for k in range(NT):
                    dve.scalar_tensor_tensor(V[b][:, k, :], pF[b][:, k * D:k * D + D], rs[b][:, NT + k:NT + k + 1],
                                             HB[b][:, k, :], ALU.mult, ALU.add).then_inc(s["v_ready"], 1)
                dve.wait_ge(s["v_ready"], 2 * g + 2)
                dve.tensor_scalar(flat(HB[b]), flat(V[b]), 0.0, None, ALU.min).then_inc(s["neg_ready"], 1)

            def l0_elu_out(g, b):
                s = f[b]
                dve.wait_ge(s["elu_exp"], g + 1)
                dve.scalar_tensor_tensor(flat(V[b]), flat(V[b]), 0.0, flat(E[b]), ALU.max,
                                         ALU.add).then_inc(s["elu_ready"], 1)
                dve.wait_ge(s["elu_ready"], g + 1)
                dve.scalar_tensor_tensor(flat(Y[b]), flat(V[b]), -1.0, flat(X0[b]), ALU.add,
                                         ALU.add).then_inc(s["y_ready"], 1)

            def l1_y_lo(g, b):
                dve.wait_ge(f[b]["yT_hi"], g + 1)
                lo(flat(yT[b][1]), pF[b][:, :], flat(yT[b][0])).then_inc(f[b]["yT_lo"], 1)

            def l1_mask(g, b):
                s = f[b]
                dve.wait_ge(s["rel_psum"], g + 1)
                dve.tensor_tensor(flat(R[b]), pF[b][:, :], flat(adjN), ALU.mult).then_inc(s["rel_masked"], 1)
                dve.wait_ge(s["rel_hi"], g + 1)
                lo(flat(pt[b][1]), flat(R[b]), flat(pt[b][0])).then_inc(s["rel_lo"], 1)

            def l1_v_lo(g, b):
                dve.wait_ge(f[b]["vv_hi"], g + 1)
                lo(flat(hs[b][1]), pF[b][:, :], flat(hs[b][0])).then_inc(f[b]["vv_lo"], 1)

            def l1_norm(g, b):
                dve.wait_ge(f[b]["norm_psum"], g + 1)
                dve.tensor_copy(rn[b][:, 0:NT], pF[b][:, 0:NT]).then_inc(f[b]["norm_copied"], 1)

            def l1_residual(g, b):
                s = f[b]
                dve.wait_ge(s["out1_psum"], g + 1)
                dve.wait_ge(s["rn_ready"], g + 1)
                for k in range(NT):
                    last = dve.scalar_tensor_tensor(Y[b][:, k, :], pF[b][:, k * D:k * D + D],
                                                    rn[b][:, NT + k:NT + k + 1], X1[b][:, k, :], ALU.mult, ALU.add)
                last.then_inc(s["y_ready"], 1)

            def l2_sup_lo(g, b):
                s = f[b]
                dve.wait_ge(s["sup_hi"], 2 * g + 2)
                for k in range(NT):
                    dve.scalar_tensor_tensor(hs[b][1][:, k, :], pF[b][:, k * D:k * D + D], dinv[:, k:k + 1],
                                             f32(hs[b][0][:, k, :]), ALU.mult, ALU.subtract).then_inc(s["sup_lo"], 1)

            def l2_residual(g, b):
                s = f[b]
                dve.wait_ge(s["out2_psum"], g + 1)
                dve.wait_ge(s["xb_ready"], g + 1)
                for k in range(NT):
                    last = dve.scalar_tensor_tensor(Y[b][:, k, :], pF[b][:, k * D:k * D + D],
                                                    dinv[:, k:k + 1], XB[b][:, k, :], ALU.mult, ALU.add)
                last.then_inc(s["y_ready"], 1)

            def ln0(g, b):
                layernorm(f[b], b, X1[b], 3 * g, f[b]["x1_ready"])

            def ln1(g, b):
                layernorm(f[b], b, X2[b], 3 * g + 1, f[b]["x2_ready"])

            def ln2(g, b):
                once(dve, g3["xr_copied"], g)
                once(dve, g3["hN_hi"], 3 * g - 2)
                layernorm(f[b], b, X3[:, b], 3 * g + 2, f[b]["x3_ready"])

            def take_x3(g):
                dve.wait_ge(g3["hN_hi"], 3 * g + 1)
                lo(hN[1][:, :, :, :], X3[:, :, :, :], hN[0][:, :, :, :]).then_inc(g3["hN_lo"], 1)
                dve.wait_ge(g3["hT_hi"], 3 * g + 1)
                lo(hTs[1][:, :, :], hT[:, :, :], hTs[0][:, :, :]).then_inc(g3["hT_lo"], 1)

            def a_lo(g, t):
                dve.wait_ge(g3["a_hi"], 3 * g + t + 1)
                lo(aT[1][:, :, :], pA[:, :, :], aT[0][:, :, :]).then_inc(g3["a_lo"], 1)

            def reset(g, t):
                dve.wait_ge(g3["r_ready"], 2 * (3 * g + t + 1))
                dve.scalar_tensor_tensor(flat(rh), flat(tr), 1.0, flat(hT), ALU.add, ALU.mult).then_inc(g3["rh_ready"], 1)
                dve.wait_ge(g3["rh_hi"], 3 * g + t + 1)
                lo(rhs[1][:, :, :], rh[:, :, :], rhs[0][:, :, :]).then_inc(g3["rh_lo"], 1)

            def update(g, t):
                n = 3 * g + t
                dve.wait_ge(g3["hv_ready"], 2 * n + 2)
                dve.wait_ge(g3["rh_lo"], n + 1)
                dve.tensor_tensor(flat(dl), flat(hv), flat(hT), ALU.subtract).then_inc(g3["diff_ready"], 1)
                dve.wait_ge(g3["diff_ready"], n + 1)
                dve.wait_ge(g3["z_ready"], 2 * n + 2)
                dve.scalar_tensor_tensor(flat(dl), flat(tz), 1.0, flat(dl), ALU.add, ALU.mult).then_inc(g3["gated_ready"], 1)
                dve.wait_ge(g3["gated_ready"], n + 1)
                dve.wait_ge(g3["hT_hi"], n + 1)
                dve.scalar_tensor_tensor(flat(hT), flat(dl), 0.5, flat(hT), ALU.mult, ALU.add).then_inc(g3["h_new"], 1)

            def h_lo(g, t):
                dve.wait_ge(g3["hT_hi"], 3 * g + t + 2)
                lo(hTs[1][:, :, :], hT[:, :, :], hTs[0][:, :, :]).then_inc(g3["hT_lo"], 1)
                dve.wait_ge(g3["hN_hi"], 3 * g + t + 2)
                lo(hN[1][:, :, :, :].rearrange("p b t d -> p b (t d)"), pA[:, :, :],
                   hN[0][:, :, :, :].rearrange("p b t d -> p b (t d)")).then_inc(g3["hN_lo"], 1)

            def finish(g):
                dve.wait_ge(g3["hN_psum"], 3 * g + 3)
                dve.wait_ge(g3["xr_copied"], g + 1)
                once(dve, g3["stored"], 16 * g)
                dve.tensor_tensor(YO[:, :, :, :].rearrange("p b t d -> p b (t d)"), pA[:, :, :],
                                  XR[:, :, :, :].rearrange("p b t d -> p b (t d)"), ALU.add).then_inc(g3["yo_ready"], 1)
                dve.wait_ge(g3["yo_ready"], g + 1)
                yo = YO[:, :, :, :].rearrange("p b t d -> p (b t) d")
                for k in range(BG * NT):
                    dve.bn_stats(st3[:, k, :], yo[:, k, :]).then_inc(g3["stats3"], 1)
                dve.wait_ge(g3["stats3"], 4 * g + 4)
                dve.memset(scratch[:, 0:1], 0.0)
                for k in range(BG * NT):
                    dve.bn_aggr(mv3[:, k, :], st3[:, k, :]).then_inc(g3["mean3"], 1)
                dve.wait_ge(g3["rstd3_ready"], g + 1)
                for k in range(BG * NT):
                    dve.tensor_scalar(yo[:, k, :], yo[:, k, :], mv3[:, k, 0:1], rstd3[:, 4 + k:5 + k],
                                      ALU.subtract, ALU.mult).then_inc(g3["normed3"], 1)

            def merged(front, gf, back, gb):
                def fr(*steps):
                    if front:
                        for step in steps:
                            for b in range(BG):
                                step(gf, b)

                def bk(step, *t):
                    if back:
                        step(gb, *t)

                bk(take_x3)
                fr(lambda g, b: xT_lo(g, b, 0))
                bk(a_lo, 0)
                fr(l0_s1)
                fr(l0_mask)
                bk(reset, 0)
                fr(l0_h_lo)
                fr(l0_p_lo)
                fr(l0_elu_in)
                bk(update, 0)
                fr(l0_elu_out)
                bk(h_lo, 0)
                bk(a_lo, 1)
                fr(ln0)
                bk(reset, 1)
                fr(lambda g, b: xT_lo(g, b, 1))
                fr(l1_y_lo)
                fr(l1_mask)
                fr(l1_v_lo)
                bk(update, 1)
                fr(l1_norm)
                bk(h_lo, 1)
                fr(l1_residual)
                bk(a_lo, 2)
                fr(ln1)
                bk(reset, 2)
                fr(lambda g, b: xT_lo(g, b, 2))
                fr(l2_sup_lo)
                bk(update, 2)
                fr(l2_residual)
                fr(ln2)
                bk(finish)

            merged(True, 0, False, None)
            merged(True, 1, True, 0)
            with dve.Fori(1, G - 1) as i:
                merged(True, i + 1, True, i)
            merged(False, None, True, G - 1)

        @block.gpsimd
        def _(pool):
            pool.memset(ident[:, :], 0.0).then_inc(c["ident_zero"], 1)
            pool.memset(ones[:, :], 1.0).then_inc(c["const_ready"], 1)
            pool.memset(minus_half[:, :], -0.5).then_inc(c["const_ready"], 1)
            pool.memset(eps[:, :], EPS).then_inc(c["const_ready"], 1)
            pool.wait_ge(c["ident_zero"], 1)
            pool.affine_select(out=ident[:, :], in_=ident[:, :], compare_op=ALU.not_equal, fill=1.0, base=0,
                               pattern=[[-1, P]], channel_multiplier=1).then_inc(c["ident_ready"], 1)
            pool.wait_ge(c["const_ready"], 3)
            pool.wait_ge(c["deg_step"], 2)
            pool.tensor_tensor(deg[:, 3 * NT:4 * NT], deg[:, NT:2 * NT], minus_half[:, 0:NT],
                               ALU.pow).then_inc(c["deg_pow"], 1)
            pool.wait_ge(c["setup_done"], 1)

            def rstd_of(g, b, layer):
                s = f[b]
                n = 3 * g + layer
                pool.wait_ge(s["mean_ready"], 2 * n + 2)
                pool.tensor_tensor(rstd[b][:, 0:NT], mv[b][:, :, 1], eps[:, 0:NT], ALU.add).then_inc(s["var_eps"], 1)
                pool.wait_ge(s["var_eps"], n + 1)
                pool.tensor_tensor(rstd[b][:, NT:2 * NT], rstd[b][:, 0:NT], minus_half[:, 0:NT],
                                   ALU.pow).then_inc(s["rstd_ready"], 1)

            def rnorm(g, b):
                s = f[b]
                pool.wait_ge(s["norm_copied"], g + 1)
                pool.tensor_tensor(rn[b][:, NT:2 * NT], rn[b][:, 0:NT], minus_half[:, 0:NT],
                                   ALU.pow).then_inc(s["rn_ready"], 1)

            def add_bias2(g, b):
                s = f[b]
                pool.wait_ge(s["x2_ready"], 2 * g + 2)
                pool.tensor_tensor(flat(XB[b]), flat(X2[b]), bias2_r[:, :], ALU.add).then_inc(s["xb_ready"], 1)

            def keep_x3(g):
                for b in range(BG):
                    pool.wait_ge(f[b]["x3_ready"], 2 * g + 2)
                once(pool, g3["yo_ready"], g)
                pool.tensor_tensor(pscratch[:, :], eps[:, 0:1], eps[:, 1:2], ALU.add)
                pool.tensor_copy(XR[:, :, :, :], X3[:, :, :, :]).then_inc(g3["xr_copied"], 1)

            def rstd_out(g):
                pool.wait_ge(g3["mean3"], 4 * g + 4)
                pool.tensor_tensor(rstd3[:, 0:4], mv3[:, :, 1], eps[:, 0:4], ALU.add).then_inc(g3["var_eps3"], 1)
                pool.wait_ge(g3["var_eps3"], g + 1)
                pool.tensor_tensor(rstd3[:, 4:8], rstd3[:, 0:4], minus_half[:, 0:4], ALU.pow).then_inc(g3["rstd3_ready"], 1)

            def merged(front, gf, back, gb):
                if back:
                    keep_x3(gb)
                if front:
                    for b in range(BG):
                        rstd_of(gf, b, 0)
                    for b in range(BG):
                        rnorm(gf, b)
                    for b in range(BG):
                        rstd_of(gf, b, 1)
                    for b in range(BG):
                        add_bias2(gf, b)
                    for b in range(BG):
                        rstd_of(gf, b, 2)
                if back:
                    rstd_out(gb)

            merged(True, 0, False, None)
            merged(True, 1, True, 0)
            with pool.Fori(1, G - 1) as i:
                merged(True, i + 1, True, i)
            merged(False, None, True, G - 1)


_INS = ['x', 'adj', 'L0_gnn_W', 'L0_gnn_a', 'L0_gnn_beta', 'L1_gnn_Wq', 'L1_gnn_Wk', 'L1_gnn_Wv', 'L2_gnn_weight',
        'L2_gnn_bias', 'L3_gnn_w3_w', 'L3_gnn_w3_b', 'L3_gnn_u3_w', 'L3_gnn_u3_b', 'L3_gnn_w4_w', 'L3_gnn_w4_b',
        'L3_gnn_w5_w', 'L3_gnn_w5_b', 'L3_gnn_u5_w', 'L3_gnn_u5_b']
_OUTS = [((B, N, D), 'float32')]


def kernel(**inputs):
    import numpy as _np
    import concourse.bacc as _bacc
    from concourse import mybir as _mybir
    from concourse.bass_utils import run_bass_kernel_spmd as _run

    nc = _bacc.Bacc("TRN2", target_bir_lowering=False, num_devices=1)
    arrays, args = {}, []
    for name in _INS:
        a = _np.ascontiguousarray(inputs[name])
        arrays[f"in_{name}_dram"] = a
        args.append(nc.dram_tensor(f"in_{name}_dram", a.shape, _mybir.dt.from_np(a.dtype), kind="ExternalInput").ap())
    for i, (shape, dtype) in enumerate(_OUTS):
        dt = _mybir.dt.from_np(_np.dtype(dtype))
        args.append(nc.dram_tensor(f"out_{i}_dram", shape, dt, kind="ExternalOutput").ap())
    four_layer_gnn_kernel(nc, *args)
    r = _run(nc, [arrays], core_ids=[0])
    return r.results[0]["out_0_dram"]
```

```python
from contextlib import ExitStack

import concourse.bass as bass
from concourse import mybir

P = 128
ALU = mybir.AluOpType
ACT = mybir.ActivationFunctionType
F32 = mybir.dt.float32
F32R = mybir.dt.float32r

B, N, D = 32, 256, 256
BG = 2
G = B // BG
T = 3
NT, DT = N // P, D // P
SLOPE = 0.2
EPS = 1e-5



def four_layer_gnn_kernel(
    nc: bass.Bass,
    x: bass.AP,
    adj: bass.AP,
    W0: bass.AP,
    a0: bass.AP,
    beta: bass.AP,
    Wq: bass.AP,
    Wk: bass.AP,
    Wv: bass.AP,
    W2: bass.AP,
    bias2: bass.AP,
    w3_w: bass.AP,
    w3_b: bass.AP,
    u3_w: bass.AP,
    u3_b: bass.AP,
    w4_w: bass.AP,
    w4_b: bass.AP,
    w5_w: bass.AP,
    w5_b: bass.AP,
    u5_w: bass.AP,
    u5_b: bass.AP,
    out: bass.AP,
):
    ctx = ExitStack()
    with ctx:
        def sb(name, shape, dt=F32):
            return ctx.enter_context(nc.sbuf_tensor(name, shape, dt))

        def split(name, shape):
            return sb(name + "_hi", shape, F32R), sb(name + "_lo", shape, F32R)

        def both(name, shape, dt=F32):
            return [sb(f"{name}{b}", shape, dt) for b in range(BG)]

        def both_split(name, shape):
            return [split(f"{name}{b}", shape) for b in range(BG)]

        def sem(name):
            return ctx.enter_context(nc.semaphore(name))

        def sems(*names):
            return {n: sem(n) for n in names}

        def sems_b(*names):
            return [{n: sem(f"{n}{b}") for n in names} for b in range(BG)]

        def banks(name):
            return [ctx.enter_context(nc.psum_tensor(f"{name}{b}", [P, 512], F32)) for b in range(BG)]

        pF, pA, pR, pH = banks("front"), banks("aggregate"), banks("gates"), banks("candidate")

        ident = sb("ident", [P, P])
        ones = sb("ones", [P, 2])
        minus_half = sb("minus_half", [P, NT])
        eps = sb("eps", [P, NT])
        scratch = sb("scratch", [P, 1])
        adjN = sb("adjN", [P, NT, N])
        adjT = split("adjT", [P, NT, N])
        dinv = sb("dinv", [P, NT])
        deg = sb("deg", [P, 4 * NT])
        w0 = split("w0", [P, DT, D])
        wa1 = sb("wa1", [P, D])
        wa2 = split("wa2", [P, DT, P])
        gqk = split("gqk", [P, DT, D])
        wv = split("wv", [P, DT, D])
        w2 = split("w2", [P, DT, D])
        u3 = split("u3", [P, DT, D])
        w4 = split("w4", [P, DT, D])
        w34 = split("w34", [P, DT, D])
        w5 = split("w5", [P, DT, D])
        u5 = split("u5", [P, DT, D])
        beta_c = sb("beta_c", [P, 1])
        bias2_r = sb("bias2_r", [P, BG * 128 * 2])
        braw = sb("braw", [P, 5, DT])
        bz = sb("bz", [P, DT])
        br = sb("br", [P, DT])
        bh = sb("bh", [P, DT])
        arow = sb("arow", [P, 2, D])
        wsum = sb("wsum", [P, 8])

        X0 = both("X0", [P, NT, D])
        X1 = both("X1", [P, NT, D])
        X2 = both("X2", [P, NT, D])
        xT = both_split("xT", [P, DT, N])
        W02 = both("W02", [P, NT, N])
        E = both("E", [P, NT, N])
        E2 = both("E2", [P, NT, N])
        s1 = both("s1", [P, 2 * NT])
        nmx = both("nmx", [P, 2 * NT])
        rs = both("rs", [P, 2 * NT])
        hs = both_split("hs", [P, NT, D])
        HB = both("HB", [P, NT, D])
        pt = both_split("pt", [P, NT, N])
        V = both("V", [P, NT, D])
        Y = both("Y", [P, NT, D])
        yT = both_split("yT", [P, DT, N])
        rn = both("rn", [P, 2 * NT])
        st, st3 = both("st", [P, NT, 6]), both("st3", [P, NT, 6])
        mv, mv3 = both("mv", [P, NT, 2]), both("mv3", [P, NT, 2])
        ln, ln3 = both("ln", [P, 4, NT]), both("ln3", [P, 4, NT])
        R, SQ = E, E2
        XB = HB

        X3 = both("X3", [P, NT, D])
        XR = both("XR", [P, NT, D])
        hN = both_split("hN", [P, NT, D])
        hT = both("hT", [P, DT, N])
        hTs = both_split("hTs", [P, DT, N])
        aT = both_split("aT", [P, DT, N])
        tr = both("tr", [P, DT, N])
        tz = both("tz", [P, DT, N])
        rh = both("rh", [P, DT, N])
        rhs = both_split("rhs", [P, DT, N])
        hv = both("hv", [P, DT, N])
        YO = both("YO", [P, NT, D])

        w3_s, w4_s, w5_s = [(lo_half, hi_half) for lo_half, hi_half in (tr, tz, rh)]
        w0_s, wq_s, wk_s, wv_s, w2_s, u3_s, u5_s = [
            t[:, :, :] for t in (hv[0], hv[1], YO[0], YO[1], XR[0], XR[1], X3[0])]
        w4_sum, w34_sum, w5_sum = hT[0][:, :, :], hT[1][:, :, :], X3[1][:, :, :]

        c = sems("loaded", "ident_zero", "ident_ready", "const_ready", "matrix_in_psum", "matrix_hi", "matrix_lo",
                 "w_prep", "direct_hi", "wa_sum", "wa_ready", "wa1_turned", "deg_step", "deg_pow", "setup_done")
        f = sems_b("x_loaded", "front_psum", "part_hi", "part_lo",
                   "s1_ready", "w02_ready", "lrelu_ready", "masked_ready", "max_ready", "exp_ready", "rinv_ready",
                   "hb_ready", "v_ready", "neg_ready", "elu_exp", "elu_ready", "y_ready",
                   "stats_ready", "mean_ready", "rstd_ready", "x1_ready", "x2_ready", "x3_ready",
                   "rel_masked", "rel_hi", "rel_lo", "vv_hi", "vv_lo", "norm_copied", "rn_ready", "xb_ready",
                   "x3T_psum", "hT_copied", "xr_copied", "hT_hi", "hT_lo", "hN_psum", "hN_hi", "hN_lo",
                   "a_psum", "a_hi", "a_lo", "r_psum", "r_ready", "rh_ready", "rh_hi", "rh_lo",
                   "z_psum", "z_ready", "hv_psum", "hv_ready", "diff_ready", "gated_ready", "h_new",
                   "yo_ready", "stats3", "mean3", "rstd3_ready", "normed3", "stored")

        BANK = ["xT0", "s2", "h", "p", "att", "xT1", "yT", "rel", "v", "norm", "out1", "xT2", "sup", "out2"]
        PARTS = ["xT0", "h", "p", "xT1", "yT", "xT2", "first half of support", "support"]

        def in_bank(g, what):
            return len(BANK) * g + BANK.index(what) + 1

        def parted(g, what):
            return len(PARTS) * g + PARTS.index(what) + 1

        def flat(t):
            return t[:, :, :].rearrange("p a b -> p (a b)")

        def f32(t):
            return t.bitcast(F32)

        x_rows = x.rearrange("b (t p) d -> b p t d", p=P)
        out_rows = out.rearrange("b (t p) d -> b p t d", p=P)
        LOADS = 24

        def once(eng, semaphore, uses):
            if not isinstance(uses, int) or uses > 0:
                eng.wait_ge(semaphore, uses)

        block = ctx.enter_context(nc.Block())

        @block.sync
        def _(sp):
            def rows(w):
                return w.rearrange("(t p) d -> p t d", p=P)

            loads = [(adjN[:, :, :], rows(adj)), (w0_s, rows(W0)), (wq_s, rows(Wq)), (wk_s, rows(Wk)),
                     (wv_s, rows(Wv)), (w2_s, rows(W2)), (u3_s, rows(u3_w)), (u5_s, rows(u5_w)),
                     (arow[:, 0, :], a0[0:D, :].rearrange("f o -> o f").broadcast_to([P, D])),
                     (arow[:, 1, :], a0[D:2 * D, :].rearrange("f o -> o f").broadcast_to([P, D])),
                     (beta_c[:, :], beta.rearrange("(a o) -> a o", a=1).broadcast_to([P, 1])),
                     (bias2_r[:, 0:D], bias2.rearrange("(a o) -> a o", a=1).broadcast_to([P, D])),
                     (bias2_r[:, D:2 * D], bias2.rearrange("(a o) -> a o", a=1).broadcast_to([P, D]))]
            for staged, w in ((w3_s, w3_w), (w4_s, w4_w), (w5_s, w5_w)):
                for half in range(2):
                    loads.append((staged[half][:, :, :], rows(w[:, half * D:half * D + D])))
            for k, bvec in enumerate((w3_b, u3_b, w4_b, w5_b, u5_b)):
                loads.append((braw[:, k, :], bvec.rearrange("(t p) -> p t", p=P)))
            assert len(loads) == LOADS
            for dst, src in loads:
                sp.dma_start(dst, src, allow_slow_non_contiguous=True).then_inc(c["loaded"], 16)

            def row(dram, g, b):
                if isinstance(g, int):
                    return dram[g * BG + b]
                return dram[bass.ds(g * BG + b, 1)].rearrange("o p t d -> p (o t) d")

            def load_x(g, b):
                once(sp, f[b]["y_ready"], 3 * g - 2)
                sp.dma_start(X0[b][:, :, :], row(x_rows, g, b)).then_inc(f[b]["x_loaded"], 16)

            def keep_x3(g, b):
                sp.wait_ge(f[b]["x3_ready"], 2 * g + 2)
                once(sp, f[b]["yo_ready"], g)
                sp.dma_start(XR[b][:, :, :], X3[b][:, :, :]).then_inc(f[b]["xr_copied"], 16)

            def store(g, b):
                sp.wait_ge(f[b]["normed3"], 2 * g + 2)
                sp.dma_start(row(out_rows, g, b), YO[b][:, :, :]).then_inc(f[b]["stored"], 16)

            for g in range(2):
                for b in range(BG):
                    load_x(g, b)
            for b in range(BG):
                sp.wait_ge(c["setup_done"], 1)
                keep_x3(0, b)
            for b in range(BG):
                load_x(2, b)
            for b in range(BG):
                store(0, b)
            with sp.Fori(1, G - 2) as i:
                for b in range(BG):
                    keep_x3(i, b)
                for b in range(BG):
                    load_x(i + 2, b)
                for b in range(BG):
                    store(i, b)
            for g in range(G - 2, G):
                for b in range(BG):
                    keep_x3(g, b)
                for b in range(BG):
                    store(g, b)
            for b in range(BG):
                sp.wait_ge(f[b]["stored"], 16 * G)

        @block.tensor
        def _(pe):
            def passes(o, ls, rs_, start, stop):
                terms = []
                for (lh, ll), (rh_, rl) in zip(ls, rs_):
                    terms += [(lh, rh_), (lh, rl), (ll, rh_)]
                for j, (l, r) in enumerate(terms):
                    mm = pe.matmul(o, l, r, start=start and j == 0, stop=stop and j == len(terms) - 1,
                                   skip_group_check=True)
                return mm

            def cut(s, k, a, b):
                return s[0][:, k, a:b], s[1][:, k, a:b]

            def product(bank, left, right, n_right, start=True, stop=True):
                for i in range(2):
                    mm = passes(bank[:, i * 256:i * 256 + n_right], [cut(left, k, i * P, i * P + P) for k in range(2)],
                                [cut(right, k, 0, n_right) for k in range(2)], start and i == 0, stop)
                return mm

            def transpose_tiles(dst, src, start=True):
                for i in range(2):
                    for k in range(2):
                        mm = pe.transpose(dst[:, i * 256 + k * P:i * 256 + k * P + P], src[:, k, i * P:i * P + P],
                                          ident[:, :])
                return mm

            pe.wait_ge(c["loaded"], 16 * LOADS)
            pe.wait_ge(c["ident_ready"], 1)
            order = [(adjN, 0), (wv_s, 0), (u3_s, 0), (w4_sum, 3), (w34_sum, 3), (w5_sum, 3), (u5_s, 0)]
            for n, (src, need) in enumerate(order):
                if need:
                    pe.wait_ge(c["w_prep"], need)
                if n >= 2:
                    pe.wait_ge(c["matrix_lo"], n - 1)
                transpose_tiles(pF[n % 2], src).then_inc(c["matrix_in_psum"], 1)
            n = len(order)
            pe.wait_ge(c["matrix_lo"], n - 1)
            for i in range(2):
                for k in range(2):
                    mm = pe.matmul(pF[n % 2][:, i * 256:i * 256 + 256], wq_s[:, k, i * P:i * P + P], wk_s[:, k, :],
                                   start=(k == 0), stop=(k == 1))
            mm.then_inc(c["matrix_in_psum"], 1)
            pe.wait_ge(c["wa_ready"], 3)
            for k in range(DT):
                mm = pe.transpose(pA[0][:, k * P:k * P + P], V[1][:, k, 0:P], ident[:, :])
            mm.then_inc(c["wa1_turned"], 1)
            pe.wait_ge(c["setup_done"], 1)

            def x_to_T(g, b, layer):
                s = f[b]
                if layer == 0:
                    pe.wait_ge(s["x_loaded"], 16 * g + 16)
                    once(pe, s["y_ready"], 3 * g)
                elif layer == 1:
                    pe.wait_ge(s["x1_ready"], 2 * g + 2)
                else:
                    pe.wait_ge(s["x2_ready"], 2 * g + 2)
                transpose_tiles(pF[b], (X0, X1, X2)[layer][b]).then_inc(s["front_psum"], 1)

            def l0_scores(g, b):
                s = f[b]
                pe.wait_ge(s["part_hi"], parted(g, "xT0"))
                pe.wait_ge(s["part_lo"], parted(g, "xT0"))
                mm = passes(pF[b][:, 0:N], [cut(wa2, k, 0, P) for k in range(2)], [cut(xT[b], k, 0, N) for k in range(2)],
                       True, True)
                mm.then_inc(s["front_psum"], 1)

            def l0_project(g, b):
                s = f[b]
                pe.wait_ge(s["w02_ready"], 2 * g + 2)
                pe.wait_ge(s["lrelu_ready"], 2 * g + 2)
                product(pF[b], xT[b], w0, D).then_inc(s["front_psum"], 1)

            def l0_turn(g, b):
                s = f[b]
                pe.wait_ge(s["part_hi"], parted(g, "h"))
                pe.wait_ge(s["part_lo"], parted(g, "h"))
                pe.wait_ge(s["hb_ready"], g + 1)
                pe.wait_ge(s["exp_ready"], 2 * g + 2)
                transpose_tiles(pF[b], W02[b]).then_inc(s["front_psum"], 1)

            def l0_attend(g, b):
                s = f[b]
                pe.wait_ge(s["part_hi"], parted(g, "p"))
                pe.wait_ge(s["part_lo"], parted(g, "p"))
                product(pF[b], pt[b], hs[b], D).then_inc(s["front_psum"], 1)

            def l1_y(g, b):
                s = f[b]
                pe.wait_ge(s["part_hi"], parted(g, "xT1"))
                pe.wait_ge(s["part_lo"], parted(g, "xT1"))
                product(pF[b], gqk, xT[b], N).then_inc(s["front_psum"], 1)

            def l1_rel(g, b):
                s = f[b]
                pe.wait_ge(s["part_hi"], parted(g, "yT"))
                pe.wait_ge(s["part_lo"], parted(g, "yT"))
                product(pF[b], xT[b], yT[b], N).then_inc(s["front_psum"], 1)

            def l1_v(g, b):
                s = f[b]
                pe.wait_ge(s["rel_masked"], g + 1)
                product(pF[b], xT[b], wv, D).then_inc(s["front_psum"], 1)

            def l1_norm(g, b):
                s = f[b]
                pe.wait_ge(s["vv_hi"], g + 1)
                pe.wait_ge(s["vv_lo"], g + 1)
                pe.wait_ge(s["rel_hi"], 2 * g + 2)
                for i in range(NT):
                    for k in range(NT):
                        mm = pe.matmul(pF[b][:, i:i + 1], SQ[b][:, k, i * P:i * P + P], ones[:, 0:1],
                                       start=(k == 0), stop=(k == NT - 1), skip_group_check=True)
                mm.then_inc(s["front_psum"], 1)

            def l1_out(g, b):
                s = f[b]
                pe.wait_ge(s["norm_copied"], g + 1)
                pe.wait_ge(s["rel_hi"], 2 * g + 1)
                pe.wait_ge(s["rel_lo"], g + 1)
                product(pF[b], pt[b], hs[b], D).then_inc(s["front_psum"], 1)

            def l2_support(g, b):
                s = f[b]
                pe.wait_ge(s["part_hi"], parted(g, "xT2"))
                pe.wait_ge(s["part_lo"], parted(g, "xT2"))
                product(pF[b], xT[b], w2, D).then_inc(s["front_psum"], 1)

            def l2_out(g, b):
                s = f[b]
                pe.wait_ge(s["part_hi"], parted(g, "support"))
                pe.wait_ge(s["part_lo"], parted(g, "support"))
                product(pF[b], adjT, hs[b], D).then_inc(s["front_psum"], 1)

            def x3_to_T(g, b):
                s = f[b]
                pe.wait_ge(s["x3_ready"], 2 * g + 2)
                once(pe, s["yo_ready"], g)
                transpose_tiles(pA[b], X3[b]).then_inc(s["x3T_psum"], 1)

            def aggregate(g, b, t):
                s = f[b]
                pe.wait_ge(s["hN_hi"], 3 * g + t + 1)
                pe.wait_ge(s["hN_lo"], 3 * g + t + 1)
                pe.wait_ge(s["hT_copied"], g + 1)
                product(pA[b], hN[b], adjT, N).then_inc(s["a_psum"], 1)

            def gate_u3(g, b, t):
                s = f[b]
                pe.wait_ge(s["hT_hi"], 3 * g + t + 1)
                pe.wait_ge(s["hT_lo"], 3 * g + t + 1)
                once(pe, s["z_ready"], 2 * (3 * g + t))
                product(pR[b], u3, hTs[b], N, True, False)

            def gate_r(g, b, t):
                s = f[b]
                pe.wait_ge(s["a_hi"], 3 * g + t + 1)
                pe.wait_ge(s["a_lo"], 3 * g + t + 1)
                product(pR[b], w4, aT[b], N, False, True).then_inc(s["r_psum"], 1)

            def candidate_a(g, b, t):
                s = f[b]
                pe.wait_ge(s["a_hi"], 3 * g + t + 1)
                pe.wait_ge(s["a_lo"], 3 * g + t + 1)
                once(pe, s["hv_ready"], 2 * (3 * g + t))
                product(pH[b], w5, aT[b], N, True, False)

            def gate_z(g, b, t):
                s = f[b]
                pe.wait_ge(s["r_ready"], 2 * (3 * g + t + 1))
                product(pR[b], w34, aT[b], N, False, True).then_inc(s["z_psum"], 1)

            def candidate_rh(g, b, t):
                s = f[b]
                pe.wait_ge(s["rh_hi"], 3 * g + t + 1)
                pe.wait_ge(s["rh_lo"], 3 * g + t + 1)
                product(pH[b], u5, rhs[b], N, False, True).then_inc(s["hv_psum"], 1)

            def h_to_N(g, b, t):
                s = f[b]
                pe.wait_ge(s["h_new"], 3 * g + t + 1)
                transpose_tiles(pA[b], hT[b]).then_inc(s["hN_psum"], 1)

            def merged(front, gf, back, gb):
                def fr(step, *which):
                    if front:
                        step(gf, *which)

                def bk(step, *which):
                    if back:
                        step(gb, *which)

                fr(x_to_T, 0, 0)
                fr(x_to_T, 1, 0)
                bk(x3_to_T, 0)
                fr(l0_scores, 1)
                fr(l0_scores, 0)
                bk(x3_to_T, 1)
                bk(aggregate, 0, 0)
                bk(gate_u3, 0, 0)
                fr(l0_project, 1)
                fr(l0_project, 0)
                bk(gate_r, 0, 0)
                bk(aggregate, 1, 0)
                bk(candidate_a, 0, 0)
                fr(l0_turn, 0)
                bk(gate_u3, 1, 0)
                bk(candidate_rh, 0, 0)
                bk(gate_z, 0, 0)
                bk(candidate_a, 1, 0)
                bk(gate_r, 1, 0)
                bk(h_to_N, 0, 0)
                fr(l0_attend, 0)
                bk(gate_u3, 0, 1)
                bk(aggregate, 0, 1)
                bk(candidate_rh, 1, 0)
                fr(l0_turn, 1)
                bk(gate_z, 1, 0)
                bk(candidate_a, 0, 1)
                fr(l0_attend, 1)
                bk(h_to_N, 1, 0)
                fr(x_to_T, 0, 1)
                bk(gate_r, 0, 1)
                bk(gate_u3, 1, 1)
                bk(gate_z, 0, 1)
                bk(aggregate, 1, 1)
                bk(candidate_rh, 0, 1)
                fr(l1_y, 0)
                fr(x_to_T, 1, 1)
                bk(candidate_a, 1, 1)
                bk(gate_r, 1, 1)
                fr(l1_y, 1)
                bk(gate_z, 1, 1)
                bk(h_to_N, 0, 1)
                fr(l1_rel, 1)
                bk(gate_u3, 0, 2)
                bk(aggregate, 0, 2)
                fr(l1_rel, 0)
                bk(candidate_rh, 1, 1)
                fr(l1_v, 0)
                bk(candidate_a, 0, 2)
                fr(l1_v, 1)
                fr(l1_norm, 0)
                bk(h_to_N, 1, 1)
                fr(l1_out, 0)
                bk(gate_u3, 1, 2)
                bk(aggregate, 1, 2)
                bk(gate_r, 0, 2)
                fr(l1_norm, 1)
                fr(x_to_T, 0, 2)
                fr(l1_out, 1)
                bk(gate_r, 1, 2)
                fr(l2_support, 0)
                bk(candidate_rh, 0, 2)
                bk(gate_z, 0, 2)
                fr(l2_out, 0)
                bk(candidate_a, 1, 2)
                fr(x_to_T, 1, 2)
                bk(candidate_rh, 1, 2)
                bk(h_to_N, 0, 2)
                bk(gate_z, 1, 2)
                fr(l2_support, 1)
                bk(h_to_N, 1, 2)
                fr(l2_out, 1)

            merged(True, 0, False, None)
            merged(True, 1, True, 0)
            with pe.Fori(1, G - 1) as i:
                merged(True, i + 1, True, i)
            merged(False, None, True, G - 1)

        @block.scalar
        def _(act):
            def copy(o, i):
                return act.activation(o, i, ACT.Copy)

            targets = [adjT, wv, u3, w4, w34, w5, u5, gqk]
            for n, t in enumerate(targets):
                act.wait_ge(c["matrix_in_psum"], n + 1)
                act.activation(flat(t[0]), pF[n % 2][:, :], ACT.Copy,
                               scale=0.5 if t is u5 else 1.0).then_inc(c["matrix_hi"], 1)
            act.wait_ge(c["loaded"], 16 * LOADS)
            copy(w0[0][:, :, :], w0_s).then_inc(c["direct_hi"], 1)
            copy(w2[0][:, :, :], w2_s).then_inc(c["direct_hi"], 1)
            act.wait_ge(c["setup_done"], 1)

            def xT_hi(g, b, layer):
                s = f[b]
                act.wait_ge(s["front_psum"], in_bank(g, f"xT{layer}"))
                copy(flat(xT[b][0]), pF[b][:, :]).then_inc(s["part_hi"], 1)

            def l0_w02(g, b):
                s = f[b]
                act.wait_ge(s["front_psum"], in_bank(g, "s2"))
                act.wait_ge(s["s1_ready"], 3 * g + 3)
                for k in range(NT):
                    act.activation(W02[b][:, k, :], pF[b][:, 0:N], ACT.Identity,
                                   bias=s1[b][:, NT + k:NT + k + 1], scale=SLOPE).then_inc(s["w02_ready"], 1)

            def l0_exp(g, b):
                s = f[b]
                act.wait_ge(s["max_ready"], g + 1)
                for k in range(NT):
                    act.activation(W02[b][:, k, :], E2[b][:, k, :], ACT.Exp, bias=nmx[b][:, NT + k:NT + k + 1],
                                   accum_out=rs[b][:, k:k + 1]).then_inc(s["exp_ready"], 1)

            def l0_h_hi(g, b):
                act.wait_ge(f[b]["front_psum"], in_bank(g, "h"))
                copy(flat(hs[b][0]), pF[b][:, :]).then_inc(f[b]["part_hi"], 1)
                act.activation(flat(HB[b]), pF[b][:, :], ACT.Copy, scale=beta_c[:, 0:1]).then_inc(f[b]["hb_ready"], 1)

            def l0_p_hi(g, b):
                act.wait_ge(f[b]["front_psum"], in_bank(g, "p"))
                copy(flat(pt[b][0]), pF[b][:, :]).then_inc(f[b]["part_hi"], 1)

            def l0_elu(g, b):
                s = f[b]
                act.wait_ge(s["v_ready"], 2 * g + 2)
                act.activation(flat(HB[b]), flat(V[b]), ACT.Relu, scale=-1.0).then_inc(s["neg_ready"], 1)
                act.wait_ge(s["neg_ready"], g + 1)
                act.activation(flat(E[b]), flat(HB[b]), ACT.Exp, scale=-1.0).then_inc(s["elu_exp"], 1)

            def normalise(s, b, g, layer, o, ready):
                n = 3 * g + layer
                act.wait_ge(s["rstd_ready"], 3 * n + 3)
                for k in range(NT):
                    act.activation(o[:, k, :], Y[b][:, k, :], ACT.Identity, bias=ln[b][:, 3, k:k + 1],
                                   scale=ln[b][:, 1, k:k + 1]).then_inc(ready, 1)

            def norm0(g, b):
                normalise(f[b], b, g, 0, X1[b], f[b]["x1_ready"])

            def norm1(g, b):
                normalise(f[b], b, g, 1, X2[b], f[b]["x2_ready"])

            def norm2(g, b):
                once(act, f[b]["xr_copied"], 16 * g)
                once(act, f[b]["hN_lo"], 3 * g - 2)
                normalise(f[b], b, g, 2, X3[b], f[b]["x3_ready"])

            def norm3(g, b):
                s = f[b]
                act.wait_ge(s["rstd3_ready"], 3 * g + 3)
                for k in range(NT):
                    act.activation(YO[b][:, k, :], YO[b][:, k, :], ACT.Identity, bias=ln3[b][:, 3, k:k + 1],
                                   scale=ln3[b][:, 1, k:k + 1]).then_inc(s["normed3"], 1)

            def l1_y_hi(g, b):
                act.wait_ge(f[b]["front_psum"], in_bank(g, "yT"))
                copy(flat(yT[b][0]), pF[b][:, :]).then_inc(f[b]["part_hi"], 1)

            def l1_rel_hi(g, b):
                s = f[b]
                act.wait_ge(s["rel_masked"], g + 1)
                copy(flat(pt[b][0]), flat(R[b])).then_inc(s["rel_hi"], 1)
                act.activation(flat(SQ[b]), flat(R[b]), ACT.Square).then_inc(s["rel_hi"], 1)

            def l1_v_hi(g, b):
                act.wait_ge(f[b]["front_psum"], in_bank(g, "v"))
                copy(flat(hs[b][0]), pF[b][:, :]).then_inc(f[b]["vv_hi"], 1)

            def l2_sup_hi(g, b):
                act.wait_ge(f[b]["front_psum"], in_bank(g, "sup"))
                for k in range(NT):
                    act.activation(hs[b][0][:, k, :], pF[b][:, k * D:k * D + D], ACT.Copy,
                                   scale=dinv[:, k:k + 1]).then_inc(f[b]["part_hi"], 1)

            def take_x3(g, b):
                s = f[b]
                act.wait_ge(s["x3T_psum"], g + 1)
                copy(flat(hT[b]), pA[b][:, :]).then_inc(s["hT_copied"], 1)
                copy(flat(hN[b][0]), flat(X3[b])).then_inc(s["hN_hi"], 1)
                act.wait_ge(s["hT_copied"], g + 1)
                copy(flat(hTs[b][0]), flat(hT[b])).then_inc(s["hT_hi"], 1)

            def a_hi(g, b, t):
                s = f[b]
                act.wait_ge(s["a_psum"], 3 * g + t + 1)
                copy(flat(aT[b][0]), pA[b][:, :]).then_inc(s["a_hi"], 1)

            def gate_r(g, b, t):
                s = f[b]
                act.wait_ge(s["r_psum"], 3 * g + t + 1)
                for i in range(DT):
                    act.activation(tr[b][:, i, :], pR[b][:, i * N:i * N + N], ACT.Tanh, bias=br[:, i:i + 1],
                                   scale=0.5).then_inc(s["r_ready"], 1)

            def rh_hi(g, b, t):
                act.wait_ge(f[b]["rh_ready"], 3 * g + t + 1)
                copy(flat(rhs[b][0]), flat(rh[b])).then_inc(f[b]["rh_hi"], 1)

            def gate_z(g, b, t):
                s = f[b]
                act.wait_ge(s["z_psum"], 3 * g + t + 1)
                for i in range(DT):
                    act.activation(tz[b][:, i, :], pR[b][:, i * N:i * N + N], ACT.Tanh, bias=bz[:, i:i + 1],
                                   scale=0.5).then_inc(s["z_ready"], 1)

            def cand(g, b, t):
                s = f[b]
                act.wait_ge(s["hv_psum"], 3 * g + t + 1)
                for i in range(DT):
                    act.activation(hv[b][:, i, :], pH[b][:, i * N:i * N + N], ACT.Tanh,
                                   bias=bh[:, i:i + 1]).then_inc(s["hv_ready"], 1)

            def hT_hi(g, b, t):
                act.wait_ge(f[b]["h_new"], 3 * g + t + 1)
                copy(flat(hTs[b][0]), flat(hT[b])).then_inc(f[b]["hT_hi"], 1)

            def hN_hi(g, b, t):
                act.wait_ge(f[b]["hN_psum"], 3 * g + t + 1)
                copy(flat(hN[b][0]), pA[b][:, :]).then_inc(f[b]["hN_hi"], 1)

            def merged(front, gf, back, gb):
                def fr(step, *which):
                    if front:
                        step(gf, *which)

                def bk(step, *which):
                    if back:
                        step(gb, *which)

                fr(xT_hi, 0, 0)
                fr(xT_hi, 1, 0)
                bk(take_x3, 0)
                fr(l0_w02, 1)
                fr(l0_w02, 0)
                bk(take_x3, 1)
                bk(a_hi, 0, 0)
                fr(l0_exp, 1)
                fr(l0_exp, 0)
                fr(l0_h_hi, 1)
                fr(l0_h_hi, 0)
                bk(gate_r, 0, 0)
                bk(a_hi, 1, 0)
                bk(rh_hi, 0, 0)
                fr(l0_p_hi, 0)
                bk(cand, 0, 0)
                bk(gate_z, 0, 0)
                bk(hT_hi, 0, 0)
                bk(gate_r, 1, 0)
                bk(hN_hi, 0, 0)
                bk(rh_hi, 1, 0)
                fr(l0_elu, 0)
                bk(a_hi, 0, 1)
                bk(cand, 1, 0)
                fr(l0_p_hi, 1)
                bk(gate_z, 1, 0)
                fr(norm0, 0)
                bk(hT_hi, 1, 0)
                bk(hN_hi, 1, 0)
                fr(l0_elu, 1)
                fr(xT_hi, 0, 1)
                bk(gate_r, 0, 1)
                bk(rh_hi, 0, 1)
                bk(gate_z, 0, 1)
                bk(a_hi, 1, 1)
                fr(norm0, 1)
                bk(cand, 0, 1)
                fr(l1_y_hi, 0)
                fr(xT_hi, 1, 1)
                bk(hT_hi, 0, 1)
                bk(gate_r, 1, 1)
                fr(l1_y_hi, 1)
                bk(rh_hi, 1, 1)
                bk(gate_z, 1, 1)
                bk(hN_hi, 0, 1)
                fr(l1_rel_hi, 1)
                bk(a_hi, 0, 2)
                fr(l1_rel_hi, 0)
                bk(cand, 1, 1)
                fr(l1_v_hi, 0)
                bk(hT_hi, 1, 1)
                fr(l1_v_hi, 1)
                bk(hN_hi, 1, 1)
                bk(a_hi, 1, 2)
                fr(norm1, 0)
                bk(gate_r, 0, 2)
                fr(xT_hi, 0, 2)
                bk(rh_hi, 0, 2)
                bk(gate_r, 1, 2)
                fr(l2_sup_hi, 0)
                bk(rh_hi, 1, 2)
                fr(norm1, 1)
                bk(cand, 0, 2)
                bk(gate_z, 0, 2)
                fr(xT_hi, 1, 2)
                bk(cand, 1, 2)
                fr(norm2, 0)
                bk(gate_z, 1, 2)
                fr(l2_sup_hi, 1)
                bk(norm3, 0)
                bk(norm3, 1)
                fr(norm2, 1)

            merged(True, 0, False, None)
            merged(True, 1, True, 0)
            with act.Fori(1, G - 1) as i:
                merged(True, i + 1, True, i)
            merged(False, None, True, G - 1)

        @block.vector
        def _(dve):
            dve.wait_ge(c["loaded"], 16 * LOADS)
            dve.tensor_tensor(w4_sum, w4_s[0][:, :, :], w4_s[1][:, :, :], ALU.add).then_inc(c["w_prep"], 1)
            dve.tensor_tensor(w5_sum, w5_s[0][:, :, :], w5_s[1][:, :, :], ALU.add).then_inc(c["w_prep"], 1)
            dve.tensor_tensor(w34_sum, w3_s[0][:, :, :], w3_s[1][:, :, :], ALU.add).then_inc(c["wa_sum"], 1)
            dve.wait_ge(c["wa_sum"], 1)
            dve.wait_ge(c["w_prep"], 2)
            dve.tensor_tensor(w34_sum, w34_sum, w4_sum, ALU.subtract).then_inc(c["w_prep"], 1)
            for k in range(DT):
                for j in range(2):
                    dve.tensor_tensor_reduce(V[j][:, k, :], w0_s[:, k, :], arow[:, j, :], 1.0, 0.0, ALU.mult, ALU.add,
                                             wsum[:, 2 * k + j:2 * k + j + 1]).then_inc(c["wa_sum"], 1)
            dve.tensor_reduce(deg[:, 0:NT], adjN[:, :, :], mybir.AxisListType.X, ALU.add).then_inc(c["deg_step"], 1)
            dve.wait_ge(c["deg_step"], 1)
            dve.tensor_scalar(deg[:, NT:2 * NT], deg[:, 0:NT], 1e-38, None, ALU.max).then_inc(c["deg_step"], 1)
            dve.tensor_scalar(deg[:, 2 * NT:3 * NT], deg[:, 0:NT], 0.0, None, ALU.is_gt).then_inc(c["deg_step"], 1)
            dve.wait_ge(c["deg_pow"], 1)
            dve.wait_ge(c["deg_step"], 3)
            dve.tensor_tensor(dinv[:, :], deg[:, 3 * NT:4 * NT], deg[:, 2 * NT:3 * NT], ALU.mult).then_inc(c["deg_step"], 1)
            dve.wait_ge(c["wa_sum"], 5)
            dve.wait_ge(c["const_ready"], 3)
            dve.memset(Y[0][:, 0, 0:P], 1.0).then_inc(c["wa_ready"], 1)
            dve.wait_ge(c["wa_ready"], 1)
            for j in range(2):
                for k in range(DT):
                    dve.tensor_scalar(V[1 - j][:, k, 0:P], Y[0][:, 0, 0:P], wsum[:, 2 * k + j:2 * k + j + 1], None,
                                             ALU.mult).then_inc(c["wa_ready"], 1)
            dve.wait_ge(c["wa_ready"], 5)
            dve.tensor_copy(wa2[0][:, :, :], V[0][:, :, 0:P]).then_inc(c["wa_ready"], 1)
            dve.wait_ge(c["wa_ready"], 6)
            dve.tensor_tensor(wa2[1][:, :, :], V[0][:, :, 0:P], f32(wa2[0][:, :, :]),
                              ALU.subtract).then_inc(c["wa_ready"], 1)
            dve.tensor_tensor(bz[:, :], braw[:, 0, :], braw[:, 1, :], ALU.add).then_inc(c["wa_ready"], 1)
            dve.tensor_tensor(br[:, :], braw[:, 2, :], braw[:, 1, :], ALU.add).then_inc(c["wa_ready"], 1)
            dve.tensor_tensor(bh[:, :], braw[:, 3, :], braw[:, 4, :], ALU.add).then_inc(c["wa_ready"], 1)
            dve.wait_ge(c["wa_ready"], 10)
            dve.tensor_scalar(bz[:, :], bz[:, :], 0.5, None, ALU.mult).then_inc(c["wa_ready"], 1)
            dve.tensor_scalar(br[:, :], br[:, :], 0.5, None, ALU.mult).then_inc(c["wa_ready"], 1)
            targets = [adjT, wv, u3, w4, w34, w5, u5, gqk]
            for n, t in enumerate(targets):
                dve.wait_ge(c["matrix_hi"], n + 1)
                if t is u5:
                    dve.scalar_tensor_tensor(flat(t[1]), pF[n % 2][:, :], 0.5, f32(flat(t[0])), ALU.mult,
                                             ALU.subtract).then_inc(c["matrix_lo"], 1)
                else:
                    dve.tensor_tensor(flat(t[1]), pF[n % 2][:, :], f32(flat(t[0])),
                                      ALU.subtract).then_inc(c["matrix_lo"], 1)
            dve.wait_ge(c["direct_hi"], 2)
            dve.tensor_tensor(w0[1][:, :, :], w0_s, f32(w0[0][:, :, :]), ALU.subtract).then_inc(c["wa_ready"], 1)
            dve.tensor_tensor(w2[1][:, :, :], w2_s, f32(w2[0][:, :, :]), ALU.subtract).then_inc(c["wa_ready"], 1)
            dve.wait_ge(c["wa_ready"], 14)
            dve.wait_ge(c["wa1_turned"], 1)
            dve.tensor_copy(wa1[:, :], pA[0][:, 0:D]).then_inc(c["wa_ready"], 1)
            dve.wait_ge(c["wa_ready"], 15)
            dve.wait_ge(c["deg_step"], 4)
            dve.wait_ge(c["matrix_lo"], 8)
            dve.memset(deg[:, 0:1], 0.0).then_inc(c["setup_done"], 1)

            def lo(o, full, hi):
                return dve.tensor_tensor(o, full, f32(hi), ALU.subtract)

            def statistics(s, rows_of, sums, means, small, n, ready, mean_ready):
                for k in range(NT):
                    dve.bn_stats(sums[:, k, :], rows_of[:, k, :]).then_inc(ready, 1)
                dve.wait_ge(ready, 2 * n + 2)
                dve.memset(scratch[:, 0:1], 0.0)
                for k in range(NT):
                    dve.bn_aggr(means[:, k, :], sums[:, k, :]).then_inc(mean_ready, 1)
                dve.wait_ge(mean_ready, 3 * n + 2)
                dve.tensor_scalar(small[:, 2, :], means[:, :, 0], -1.0, None, ALU.mult).then_inc(mean_ready, 1)

            def stats(g, b, layer):
                s = f[b]
                n = 3 * g + layer
                dve.wait_ge(s["y_ready"], n + 1)
                statistics(s, Y[b], st[b], mv[b], ln[b], n, s["stats_ready"], s["mean_ready"])

            def xT_lo(g, b, layer):
                s = f[b]
                dve.wait_ge(s["part_hi"], parted(g, f"xT{layer}"))
                lo(flat(xT[b][1]), pF[b][:, :], flat(xT[b][0])).then_inc(s["part_lo"], 1)

            def l0_s1(g, b):
                s = f[b]
                dve.wait_ge(s["x_loaded"], 16 * g + 16)
                for k in range(NT):
                    dve.tensor_tensor_reduce(V[b][:, k, :], X0[b][:, k, :], wa1[:, :], 1.0, 0.0, ALU.mult, ALU.add,
                                             s1[b][:, k:k + 1]).then_inc(s["s1_ready"], 1)
                dve.wait_ge(s["s1_ready"], 3 * g + 2)
                dve.tensor_scalar(s1[b][:, NT:2 * NT], s1[b][:, 0:NT], SLOPE, None, ALU.mult).then_inc(s["s1_ready"], 1)

            def l0_mask(g, b):
                s = f[b]
                dve.wait_ge(s["w02_ready"], 2 * g + 2)
                for k in range(NT):
                    dve.scalar_tensor_tensor(E[b][:, k, :], pF[b][:, 0:N], s1[b][:, k:k + 1], W02[b][:, k, :],
                                             ALU.add, ALU.max).then_inc(s["lrelu_ready"], 1)
                dve.wait_ge(c["setup_done"], 1)
                dve.wait_ge(s["lrelu_ready"], 2 * g + 2)
                for k in range(NT):
                    dve.tensor_tensor_reduce(E2[b][:, k, :], E[b][:, k, :], adjN[:, k, :], 1.0, -3e38, ALU.mult, ALU.max,
                                             nmx[b][:, k:k + 1]).then_inc(s["masked_ready"], 1)
                dve.wait_ge(s["masked_ready"], 2 * g + 2)
                dve.tensor_scalar(nmx[b][:, NT:2 * NT], nmx[b][:, 0:NT], -1.0, None, ALU.mult).then_inc(s["max_ready"], 1)

            def l0_h_lo(g, b):
                s = f[b]
                dve.wait_ge(s["part_hi"], parted(g, "h"))
                dve.wait_ge(s["hb_ready"], g + 1)
                lo(flat(hs[b][1]), pF[b][:, :], flat(hs[b][0])).then_inc(s["part_lo"], 1)

            def l0_p_lo(g, b):
                s = f[b]
                dve.wait_ge(s["part_hi"], parted(g, "p"))
                lo(flat(pt[b][1]), pF[b][:, :], flat(pt[b][0])).then_inc(s["part_lo"], 1)
                dve.wait_ge(s["exp_ready"], 2 * g + 2)
                dve.reciprocal(rs[b][:, NT:2 * NT], rs[b][:, 0:NT]).then_inc(s["rinv_ready"], 1)

            def l0_elu_in(g, b):
                s = f[b]
                dve.wait_ge(s["front_psum"], in_bank(g, "att"))
                dve.wait_ge(s["rinv_ready"], g + 1)
                for k in range(NT):
                    dve.scalar_tensor_tensor(V[b][:, k, :], pF[b][:, k * D:k * D + D], rs[b][:, NT + k:NT + k + 1],
                                             HB[b][:, k, :], ALU.mult, ALU.add).then_inc(s["v_ready"], 1)

            def l0_elu_out(g, b):
                s = f[b]
                dve.wait_ge(s["elu_exp"], g + 1)
                dve.scalar_tensor_tensor(flat(V[b]), flat(V[b]), 0.0, flat(E[b]), ALU.max,
                                         ALU.add).then_inc(s["elu_ready"], 1)
                dve.wait_ge(s["elu_ready"], g + 1)
                dve.scalar_tensor_tensor(flat(Y[b]), flat(V[b]), -1.0, flat(X0[b]), ALU.add,
                                         ALU.add).then_inc(s["y_ready"], 1)

            def l1_y_lo(g, b):
                dve.wait_ge(f[b]["part_hi"], parted(g, "yT"))
                lo(flat(yT[b][1]), pF[b][:, :], flat(yT[b][0])).then_inc(f[b]["part_lo"], 1)

            def l1_mask(g, b):
                s = f[b]
                dve.wait_ge(s["front_psum"], in_bank(g, "rel"))
                dve.tensor_tensor(flat(R[b]), pF[b][:, :], flat(adjN), ALU.mult).then_inc(s["rel_masked"], 1)

            def l1_rel_lo(g, b):
                s = f[b]
                dve.wait_ge(s["rel_hi"], 2 * g + 1)
                lo(flat(pt[b][1]), flat(R[b]), flat(pt[b][0])).then_inc(s["rel_lo"], 1)

            def l1_v_lo(g, b):
                dve.wait_ge(f[b]["vv_hi"], g + 1)
                lo(flat(hs[b][1]), pF[b][:, :], flat(hs[b][0])).then_inc(f[b]["vv_lo"], 1)

            def l1_norm(g, b):
                dve.wait_ge(f[b]["front_psum"], in_bank(g, "norm"))
                dve.tensor_copy(rn[b][:, 0:NT], pF[b][:, 0:NT]).then_inc(f[b]["norm_copied"], 1)

            def l1_residual(g, b):
                s = f[b]
                dve.wait_ge(s["front_psum"], in_bank(g, "out1"))
                dve.wait_ge(s["rn_ready"], g + 1)
                for k in range(NT):
                    last = dve.scalar_tensor_tensor(Y[b][:, k, :], pF[b][:, k * D:k * D + D],
                                                    rn[b][:, NT + k:NT + k + 1], X1[b][:, k, :], ALU.mult, ALU.add)
                last.then_inc(s["y_ready"], 1)

            def l2_sup_lo(g, b):
                s = f[b]
                dve.wait_ge(s["part_hi"], parted(g, "support"))
                for k in range(NT):
                    dve.scalar_tensor_tensor(hs[b][1][:, k, :], pF[b][:, k * D:k * D + D], dinv[:, k:k + 1],
                                             f32(hs[b][0][:, k, :]), ALU.mult, ALU.subtract).then_inc(s["part_lo"], 1)

            def l2_residual(g, b):
                s = f[b]
                dve.wait_ge(s["front_psum"], in_bank(g, "out2"))
                dve.wait_ge(s["xb_ready"], g + 1)
                for k in range(NT):
                    last = dve.scalar_tensor_tensor(Y[b][:, k, :], pF[b][:, k * D:k * D + D],
                                                    dinv[:, k:k + 1], XB[b][:, k, :], ALU.mult, ALU.add)
                last.then_inc(s["y_ready"], 1)

            def take_x3(g, b):
                s = f[b]
                dve.wait_ge(s["hN_hi"], 3 * g + 1)
                lo(flat(hN[b][1]), flat(X3[b]), flat(hN[b][0])).then_inc(s["hN_lo"], 1)
                dve.wait_ge(s["hT_hi"], 3 * g + 1)
                lo(flat(hTs[b][1]), flat(hT[b]), flat(hTs[b][0])).then_inc(s["hT_lo"], 1)

            def a_lo(g, b, t):
                dve.wait_ge(f[b]["a_hi"], 3 * g + t + 1)
                lo(flat(aT[b][1]), pA[b][:, :], flat(aT[b][0])).then_inc(f[b]["a_lo"], 1)

            def reset(g, b, t):
                dve.wait_ge(f[b]["r_ready"], 2 * (3 * g + t + 1))
                dve.scalar_tensor_tensor(flat(rh[b]), flat(tr[b]), 1.0, flat(hT[b]), ALU.add,
                                         ALU.mult).then_inc(f[b]["rh_ready"], 1)

            def rh_lo(g, b, t):
                dve.wait_ge(f[b]["rh_hi"], 3 * g + t + 1)
                lo(flat(rhs[b][1]), flat(rh[b]), flat(rhs[b][0])).then_inc(f[b]["rh_lo"], 1)

            def diff(g, b, t):
                n = 3 * g + t
                dve.wait_ge(f[b]["hv_ready"], 2 * n + 2)
                dve.tensor_tensor(flat(rh[b]), flat(hv[b]), flat(hT[b]), ALU.subtract).then_inc(f[b]["diff_ready"], 1)

            def gated(g, b, t):
                n = 3 * g + t
                dve.wait_ge(f[b]["diff_ready"], n + 1)
                dve.wait_ge(f[b]["z_ready"], 2 * n + 2)
                dve.scalar_tensor_tensor(flat(rh[b]), flat(tz[b]), 1.0, flat(rh[b]), ALU.add,
                                         ALU.mult).then_inc(f[b]["gated_ready"], 1)

            def h_new(g, b, t):
                dve.wait_ge(f[b]["gated_ready"], 3 * g + t + 1)
                dve.scalar_tensor_tensor(flat(hT[b]), flat(rh[b]), 0.5, flat(hT[b]), ALU.mult,
                                         ALU.add).then_inc(f[b]["h_new"], 1)

            def hT_lo(g, b, t):
                dve.wait_ge(f[b]["hT_hi"], 3 * g + t + 2)
                lo(flat(hTs[b][1]), flat(hT[b]), flat(hTs[b][0])).then_inc(f[b]["hT_lo"], 1)

            def hN_lo(g, b, t):
                dve.wait_ge(f[b]["hN_hi"], 3 * g + t + 2)
                lo(flat(hN[b][1]), pA[b][:, :], flat(hN[b][0])).then_inc(f[b]["hN_lo"], 1)

            def residual3(g, b):
                s = f[b]
                dve.wait_ge(s["hN_psum"], 3 * g + 3)
                dve.wait_ge(s["xr_copied"], 16 * g + 16)
                once(dve, s["stored"], 16 * g)
                dve.tensor_tensor(flat(YO[b]), pA[b][:, :], flat(XR[b]), ALU.add).then_inc(s["yo_ready"], 1)

            def stats3(g, b):
                s = f[b]
                dve.wait_ge(s["yo_ready"], g + 1)
                statistics(s, YO[b], st3[b], mv3[b], ln3[b], g, s["stats3"], s["mean3"])

            def merged(front, gf, back, gb):
                def fr(step, *which):
                    if front:
                        step(gf, *which)

                def bk(step, *which):
                    if back:
                        step(gb, *which)

                fr(l0_s1, 0)
                fr(l0_s1, 1)
                fr(xT_lo, 1, 0)
                fr(xT_lo, 0, 0)
                bk(take_x3, 0)
                fr(l0_mask, 1)
                fr(l0_mask, 0)
                bk(a_lo, 0, 0)
                bk(take_x3, 1)
                fr(l0_h_lo, 1)
                fr(l0_h_lo, 0)
                bk(reset, 0, 0)
                bk(a_lo, 1, 0)
                bk(rh_lo, 0, 0)
                fr(l0_p_lo, 0)
                bk(diff, 0, 0)
                bk(gated, 0, 0)
                bk(h_new, 0, 0)
                bk(hT_lo, 0, 0)
                bk(reset, 1, 0)
                bk(hN_lo, 0, 0)
                fr(l0_elu_in, 0)
                bk(rh_lo, 1, 0)
                fr(l0_elu_out, 0)
                bk(a_lo, 0, 1)
                fr(stats, 0, 0)
                fr(l0_p_lo, 1)
                bk(diff, 1, 0)
                bk(gated, 1, 0)
                bk(h_new, 1, 0)
                fr(l0_elu_in, 1)
                bk(hT_lo, 1, 0)
                bk(hN_lo, 1, 0)
                fr(l0_elu_out, 1)
                bk(reset, 0, 1)
                fr(stats, 1, 0)
                bk(rh_lo, 0, 1)
                fr(xT_lo, 0, 1)
                bk(a_lo, 1, 1)
                bk(diff, 0, 1)
                bk(gated, 0, 1)
                fr(l1_y_lo, 0)
                bk(h_new, 0, 1)
                fr(xT_lo, 1, 1)
                bk(hT_lo, 0, 1)
                bk(reset, 1, 1)
                fr(l1_y_lo, 1)
                bk(rh_lo, 1, 1)
                bk(hN_lo, 0, 1)
                fr(l1_mask, 1)
                fr(l1_rel_lo, 1)
                bk(a_lo, 0, 2)
                fr(l1_mask, 0)
                fr(l1_rel_lo, 0)
                bk(diff, 1, 1)
                fr(l1_v_lo, 0)
                bk(gated, 1, 1)
                bk(h_new, 1, 1)
                fr(l1_norm, 0)
                bk(hT_lo, 1, 1)
                fr(l1_v_lo, 1)
                bk(hN_lo, 1, 1)
                fr(l1_residual, 0)
                fr(stats, 0, 1)
                bk(a_lo, 1, 2)
                fr(l1_norm, 1)
                bk(reset, 0, 2)
                fr(xT_lo, 0, 2)
                fr(l1_residual, 1)
                bk(rh_lo, 0, 2)
                fr(stats, 1, 1)
                bk(reset, 1, 2)
                fr(l2_sup_lo, 0)
                bk(rh_lo, 1, 2)
                bk(diff, 0, 2)
                bk(gated, 0, 2)
                fr(l2_residual, 0)
                bk(h_new, 0, 2)
                fr(stats, 0, 2)
                fr(xT_lo, 1, 2)
                bk(residual3, 0)
                bk(diff, 1, 2)
                bk(stats3, 0)
                bk(gated, 1, 2)
                bk(h_new, 1, 2)
                fr(l2_sup_lo, 1)
                bk(residual3, 1)
                bk(stats3, 1)
                fr(l2_residual, 1)
                fr(stats, 1, 2)

            merged(True, 0, False, None)
            merged(True, 1, True, 0)
            with dve.Fori(1, G - 1) as i:
                merged(True, i + 1, True, i)
            merged(False, None, True, G - 1)

        @block.gpsimd
        def _(pool):
            pool.memset(ident[:, :], 0.0).then_inc(c["ident_zero"], 1)
            pool.memset(ones[:, :], 1.0).then_inc(c["const_ready"], 1)
            pool.memset(minus_half[:, :], -0.5).then_inc(c["const_ready"], 1)
            pool.memset(eps[:, :], EPS).then_inc(c["const_ready"], 1)
            pool.wait_ge(c["ident_zero"], 1)
            pool.affine_select(out=ident[:, :], in_=ident[:, :], compare_op=ALU.not_equal, fill=1.0, base=0,
                               pattern=[[-1, P]], channel_multiplier=1).then_inc(c["ident_ready"], 1)
            pool.wait_ge(c["const_ready"], 3)
            pool.wait_ge(c["deg_step"], 2)
            pool.tensor_tensor(deg[:, 3 * NT:4 * NT], deg[:, NT:2 * NT], minus_half[:, 0:NT],
                               ALU.pow).then_inc(c["deg_pow"], 1)
            pool.wait_ge(c["setup_done"], 1)

            def deviation(means, small, n, mean_ready, ready):
                pool.wait_ge(mean_ready, 3 * n + 3)
                pool.tensor_tensor(small[:, 0, :], means[:, :, 1], eps[:, :], ALU.add).then_inc(ready, 1)
                pool.wait_ge(ready, 3 * n + 1)
                pool.tensor_tensor(small[:, 1, :], small[:, 0, :], minus_half[:, :], ALU.pow).then_inc(ready, 1)
                pool.wait_ge(ready, 3 * n + 2)
                pool.tensor_tensor(small[:, 3, :], small[:, 2, :], small[:, 1, :], ALU.mult).then_inc(ready, 1)

            def rstd_of(g, b, layer):
                deviation(mv[b], ln[b], 3 * g + layer, f[b]["mean_ready"], f[b]["rstd_ready"])

            def rstd3_of(g, b):
                deviation(mv3[b], ln3[b], g, f[b]["mean3"], f[b]["rstd3_ready"])

            def rnorm(g, b):
                s = f[b]
                pool.wait_ge(s["norm_copied"], g + 1)
                pool.tensor_tensor(rn[b][:, NT:2 * NT], rn[b][:, 0:NT], minus_half[:, 0:NT],
                                   ALU.pow).then_inc(s["rn_ready"], 1)

            def add_bias2(g, b):
                s = f[b]
                pool.wait_ge(s["x2_ready"], 2 * g + 2)
                pool.tensor_tensor(flat(XB[b]), flat(X2[b]), bias2_r[:, :], ALU.add).then_inc(s["xb_ready"], 1)

            def merged(front, gf, back, gb):
                def fr(step, *which):
                    if front:
                        step(gf, *which)

                def bk(step, *which):
                    if back:
                        step(gb, *which)

                fr(rstd_of, 0, 0)
                fr(rstd_of, 1, 0)
                fr(rnorm, 0)
                fr(rstd_of, 0, 1)
                fr(add_bias2, 0)
                fr(rnorm, 1)
                fr(rstd_of, 1, 1)
                fr(add_bias2, 1)
                fr(rstd_of, 0, 2)
                bk(rstd3_of, 0)
                bk(rstd3_of, 1)
                fr(rstd_of, 1, 2)

            merged(True, 0, False, None)
            merged(True, 1, True, 0)
            with pool.Fori(1, G - 1) as i:
                merged(True, i + 1, True, i)
            merged(False, None, True, G - 1)


_INS = ['x', 'adj', 'L0_gnn_W', 'L0_gnn_a', 'L0_gnn_beta', 'L1_gnn_Wq', 'L1_gnn_Wk', 'L1_gnn_Wv', 'L2_gnn_weight',
        'L2_gnn_bias', 'L3_gnn_w3_w', 'L3_gnn_w3_b', 'L3_gnn_u3_w', 'L3_gnn_u3_b', 'L3_gnn_w4_w', 'L3_gnn_w4_b',
        'L3_gnn_w5_w', 'L3_gnn_w5_b', 'L3_gnn_u5_w', 'L3_gnn_u5_b']
_OUTS = [((B, N, D), 'float32')]


def kernel(**inputs):
    import numpy as _np
    import concourse.bacc as _bacc
    from concourse import mybir as _mybir
    from concourse.bass_utils import run_bass_kernel_spmd as _run

    nc = _bacc.Bacc("TRN2", target_bir_lowering=False, num_devices=1)
    arrays, args = {}, []
    for name in _INS:
        a = _np.ascontiguousarray(inputs[name])
        arrays[f"in_{name}_dram"] = a
        args.append(nc.dram_tensor(f"in_{name}_dram", a.shape, _mybir.dt.from_np(a.dtype), kind="ExternalInput").ap())
    for i, (shape, dtype) in enumerate(_OUTS):
        dt = _mybir.dt.from_np(_np.dtype(dtype))
        args.append(nc.dram_tensor(f"out_{i}_dram", shape, dt, kind="ExternalOutput").ap())
    four_layer_gnn_kernel(nc, *args)
    r = _run(nc, [arrays], core_ids=[0])
    return r.results[0]["out_0_dram"]
```

```python
from contextlib import ExitStack

import concourse.bass as bass
from concourse import mybir

P = 128
ALU = mybir.AluOpType
ACT = mybir.ActivationFunctionType
F32 = mybir.dt.float32
F32R = mybir.dt.float32r

B, N, D = 32, 256, 256
BG = 2
G = B // BG
T = 3
NT, DT = N // P, D // P
SLOPE = 0.2
EPS = 1e-5



def four_layer_gnn_kernel(
    nc: bass.Bass,
    x: bass.AP,
    adj: bass.AP,
    W0: bass.AP,
    a0: bass.AP,
    beta: bass.AP,
    Wq: bass.AP,
    Wk: bass.AP,
    Wv: bass.AP,
    W2: bass.AP,
    bias2: bass.AP,
    w3_w: bass.AP,
    w3_b: bass.AP,
    u3_w: bass.AP,
    u3_b: bass.AP,
    w4_w: bass.AP,
    w4_b: bass.AP,
    w5_w: bass.AP,
    w5_b: bass.AP,
    u5_w: bass.AP,
    u5_b: bass.AP,
    out: bass.AP,
):
    ctx = ExitStack()
    with ctx:
        def sb(name, shape, dt=F32):
            return ctx.enter_context(nc.sbuf_tensor(name, shape, dt))

        def split(name, shape):
            return sb(name + "_hi", shape, F32R), sb(name + "_lo", shape, F32R)

        def both(name, shape, dt=F32):
            return [sb(f"{name}{b}", shape, dt) for b in range(BG)]

        def both_split(name, shape):
            return [split(f"{name}{b}", shape) for b in range(BG)]

        def sem(name):
            return ctx.enter_context(nc.semaphore(name))

        def sems(*names):
            return {n: sem(n) for n in names}

        def sems_b(*names):
            return [{n: sem(f"{n}{b}") for n in names} for b in range(BG)]

        def banks(name):
            return [ctx.enter_context(nc.psum_tensor(f"{name}{b}", [P, 512], F32)) for b in range(BG)]

        pF, pA, pR, pH = banks("front"), banks("aggregate"), banks("gates"), banks("candidate")

        ident = sb("ident", [P, P])
        minus_half = sb("minus_half", [P, NT])
        eps = sb("eps", [P, NT])
        scratch = sb("scratch", [P, 1])
        flags = sb("flags", [P, 1])
        flag = sb("flag", [1, 1])
        adjN = sb("adjN", [P, NT, N])
        adjT = split("adjT", [P, NT, N])
        dinv = sb("dinv", [P, NT])
        deg = sb("deg", [P, 4 * NT])
        w0 = split("w0", [P, DT, D])
        wa = sb("wa", [P, 2, D])
        beta_ident = sb("beta_ident", [P, NT, P])
        gqk = split("gqk", [P, DT, D])
        wv = split("wv", [P, DT, D])
        w2 = split("w2", [P, DT, D])
        u3 = split("u3", [P, DT, D])
        w4 = split("w4", [P, DT, D])
        w34 = split("w34", [P, DT, D])
        w5 = split("w5", [P, DT, D])
        u5 = split("u5", [P, DT, D])
        beta_c = sb("beta_c", [P, 1])
        bias2_r = sb("bias2_r", [P, NT * D])
        braw = sb("braw", [P, 5, DT])
        bz = sb("bz", [P, DT])
        br = sb("br", [P, DT])
        bh = sb("bh", [P, DT])
        arow = sb("arow", [P, 2, D])
        wsum = sb("wsum", [P, DT, 2])

        X0 = both("X0", [P, NT, D])
        X1 = both("X1", [P, NT, D])
        X2 = both("X2", [P, NT, D])
        xT = both_split("xT", [P, DT, N])
        W02 = both("W02", [P, NT, N])
        E = both("E", [P, NT, N])
        E2 = both("E2", [P, NT, N])
        s12 = both("s12", [P, NT, 2])
        s1x = both("s1x", [P, NT])
        products = both("products", [P, NT, 2, D])
        nmx = both("nmx", [P, 2 * NT])
        rs = both("rs", [P, 2 * NT])
        hs = both_split("hs", [P, NT, D])
        HB = both("HB", [P, NT, D])
        pt = both_split("pt", [P, NT, N])
        V = both("V", [P, NT, D])
        Y = both("Y", [P, NT, D])
        yT = both_split("yT", [P, DT, N])
        rn = both("rn", [P, 2 * NT])
        st, st3 = both("st", [P, NT, 6]), both("st3", [P, NT, 6])
        mv, mv3 = both("mv", [P, NT, 2]), both("mv3", [P, NT, 2])
        ln, ln3 = both("ln", [P, 4, NT]), both("ln3", [P, 4, NT])
        R, SQ = E, E2
        XB = HB

        X3 = both("X3", [P, NT, D])
        XR = both("XR", [P, NT, D])
        hN = both_split("hN", [P, NT, D])
        hT = both("hT", [P, DT, N])
        hTs = both_split("hTs", [P, DT, N])
        aT = both_split("aT", [P, DT, N])
        tr2 = sb("tr", [P, BG, DT, N])
        tz2 = sb("tz", [P, BG, DT, N])
        rh2 = sb("rh", [P, BG, DT, N])
        tr, tz, rh = [[t[:, b, :, :] for b in range(BG)] for t in (tr2, tz2, rh2)]
        rhs = both_split("rhs", [P, DT, N])
        hv = both("hv", [P, DT, N])
        YO = both("YO", [P, NT, D])

        w3_s, w4_s, w5_s = [t[:, :, :, :].rearrange("p b t n -> p (b t n)").rearrange("p (k c) -> p k c", k=DT)
                            for t in (tr2, tz2, rh2)]
        w0_s, wq_s, wk_s, wv_s, w2_s, u3_s, u5_s = [
            t[:, :, :] for t in (hv[0], hv[1], YO[0], YO[1], XR[0], XR[1], X3[0])]
        w4_sum, w34_sum, w5_sum = hT[0][:, :, :], hT[1][:, :, :], X3[1][:, :, :]

        c = sems("loaded_first", "loaded_second", "loaded_third", "ident_zero", "ident_ready", "const_ready",
                 "matrix_in_psum", "matrix_hi", "matrix_lo", "w_sum", "w_sums", "wa_sum", "wa_turned", "wa_ready",
                 "beta_ready", "direct_hi", "direct_lo", "deg_step", "deg_pow", "dinv_ready", "bias_step", "bias_ready",
                 "lo_flags", "flags_turned", "adj_flag")
        f = sems_b("x_loaded", "front_psum", "part_hi", "part_lo",
                   "x0_hi", "x0_lo", "s_ready", "w02_ready", "lrelu_ready", "masked_ready", "max_ready", "exp_ready",
                   "rinv_ready",
                   "scaled_ready", "p_ready", "neg_ready", "elu_exp", "elu_ready", "y_ready",
                   "stats_ready", "mean_ready", "rstd_ready", "x1_ready", "x2_ready", "x3_ready",
                   "rel_masked", "rel_hi", "rel_lo", "vv_hi", "vv_lo", "norm_ready", "rn_ready", "xb_ready",
                   "x3T_psum", "hT_copied", "xr_copied", "hT_hi", "hT_lo", "hN_psum", "hN_hi", "hN_lo",
                   "a_psum", "a_hi", "a_lo", "r_psum", "r_ready", "rh_ready", "rh_hi", "rh_lo",
                   "z_psum", "z_ready", "hv_psum", "hv_ready", "diff_ready", "gated_ready", "h_new",
                   "yo_ready", "stats3", "mean3", "rstd3_ready", "normed3", "stored")

        BANK = ["s2", "p", "u0", "out0", "xT1", "yT", "rel", "v", "relT", "out1", "u2", "out2"]
        PARTS = ["p", "u0", "xT1", "yT", "first half of x2", "x2", "u2"]

        def in_bank(g, what):
            return len(BANK) * g + BANK.index(what) + 1

        def parted(g, what):
            return len(PARTS) * g + PARTS.index(what) + 1

        MATRICES = ["adjT", "gqk", "wv", "u3", "w4", "w34", "w5", "u5"]
        matrix = dict(zip(MATRICES, (adjT, gqk, wv, u3, w4, w34, w5, u5)))
        matrix_bank = dict(zip(MATRICES, (pA[0], pR[0], pR[1], pH[0], pH[1], pA[0], pA[1], pR[0])))

        def made(name):
            return MATRICES.index(name) + 1

        def flat(t):
            return t[:, :, :].rearrange("p a b -> p (a b)")

        def f32(t):
            return t.bitcast(F32)

        x_rows = x.rearrange("b (t p) d -> b p t d", p=P)
        out_rows = out.rearrange("b (t p) d -> b p t d", p=P)
        FIRST, SECOND, THIRD = 5, 3, 13

        def once(eng, semaphore, uses):
            if not isinstance(uses, int) or uses > 0:
                eng.wait_ge(semaphore, uses)

        def first(eng, g, semaphore, value):
            if isinstance(g, int) and g == 0:
                eng.wait_ge(semaphore, value)

        block = ctx.enter_context(nc.Block())

        @block.sync
        def _(sp):
            def rows(w):
                return w.rearrange("(t p) d -> p t d", p=P)

            def load(pairs, count, loaded):
                assert len(pairs) == count
                for dst, src in pairs:
                    sp.dma_start(dst, src, allow_slow_non_contiguous=True).then_inc(loaded, 16)

            def load_first():
                load([(w0_s, rows(W0)),
                      (arow[:, 0, :], a0[0:D, :].rearrange("f o -> o f").broadcast_to([P, D])),
                      (arow[:, 1, :], a0[D:2 * D, :].rearrange("f o -> o f").broadcast_to([P, D])),
                      (adjN[:, :, :], rows(adj)),
                      (beta_c[:, :], beta.rearrange("(a o) -> a o", a=1).broadcast_to([P, 1]))],
                     FIRST, c["loaded_first"])

            def load_second():
                load([(wq_s, rows(Wq)), (wk_s, rows(Wk)), (wv_s, rows(Wv))], SECOND, c["loaded_second"])

            def load_third():
                load([(w2_s, rows(W2)), (u3_s, rows(u3_w)), (w4_s, rows(w4_w)), (w3_s, rows(w3_w)), (w5_s, rows(w5_w)),
                      (u5_s, rows(u5_w)),
                      (bias2_r[:, 0:D], bias2.rearrange("(a o) -> a o", a=1).broadcast_to([P, D])),
                      (bias2_r[:, D:2 * D], bias2.rearrange("(a o) -> a o", a=1).broadcast_to([P, D]))]
                     + [(braw[:, k, :], bvec.rearrange("(t p) -> p t", p=P))
                        for k, bvec in enumerate((w3_b, u3_b, w4_b, w5_b, u5_b))],
                     THIRD, c["loaded_third"])

            def row(dram, g, b):
                if isinstance(g, int):
                    return dram[g * BG + b]
                return dram[bass.ds(g * BG + b, 1)].rearrange("o p t d -> p (o t) d")

            def load_x(g, b):
                once(sp, f[b]["y_ready"], 3 * g - 2)
                sp.dma_start(X0[b][:, :, :], row(x_rows, g, b)).then_inc(f[b]["x_loaded"], 16)

            def keep_x3(g, b):
                sp.wait_ge(f[b]["x3_ready"], 2 * g + 2)
                once(sp, f[b]["yo_ready"], g)
                sp.dma_start(XR[b][:, :, :], X3[b][:, :, :]).then_inc(f[b]["xr_copied"], 16)

            def store(g, b):
                sp.wait_ge(f[b]["normed3"], 2 * g + 2)
                sp.dma_start(row(out_rows, g, b), YO[b][:, :, :]).then_inc(f[b]["stored"], 16)

            def first_turns():
                load_first(); load_x(0, 0); load_x(0, 1); load_third(); load_second(); load_x(1, 0)
                load_x(1, 1); keep_x3(0, 0); keep_x3(0, 1); load_x(2, 0); load_x(2, 1); keep_x3(1, 0)
                load_x(3, 0); store(0, 0); keep_x3(1, 1); store(0, 1); load_x(3, 1)

            def merged(turn, *lags):
                def at(lag, step, *which):
                    if lag in lags:
                        step(turn - lag, *which)

                at(1, keep_x3, 0)
                at(-1, load_x, 0)
                at(2, store, 0)
                at(1, keep_x3, 1)
                at(2, store, 1)
                at(-1, load_x, 1)

            def last_turns():
                keep_x3(G - 1, 0); store(G - 2, 0); keep_x3(G - 1, 1); store(G - 2, 1); store(G - 1, 0)
                store(G - 1, 1)

            first_turns()
            with sp.Fori(3, G - 1) as i:
                merged(i, -1, 0, 1, 2)
            merged(G - 1, 0, 1, 2)
            last_turns()
            for b in range(BG):
                sp.wait_ge(f[b]["stored"], 16 * G)

        @block.tensor
        def _(pe):
            def passes(o, ls, rs_, start, stop):
                terms = []
                for (lh, ll), (rh_, rl) in zip(ls, rs_):
                    terms += [(l, r) for l, r in ((lh, rh_), (lh, rl), (ll, rh_)) if l is not None and r is not None]
                for j, (l, r) in enumerate(terms):
                    mm = pe.matmul(o, l, r, start=start and j == 0, stop=stop and j == len(terms) - 1,
                                   skip_group_check=True)
                return mm

            def cut(s, k, a, b):
                return s[0][:, k, a:b], None if s[1] is None else s[1][:, k, a:b]

            def product(bank, left, right, n_right, start=True, stop=True):
                for i in range(2):
                    mm = passes(bank[:, i * 256:i * 256 + n_right], [cut(left, k, i * P, i * P + P) for k in range(2)],
                                [cut(right, k, 0, n_right) for k in range(2)], start and i == 0, stop)
                return mm

            def transpose_tiles(dst, src, start=True):
                for i in range(2):
                    for k in range(2):
                        mm = pe.transpose(dst[:, i * 256 + k * P:i * 256 + k * P + P], src[:, k, i * P:i * P + P],
                                          ident[:, :])
                return mm

            sources = dict(adjT=adjN, wv=wv_s, u3=u3_s, w4=w4_sum, w34=w34_sum, w5=w5_sum, u5=u5_s)

            def turn_matrix(name):
                bank = matrix_bank[name]
                if name == "adjT":
                    pe.wait_ge(c["loaded_first"], 16 * FIRST)
                    pe.wait_ge(c["ident_ready"], 1)
                elif name == "gqk":
                    pe.wait_ge(c["loaded_second"], 16 * SECOND)
                elif name == "u3":
                    pe.wait_ge(c["loaded_third"], 16 * THIRD)
                elif name in ("w4", "w34", "w5"):
                    pe.wait_ge(c["w_sums"], {"w4": 1, "w34": 2, "w5": 3}[name])
                if name == "w34":
                    pe.wait_ge(c["matrix_lo"], made("adjT"))
                elif name == "w5":
                    pe.wait_ge(c["wa_ready"], 1)
                elif name == "u5":
                    pe.wait_ge(c["matrix_lo"], made("gqk"))
                if name != "gqk":
                    transpose_tiles(bank, sources[name]).then_inc(c["matrix_in_psum"], 1)
                    return
                for i in range(2):
                    for k in range(2):
                        mm = pe.matmul(bank[:, i * 256:i * 256 + 256], wq_s[:, k, i * P:i * P + P], wk_s[:, k, :],
                                       start=(k == 0), stop=(k == 1))
                mm.then_inc(c["matrix_in_psum"], 1)

            def turn_wa():
                pe.wait_ge(c["wa_sum"], 4)
                for j in range(2):
                    for k in range(DT):
                        mm = pe.transpose(pA[1][:, j * D + k * P:j * D + k * P + P],
                                          wsum[:, k, j:j + 1].broadcast_to([P, P]), ident[:, :])
                mm.then_inc(c["wa_turned"], 1)

            def turn_flags():
                pe.wait_ge(c["lo_flags"], 2)
                pe.transpose(pH[0][0:1, 0:P], flags[:, :], ident[:, :]).then_inc(c["flags_turned"], 1)

            def l0_s2_rows(g, b):
                s = f[b]
                pe.wait_ge(s["s_ready"], 5 * g + 5)
                once(pe, s["y_ready"], 3 * g)
                for k in range(NT):
                    mm = pe.transpose(pF[b][:, k * P:k * P + P], s12[b][:, k, 1:2].broadcast_to([P, P]), ident[:, :])
                mm.then_inc(s["front_psum"], 1)

            def l0_turn(g, b):
                s = f[b]
                pe.wait_ge(s["p_ready"], g + 1)
                transpose_tiles(pF[b], W02[b]).then_inc(s["front_psum"], 1)

            def l0_attend(g, b):
                s = f[b]
                pe.wait_ge(s["x0_hi"], g + 1)
                pe.wait_ge(s["x0_lo"], g + 1)
                pe.wait_ge(s["part_hi"], parted(g, "p"))
                pe.wait_ge(s["part_lo"], parted(g, "p"))
                product(pF[b], hs[b], pt[b], N).then_inc(s["front_psum"], 1)

            def l0_project(g, b):
                s = f[b]
                first(pe, g, c["direct_lo"], 1)
                pe.wait_ge(s["part_hi"], parted(g, "u0"))
                pe.wait_ge(s["part_lo"], parted(g, "u0"))
                product(pF[b], yT[b], w0, D).then_inc(s["front_psum"], 1)

            def x1_to_T(g, b):
                s = f[b]
                pe.wait_ge(s["x1_ready"], 2 * g + 2)
                transpose_tiles(pF[b], X1[b]).then_inc(s["front_psum"], 1)

            def l1_y(g, b):
                s = f[b]
                first(pe, g, c["matrix_lo"], made("gqk"))
                pe.wait_ge(s["part_hi"], parted(g, "xT1"))
                pe.wait_ge(s["part_lo"], parted(g, "xT1"))
                product(pF[b], gqk, xT[b], N).then_inc(s["front_psum"], 1)

            def l1_rel(g, b):
                s = f[b]
                pe.wait_ge(s["part_hi"], parted(g, "yT"))
                pe.wait_ge(s["part_lo"], parted(g, "yT"))
                product(pF[b], xT[b], yT[b], N).then_inc(s["front_psum"], 1)

            def l1_v(g, b):
                s = f[b]
                first(pe, g, c["matrix_lo"], made("wv"))
                pe.wait_ge(s["rel_masked"], g + 1)
                product(pF[b], xT[b], wv, D).then_inc(s["front_psum"], 1)

            def l1_turn_rel(g, b):
                s = f[b]
                pe.wait_ge(s["vv_hi"], g + 1)
                pe.wait_ge(s["vv_lo"], g + 1)
                pe.wait_ge(s["rel_masked"], g + 1)
                transpose_tiles(pF[b], R[b]).then_inc(s["front_psum"], 1)

            def l1_out(g, b):
                s = f[b]
                pe.wait_ge(s["norm_ready"], 2 * g + 2)
                pe.wait_ge(s["rel_hi"], g + 1)
                pe.wait_ge(s["rel_lo"], g + 1)
                product(pF[b], pt[b], hs[b], D).then_inc(s["front_psum"], 1)

            def l2_aggregate(g, b, adj):
                s = f[b]
                pe.wait_ge(s["part_hi"], parted(g, "x2"))
                pe.wait_ge(s["part_lo"], parted(g, "x2"))
                product(pF[b], hs[b], adj, N).then_inc(s["front_psum"], 1)

            def l2_out(g, b):
                s = f[b]
                first(pe, g, c["direct_lo"], 2)
                pe.wait_ge(s["part_hi"], parted(g, "u2"))
                pe.wait_ge(s["part_lo"], parted(g, "u2"))
                product(pF[b], yT[b], w2, D).then_inc(s["front_psum"], 1)

            def x3_to_T(g, b):
                s = f[b]
                first(pe, g, c["matrix_lo"], made("u5"))
                pe.wait_ge(s["x3_ready"], 2 * g + 2)
                once(pe, s["yo_ready"], g)
                transpose_tiles(pA[b], X3[b]).then_inc(s["x3T_psum"], 1)

            def aggregate(g, b, t, adj):
                s = f[b]
                pe.wait_ge(s["hN_hi"], 3 * g + t + 1)
                pe.wait_ge(s["hN_lo"], 3 * g + t + 1)
                pe.wait_ge(s["hT_copied"], g + 1)
                product(pA[b], hN[b], adj, N).then_inc(s["a_psum"], 1)

            def gate_u3(g, b, t):
                s = f[b]
                pe.wait_ge(s["hT_hi"], 3 * g + t + 1)
                pe.wait_ge(s["hT_lo"], 3 * g + t + 1)
                once(pe, s["z_ready"], 2 * (3 * g + t))
                product(pR[b], u3, hTs[b], N, True, False)

            def gate_r(g, b, t):
                s = f[b]
                pe.wait_ge(s["a_hi"], 3 * g + t + 1)
                pe.wait_ge(s["a_lo"], 3 * g + t + 1)
                product(pR[b], w4, aT[b], N, False, True).then_inc(s["r_psum"], 1)

            def candidate_a(g, b, t):
                s = f[b]
                pe.wait_ge(s["a_hi"], 3 * g + t + 1)
                pe.wait_ge(s["a_lo"], 3 * g + t + 1)
                once(pe, s["hv_ready"], 2 * (3 * g + t))
                product(pH[b], w5, aT[b], N, True, False)

            def gate_z(g, b, t):
                s = f[b]
                pe.wait_ge(s["r_ready"], 2 * (3 * g + t + 1))
                product(pR[b], w34, aT[b], N, False, True).then_inc(s["z_psum"], 1)

            def candidate_rh(g, b, t):
                s = f[b]
                pe.wait_ge(s["rh_hi"], 3 * g + t + 1)
                pe.wait_ge(s["rh_lo"], 3 * g + t + 1)
                product(pH[b], u5, rhs[b], N, False, True).then_inc(s["hv_psum"], 1)

            def h_to_N(g, b, t):
                s = f[b]
                pe.wait_ge(s["h_new"], 3 * g + t + 1)
                transpose_tiles(pA[b], hT[b]).then_inc(s["hN_psum"], 1)

            def turns(adj):
                def first_turns():
                    l0_s2_rows(0, 0); l0_s2_rows(0, 1); turn_matrix("gqk"); turn_matrix("wv"); turn_matrix("u3")
                    turn_matrix("w4"); l0_turn(0, 0); turn_matrix("w34"); l0_turn(0, 1); turn_matrix("w5")
                    l0_attend(0, 0); l0_attend(0, 1); turn_matrix("u5"); l0_project(0, 0); l0_project(0, 1)
                    x1_to_T(0, 0); x1_to_T(0, 1); l1_y(0, 0); l1_y(0, 1); l1_rel(0, 0); l1_rel(0, 1); l1_v(0, 0)
                    l1_v(0, 1); l1_turn_rel(0, 0); l1_turn_rel(0, 1); l1_out(0, 0); l1_out(0, 1)
                    l2_aggregate(0, 0, adj); l2_aggregate(0, 1, adj); l2_out(0, 0); l2_out(0, 1); l0_s2_rows(1, 0)
                    l0_s2_rows(1, 1); x3_to_T(0, 0); aggregate(0, 0, 0, adj); x3_to_T(0, 1); gate_u3(0, 0, 0)
                    l0_turn(1, 0); candidate_a(0, 0, 0); gate_r(0, 0, 0); l0_attend(1, 0); l0_turn(1, 1)
                    gate_z(0, 0, 0); l0_project(1, 0); l0_attend(1, 1); candidate_rh(0, 0, 0)
                    aggregate(0, 1, 0, adj); gate_u3(0, 1, 0); l0_project(1, 1); candidate_a(0, 1, 0); x1_to_T(1, 0)
                    gate_r(0, 1, 0); h_to_N(0, 0, 0); gate_z(0, 1, 0); l1_y(1, 0); aggregate(0, 0, 1, adj)
                    gate_u3(0, 0, 1); candidate_rh(0, 1, 0); l1_rel(1, 0); x1_to_T(1, 1); gate_r(0, 0, 1)
                    l1_v(1, 0); gate_z(0, 0, 1); h_to_N(0, 1, 0); gate_u3(0, 1, 1); l1_turn_rel(1, 0)
                    candidate_a(0, 0, 1); l1_out(1, 0); aggregate(0, 1, 1, adj); candidate_rh(0, 0, 1); l1_y(1, 1)
                    candidate_a(0, 1, 1); gate_r(0, 1, 1); h_to_N(0, 0, 1); l1_rel(1, 1); l2_aggregate(1, 0, adj)
                    gate_z(0, 1, 1); aggregate(0, 0, 2, adj); l2_out(1, 0); l1_v(1, 1); l0_s2_rows(2, 0)
                    gate_u3(0, 0, 2); candidate_rh(0, 1, 1); gate_r(0, 0, 2); l1_turn_rel(1, 1)
                    candidate_a(0, 0, 2); gate_z(0, 0, 2); l0_turn(2, 0); h_to_N(0, 1, 1); l1_out(1, 1)
                    candidate_rh(0, 0, 2); l0_attend(2, 0); gate_u3(0, 1, 2); aggregate(0, 1, 2, adj)
                    l0_project(2, 0); h_to_N(0, 0, 2); gate_r(0, 1, 2); l2_aggregate(1, 1, adj); x3_to_T(1, 0)
                    candidate_a(0, 1, 2); gate_z(0, 1, 2); l2_out(1, 1); aggregate(1, 0, 0, adj)
                    candidate_rh(0, 1, 2); l0_s2_rows(2, 1); gate_u3(1, 0, 0); x1_to_T(2, 0); gate_r(1, 0, 0)
                    candidate_a(1, 0, 0); gate_z(1, 0, 0); l1_y(2, 0); candidate_rh(1, 0, 0); h_to_N(0, 1, 2)
                    l0_turn(2, 1); l1_rel(2, 0); x3_to_T(1, 1); l0_attend(2, 1); l1_v(2, 0); aggregate(1, 1, 0, adj)
                    h_to_N(1, 0, 0); gate_u3(1, 1, 0); l0_project(2, 1); l1_turn_rel(2, 0); candidate_a(1, 1, 0)
                    gate_r(1, 1, 0); l1_out(2, 0); gate_z(1, 1, 0); aggregate(1, 0, 1, adj); candidate_rh(1, 1, 0)
                    x1_to_T(2, 1); gate_u3(1, 0, 1); candidate_a(1, 0, 1); gate_r(1, 0, 1); h_to_N(1, 1, 0)
                    l2_aggregate(2, 0, adj); gate_z(1, 0, 1); aggregate(1, 1, 1, adj); l2_out(2, 0)
                    candidate_rh(1, 0, 1); l1_y(2, 1); gate_u3(1, 1, 1)

                def merged(turn, *lags):
                    def at(lag, step, *which):
                        if lag in lags:
                            step(turn - lag, *which)

                    at(2, candidate_a, 1, 1)
                    at(1, l1_rel, 1)
                    at(2, h_to_N, 0, 1)
                    at(2, gate_r, 1, 1)
                    at(1, l1_v, 1)
                    at(2, gate_z, 1, 1)
                    at(0, l0_s2_rows, 0)
                    at(2, aggregate, 0, 2, adj)
                    at(2, gate_u3, 0, 2)
                    at(2, candidate_rh, 1, 1)
                    at(2, gate_r, 0, 2)
                    at(1, l1_turn_rel, 1)
                    at(2, candidate_a, 0, 2)
                    at(2, gate_z, 0, 2)
                    at(2, h_to_N, 1, 1)
                    at(0, l0_turn, 0)
                    at(1, l1_out, 1)
                    at(2, candidate_rh, 0, 2)
                    at(0, l0_attend, 0)
                    at(2, gate_u3, 1, 2)
                    at(2, aggregate, 1, 2, adj)
                    at(0, l0_project, 0)
                    at(2, h_to_N, 0, 2)
                    at(2, gate_r, 1, 2)
                    at(1, l2_aggregate, 1, adj)
                    at(1, x3_to_T, 0)
                    at(2, candidate_a, 1, 2)
                    at(2, gate_z, 1, 2)
                    at(1, l2_out, 1)
                    at(1, aggregate, 0, 0, adj)
                    at(2, candidate_rh, 1, 2)
                    at(0, l0_s2_rows, 1)
                    at(1, gate_u3, 0, 0)
                    at(0, x1_to_T, 0)
                    at(1, gate_r, 0, 0)
                    at(1, candidate_a, 0, 0)
                    at(1, gate_z, 0, 0)
                    at(0, l1_y, 0)
                    at(2, h_to_N, 1, 2)
                    at(0, l0_turn, 1)
                    at(1, candidate_rh, 0, 0)
                    at(0, l1_rel, 0)
                    at(1, x3_to_T, 1)
                    at(0, l0_attend, 1)
                    at(0, l1_v, 0)
                    at(1, h_to_N, 0, 0)
                    at(1, aggregate, 1, 0, adj)
                    at(1, gate_u3, 1, 0)
                    at(0, l0_project, 1)
                    at(0, l1_turn_rel, 0)
                    at(1, candidate_a, 1, 0)
                    at(1, gate_r, 1, 0)
                    at(0, l1_out, 0)
                    at(1, gate_z, 1, 0)
                    at(1, aggregate, 0, 1, adj)
                    at(1, candidate_rh, 1, 0)
                    at(0, x1_to_T, 1)
                    at(1, gate_u3, 0, 1)
                    at(1, candidate_a, 0, 1)
                    at(1, gate_r, 0, 1)
                    at(1, h_to_N, 1, 0)
                    at(0, l2_aggregate, 0, adj)
                    at(0, l1_y, 1)
                    at(1, aggregate, 1, 1, adj)
                    at(0, l2_out, 0)
                    at(1, candidate_rh, 0, 1)
                    at(1, gate_z, 0, 1)
                    at(1, gate_u3, 1, 1)

                def last_turns():
                    candidate_a(G - 2, 1, 1); gate_r(G - 2, 1, 1); l1_rel(G - 1, 1); h_to_N(G - 2, 0, 1)
                    gate_z(G - 2, 1, 1); l1_v(G - 1, 1); candidate_rh(G - 2, 1, 1); aggregate(G - 2, 0, 2, adj)
                    l1_turn_rel(G - 1, 1); gate_u3(G - 2, 0, 2); l1_out(G - 1, 1); h_to_N(G - 2, 1, 1)
                    gate_r(G - 2, 0, 2); candidate_a(G - 2, 0, 2); aggregate(G - 2, 1, 2, adj); gate_u3(G - 2, 1, 2)
                    gate_z(G - 2, 0, 2); candidate_rh(G - 2, 0, 2); candidate_a(G - 2, 1, 2); gate_r(G - 2, 1, 2)
                    l2_aggregate(G - 1, 1, adj); h_to_N(G - 2, 0, 2); gate_z(G - 2, 1, 2); x3_to_T(G - 1, 0)
                    l2_out(G - 1, 1); candidate_rh(G - 2, 1, 2); aggregate(G - 1, 0, 0, adj); gate_u3(G - 1, 0, 0)
                    gate_r(G - 1, 0, 0); candidate_a(G - 1, 0, 0); h_to_N(G - 2, 1, 2); gate_z(G - 1, 0, 0)
                    x3_to_T(G - 1, 1); candidate_rh(G - 1, 0, 0); aggregate(G - 1, 1, 0, adj); gate_u3(G - 1, 1, 0)
                    h_to_N(G - 1, 0, 0); gate_r(G - 1, 1, 0); candidate_a(G - 1, 1, 0); gate_z(G - 1, 1, 0)
                    aggregate(G - 1, 0, 1, adj); gate_u3(G - 1, 0, 1); candidate_rh(G - 1, 1, 0)
                    gate_r(G - 1, 0, 1); candidate_a(G - 1, 0, 1); gate_z(G - 1, 0, 1); h_to_N(G - 1, 1, 0)
                    candidate_rh(G - 1, 0, 1); gate_u3(G - 1, 1, 1); aggregate(G - 1, 1, 1, adj)
                    h_to_N(G - 1, 0, 1); candidate_a(G - 1, 1, 1); gate_r(G - 1, 1, 1); gate_u3(G - 1, 0, 2)
                    aggregate(G - 1, 0, 2, adj); gate_z(G - 1, 1, 1); candidate_rh(G - 1, 1, 1)
                    candidate_a(G - 1, 0, 2); gate_r(G - 1, 0, 2); h_to_N(G - 1, 1, 1); gate_z(G - 1, 0, 2)
                    gate_u3(G - 1, 1, 2); aggregate(G - 1, 1, 2, adj); candidate_rh(G - 1, 0, 2)
                    gate_r(G - 1, 1, 2); candidate_a(G - 1, 1, 2); gate_z(G - 1, 1, 2); h_to_N(G - 1, 0, 2)
                    candidate_rh(G - 1, 1, 2); h_to_N(G - 1, 1, 2)

                first_turns()
                with pe.Fori(3, G) as i:
                    merged(i, 0, 1, 2)
                last_turns()

            turn_matrix("adjT")
            turn_wa()
            turn_flags()
            pe.wait_ge(c["adj_flag"], 1)
            adj_has_lo = pe.value_load(flag[0:1, 0:1].bitcast(mybir.dt.int32))
            with pe.If(adj_has_lo == 0):
                turns((adjT[0], None))
            with pe.Else():
                turns(adjT)

        @block.scalar
        def _(act):
            def copy(o, i):
                return act.activation(o, i, ACT.Copy)

            def matrix_hi(name):
                act.wait_ge(c["matrix_in_psum"], made(name))
                act.activation(flat(matrix[name][0]), matrix_bank[name][:, :], ACT.Copy,
                               scale=0.5 if name == "u5" else 1.0).then_inc(c["matrix_hi"], 1)

            def w0_hi():
                act.wait_ge(c["loaded_first"], 16 * FIRST)
                copy(w0[0][:, :, :], w0_s).then_inc(c["direct_hi"], 1)

            def w2_hi():
                act.wait_ge(c["loaded_third"], 16 * THIRD)
                copy(w2[0][:, :, :], w2_s).then_inc(c["direct_hi"], 1)

            def x0_hi(g, b):
                s = f[b]
                act.wait_ge(s["x_loaded"], 16 * g + 16)
                once(act, s["front_psum"], len(BANK) * g)
                copy(flat(hs[b][0]), flat(X0[b])).then_inc(s["x0_hi"], 1)

            def l0_w02(g, b):
                s = f[b]
                act.wait_ge(s["front_psum"], in_bank(g, "s2"))
                act.wait_ge(s["s_ready"], 5 * g + 5)
                for k in range(NT):
                    act.activation(W02[b][:, k, :], pF[b][:, 0:N], ACT.Identity,
                                   bias=s1x[b][:, k:k + 1], scale=SLOPE).then_inc(s["w02_ready"], 1)

            def l0_exp(g, b):
                s = f[b]
                act.wait_ge(s["max_ready"], g + 1)
                for k in range(NT):
                    act.activation(W02[b][:, k, :], E2[b][:, k, :], ACT.Exp, bias=nmx[b][:, NT + k:NT + k + 1],
                                   accum_out=rs[b][:, k:k + 1]).then_inc(s["exp_ready"], 1)

            def l0_scale(g, b):
                s = f[b]
                act.wait_ge(s["rinv_ready"], g + 1)
                for k in range(NT):
                    act.activation(W02[b][:, k, :], W02[b][:, k, :], ACT.Copy,
                                   scale=rs[b][:, NT + k:NT + k + 1]).then_inc(s["scaled_ready"], 1)

            def l0_p_hi(g, b):
                act.wait_ge(f[b]["front_psum"], in_bank(g, "p"))
                copy(flat(pt[b][0]), pF[b][:, :]).then_inc(f[b]["part_hi"], 1)

            def l0_u_hi(g, b):
                act.wait_ge(f[b]["front_psum"], in_bank(g, "u0"))
                copy(flat(yT[b][0]), pF[b][:, :]).then_inc(f[b]["part_hi"], 1)

            def l0_elu(g, b):
                s = f[b]
                act.wait_ge(s["front_psum"], in_bank(g, "out0"))
                act.activation(flat(HB[b]), pF[b][:, :], ACT.Relu, scale=-1.0).then_inc(s["neg_ready"], 1)
                act.wait_ge(s["neg_ready"], g + 1)
                act.activation(flat(E[b]), flat(HB[b]), ACT.Exp, scale=-1.0).then_inc(s["elu_exp"], 1)

            def x1T_hi(g, b):
                s = f[b]
                act.wait_ge(s["front_psum"], in_bank(g, "xT1"))
                copy(flat(xT[b][0]), pF[b][:, :]).then_inc(s["part_hi"], 1)

            def normalise(s, b, g, layer, o, ready):
                n = 3 * g + layer
                act.wait_ge(s["rstd_ready"], 3 * n + 3)
                for k in range(NT):
                    act.activation(o[:, k, :], Y[b][:, k, :], ACT.Identity, bias=ln[b][:, 3, k:k + 1],
                                   scale=ln[b][:, 1, k:k + 1]).then_inc(ready, 1)

            def norm0(g, b):
                normalise(f[b], b, g, 0, X1[b], f[b]["x1_ready"])

            def norm1(g, b):
                normalise(f[b], b, g, 1, X2[b], f[b]["x2_ready"])

            def norm2(g, b):
                first(act, g, c["matrix_in_psum"], made("u5"))
                once(act, f[b]["xr_copied"], 16 * g)
                once(act, f[b]["hN_lo"], 3 * g - 2)
                normalise(f[b], b, g, 2, X3[b], f[b]["x3_ready"])

            def norm3(g, b):
                s = f[b]
                act.wait_ge(s["rstd3_ready"], 3 * g + 3)
                for k in range(NT):
                    act.activation(YO[b][:, k, :], YO[b][:, k, :], ACT.Identity, bias=ln3[b][:, 3, k:k + 1],
                                   scale=ln3[b][:, 1, k:k + 1]).then_inc(s["normed3"], 1)

            def l1_y_hi(g, b):
                act.wait_ge(f[b]["front_psum"], in_bank(g, "yT"))
                copy(flat(yT[b][0]), pF[b][:, :]).then_inc(f[b]["part_hi"], 1)

            def l1_rel_hi(g, b):
                s = f[b]
                act.wait_ge(s["rel_masked"], g + 1)
                copy(flat(pt[b][0]), flat(R[b])).then_inc(s["rel_hi"], 1)

            def l1_norm(g, b):
                s = f[b]
                act.wait_ge(s["front_psum"], in_bank(g, "relT"))
                for i in range(NT):
                    act.activation(SQ[b][:, i, :], pF[b][:, i * N:i * N + N], ACT.Square,
                                   accum_out=rn[b][:, i:i + 1]).then_inc(s["norm_ready"], 1)

            def l1_v_hi(g, b):
                act.wait_ge(f[b]["front_psum"], in_bank(g, "v"))
                copy(flat(hs[b][0]), pF[b][:, :]).then_inc(f[b]["vv_hi"], 1)

            def l2_x_hi(g, b):
                first(act, g, c["dinv_ready"], 1)
                act.wait_ge(f[b]["x2_ready"], 2 * g + 2)
                for k in range(NT):
                    act.activation(hs[b][0][:, k, :], X2[b][:, k, :], ACT.Copy,
                                   scale=dinv[:, k:k + 1]).then_inc(f[b]["part_hi"], 1)

            def l2_u_hi(g, b):
                act.wait_ge(f[b]["front_psum"], in_bank(g, "u2"))
                copy(flat(yT[b][0]), pF[b][:, :]).then_inc(f[b]["part_hi"], 1)

            def take_x3(g, b):
                s = f[b]
                act.wait_ge(s["x3T_psum"], g + 1)
                copy(flat(hT[b]), pA[b][:, :]).then_inc(s["hT_copied"], 1)
                copy(flat(hN[b][0]), flat(X3[b])).then_inc(s["hN_hi"], 1)

            def take_x3_hi(g, b):
                s = f[b]
                act.wait_ge(s["hT_copied"], g + 1)
                copy(flat(hTs[b][0]), flat(hT[b])).then_inc(s["hT_hi"], 1)

            def a_hi(g, b, t):
                s = f[b]
                act.wait_ge(s["a_psum"], 3 * g + t + 1)
                copy(flat(aT[b][0]), pA[b][:, :]).then_inc(s["a_hi"], 1)

            def gate_r(g, b, t):
                s = f[b]
                first(act, g, c["bias_ready"], 3)
                act.wait_ge(s["r_psum"], 3 * g + t + 1)
                for i in range(DT):
                    act.activation(tr[b][:, i, :], pR[b][:, i * N:i * N + N], ACT.Tanh, bias=br[:, i:i + 1],
                                   scale=0.5).then_inc(s["r_ready"], 1)

            def rh_hi(g, b, t):
                act.wait_ge(f[b]["rh_ready"], 3 * g + t + 1)
                copy(flat(rhs[b][0]), flat(rh[b])).then_inc(f[b]["rh_hi"], 1)

            def gate_z(g, b, t):
                s = f[b]
                act.wait_ge(s["z_psum"], 3 * g + t + 1)
                for i in range(DT):
                    act.activation(tz[b][:, i, :], pR[b][:, i * N:i * N + N], ACT.Tanh, bias=bz[:, i:i + 1],
                                   scale=0.5).then_inc(s["z_ready"], 1)

            def cand(g, b, t):
                s = f[b]
                act.wait_ge(s["hv_psum"], 3 * g + t + 1)
                for i in range(DT):
                    act.activation(hv[b][:, i, :], pH[b][:, i * N:i * N + N], ACT.Tanh,
                                   bias=bh[:, i:i + 1]).then_inc(s["hv_ready"], 1)

            def hT_hi(g, b, t):
                act.wait_ge(f[b]["h_new"], 3 * g + t + 1)
                copy(flat(hTs[b][0]), flat(hT[b])).then_inc(f[b]["hT_hi"], 1)

            def hN_hi(g, b, t):
                act.wait_ge(f[b]["hN_psum"], 3 * g + t + 1)
                copy(flat(hN[b][0]), pA[b][:, :]).then_inc(f[b]["hN_hi"], 1)

            def first_turns():
                w0_hi(); x0_hi(0, 0); matrix_hi("adjT"); x0_hi(0, 1); l0_w02(0, 0); w2_hi(); l0_w02(0, 1)
                l0_exp(0, 0); matrix_hi("gqk"); l0_exp(0, 1); l0_scale(0, 0); l0_scale(0, 1); matrix_hi("wv")
                matrix_hi("u3"); l0_p_hi(0, 0); matrix_hi("w4"); matrix_hi("w34"); l0_p_hi(0, 1)
                matrix_hi("w5"); l0_u_hi(0, 0); l0_u_hi(0, 1); matrix_hi("u5"); l0_elu(0, 0); l0_elu(0, 1)
                norm0(0, 0); norm0(0, 1); x1T_hi(0, 0); x1T_hi(0, 1); l1_y_hi(0, 0); l1_y_hi(0, 1)
                l1_rel_hi(0, 0); l1_rel_hi(0, 1); l1_v_hi(0, 0); l1_v_hi(0, 1); l1_norm(0, 0); l1_norm(0, 1)
                norm1(0, 0); l2_x_hi(0, 0); norm1(0, 1); l2_x_hi(0, 1); l2_u_hi(0, 0); l2_u_hi(0, 1)
                x0_hi(1, 0); x0_hi(1, 1); l0_w02(1, 0); norm2(0, 0); l0_w02(1, 1); take_x3(0, 0); l0_exp(1, 0)
                norm2(0, 1); take_x3_hi(0, 0); l0_scale(1, 0); a_hi(0, 0, 0); take_x3(0, 1); l0_exp(1, 1)
                take_x3_hi(0, 1); l0_p_hi(1, 0); l0_scale(1, 1); gate_r(0, 0, 0); l0_u_hi(1, 0); l0_p_hi(1, 1)
                rh_hi(0, 0, 0); gate_z(0, 0, 0); l0_elu(1, 0); l0_u_hi(1, 1); cand(0, 0, 0); a_hi(0, 1, 0)
                norm0(1, 0); l0_elu(1, 1); x1T_hi(1, 0); hT_hi(0, 0, 0); gate_r(0, 1, 0); hN_hi(0, 0, 0)
                rh_hi(0, 1, 0); gate_z(0, 1, 0); l1_y_hi(1, 0); norm0(1, 1); a_hi(0, 0, 1); cand(0, 1, 0)
                x1T_hi(1, 1); l1_rel_hi(1, 0); gate_r(0, 0, 1); hT_hi(0, 1, 0); l1_v_hi(1, 0); rh_hi(0, 0, 1)
                gate_z(0, 0, 1); hN_hi(0, 1, 0); l1_norm(1, 0); a_hi(0, 1, 1); cand(0, 0, 1); l1_y_hi(1, 1)
                norm1(1, 0); l2_x_hi(1, 0); hT_hi(0, 0, 1); gate_r(0, 1, 1); hN_hi(0, 0, 1); rh_hi(0, 1, 1)
                l2_u_hi(1, 0); l1_rel_hi(1, 1); gate_z(0, 1, 1); a_hi(0, 0, 2); x0_hi(2, 0); l1_v_hi(1, 1)
                l0_w02(2, 0); norm2(1, 0); cand(0, 1, 1); l0_exp(2, 0); gate_r(0, 0, 2); l0_scale(2, 0)
                l1_norm(1, 1); rh_hi(0, 0, 2); hT_hi(0, 1, 1); l0_p_hi(2, 0); hN_hi(0, 1, 1); gate_z(0, 0, 2)
                cand(0, 0, 2); l0_u_hi(2, 0); norm1(1, 1); a_hi(0, 1, 2); l2_x_hi(1, 1); l0_elu(2, 0)
                gate_r(0, 1, 2); l2_u_hi(1, 1); take_x3(1, 0); rh_hi(0, 1, 2); take_x3_hi(1, 0); gate_z(0, 1, 2)
                norm0(2, 0); x0_hi(2, 1); a_hi(1, 0, 0); norm3(0, 0); l0_w02(2, 1); cand(0, 1, 2); norm2(1, 1)
                gate_r(1, 0, 0); x1T_hi(2, 0); l0_exp(2, 1); rh_hi(1, 0, 0); gate_z(1, 0, 0); l0_scale(2, 1)
                l1_y_hi(2, 0); cand(1, 0, 0); l0_p_hi(2, 1); take_x3(1, 1); l1_rel_hi(2, 0); take_x3_hi(1, 1)
                l0_u_hi(2, 1); l1_v_hi(2, 0); hT_hi(1, 0, 0); a_hi(1, 1, 0); hN_hi(1, 0, 0); norm3(0, 1)
                l0_elu(2, 1); l1_norm(2, 0); gate_r(1, 1, 0); rh_hi(1, 1, 0); norm0(2, 1); gate_z(1, 1, 0)
                a_hi(1, 0, 1); cand(1, 1, 0); x1T_hi(2, 1); norm1(2, 0); l2_x_hi(2, 0); hT_hi(1, 1, 0)
                gate_r(1, 0, 1); hN_hi(1, 1, 0); l2_u_hi(2, 0); rh_hi(1, 0, 1); gate_z(1, 0, 1); a_hi(1, 1, 1)
                cand(1, 0, 1); l1_y_hi(2, 1); norm2(2, 0)

            def merged(turn, *lags):
                def at(lag, step, *which):
                    if lag in lags:
                        step(turn - lag, *which)

                at(2, hT_hi, 0, 1)
                at(0, x0_hi, 0)
                at(2, hN_hi, 0, 1)
                at(1, l1_rel_hi, 1)
                at(2, gate_r, 1, 1)
                at(1, l1_v_hi, 1)
                at(2, rh_hi, 1, 1)
                at(2, gate_z, 1, 1)
                at(0, l0_w02, 0)
                at(2, a_hi, 0, 2)
                at(2, cand, 1, 1)
                at(0, l0_exp, 0)
                at(2, gate_r, 0, 2)
                at(1, l1_norm, 1)
                at(0, l0_scale, 0)
                at(2, hT_hi, 1, 1)
                at(2, rh_hi, 0, 2)
                at(2, hN_hi, 1, 1)
                at(0, l0_p_hi, 0)
                at(2, gate_z, 0, 2)
                at(2, cand, 0, 2)
                at(0, l0_u_hi, 0)
                at(1, norm1, 1)
                at(2, a_hi, 1, 2)
                at(1, l2_x_hi, 1)
                at(0, l0_elu, 0)
                at(2, gate_r, 1, 2)
                at(1, l2_u_hi, 1)
                at(1, take_x3, 0)
                at(1, take_x3_hi, 0)
                at(2, rh_hi, 1, 2)
                at(2, norm3, 0)
                at(2, gate_z, 1, 2)
                at(0, x0_hi, 1)
                at(0, norm0, 0)
                at(1, a_hi, 0, 0)
                at(2, cand, 1, 2)
                at(0, l0_w02, 1)
                at(1, norm2, 1)
                at(0, x1T_hi, 0)
                at(1, gate_r, 0, 0)
                at(0, l0_exp, 1)
                at(0, l0_scale, 1)
                at(1, rh_hi, 0, 0)
                at(1, gate_z, 0, 0)
                at(0, l1_y_hi, 0)
                at(0, l0_p_hi, 1)
                at(1, cand, 0, 0)
                at(1, take_x3, 1)
                at(0, l1_rel_hi, 0)
                at(1, take_x3_hi, 1)
                at(0, l0_u_hi, 1)
                at(1, hT_hi, 0, 0)
                at(1, hN_hi, 0, 0)
                at(0, l1_v_hi, 0)
                at(1, a_hi, 1, 0)
                at(2, norm3, 1)
                at(0, l0_elu, 1)
                at(0, l1_norm, 0)
                at(1, gate_r, 1, 0)
                at(1, rh_hi, 1, 0)
                at(0, norm0, 1)
                at(1, gate_z, 1, 0)
                at(1, a_hi, 0, 1)
                at(1, cand, 1, 0)
                at(0, x1T_hi, 1)
                at(0, norm1, 0)
                at(0, l2_x_hi, 0)
                at(1, hT_hi, 1, 0)
                at(1, gate_r, 0, 1)
                at(1, hN_hi, 1, 0)
                at(0, l2_u_hi, 0)
                at(1, rh_hi, 0, 1)
                at(0, l1_y_hi, 1)
                at(1, a_hi, 1, 1)
                at(1, cand, 0, 1)
                at(1, gate_z, 0, 1)
                at(0, norm2, 0)

            def last_turns():
                hT_hi(G - 2, 0, 1); gate_r(G - 2, 1, 1); rh_hi(G - 2, 1, 1); hN_hi(G - 2, 0, 1)
                l1_rel_hi(G - 1, 1); gate_z(G - 2, 1, 1); l1_v_hi(G - 1, 1); cand(G - 2, 1, 1)
                a_hi(G - 2, 0, 2); l1_norm(G - 1, 1); hT_hi(G - 2, 1, 1); hN_hi(G - 2, 1, 1)
                gate_r(G - 2, 0, 2); rh_hi(G - 2, 0, 2); a_hi(G - 2, 1, 2); norm1(G - 1, 1); l2_x_hi(G - 1, 1)
                gate_z(G - 2, 0, 2); cand(G - 2, 0, 2); gate_r(G - 2, 1, 2); l2_u_hi(G - 1, 1)
                rh_hi(G - 2, 1, 2); gate_z(G - 2, 1, 2); take_x3(G - 1, 0); take_x3_hi(G - 1, 0)
                cand(G - 2, 1, 2); a_hi(G - 1, 0, 0); norm3(G - 2, 0); norm2(G - 1, 1); gate_r(G - 1, 0, 0)
                rh_hi(G - 1, 0, 0); gate_z(G - 1, 0, 0); take_x3(G - 1, 1); cand(G - 1, 0, 0)
                take_x3_hi(G - 1, 1); norm3(G - 2, 1); a_hi(G - 1, 1, 0); hT_hi(G - 1, 0, 0); hN_hi(G - 1, 0, 0)
                gate_r(G - 1, 1, 0); rh_hi(G - 1, 1, 0); gate_z(G - 1, 1, 0); a_hi(G - 1, 0, 1)
                cand(G - 1, 1, 0); gate_r(G - 1, 0, 1); rh_hi(G - 1, 0, 1); hT_hi(G - 1, 1, 0)
                gate_z(G - 1, 0, 1); hN_hi(G - 1, 1, 0); cand(G - 1, 0, 1); a_hi(G - 1, 1, 1)
                hT_hi(G - 1, 0, 1); hN_hi(G - 1, 0, 1); gate_r(G - 1, 1, 1); rh_hi(G - 1, 1, 1)
                a_hi(G - 1, 0, 2); gate_z(G - 1, 1, 1); cand(G - 1, 1, 1); gate_r(G - 1, 0, 2)
                hT_hi(G - 1, 1, 1); hN_hi(G - 1, 1, 1); rh_hi(G - 1, 0, 2); gate_z(G - 1, 0, 2)
                a_hi(G - 1, 1, 2); cand(G - 1, 0, 2); gate_r(G - 1, 1, 2); rh_hi(G - 1, 1, 2)
                gate_z(G - 1, 1, 2); cand(G - 1, 1, 2); norm3(G - 1, 0); norm3(G - 1, 1)

            first_turns()
            with act.Fori(3, G) as i:
                merged(i, 0, 1, 2)
            last_turns()

        @block.vector
        def _(dve):
            def sum_halves(name):
                dve.wait_ge(c["loaded_third"], 16 * THIRD)
                whole, w = dict(w4=(w4_sum, w4_s), w5=(w5_sum, w5_s), w34=(w34_sum, w3_s))[name]
                total = dve.tensor_tensor(whole, w[:, :, 0:D], w[:, :, D:2 * D], ALU.add)
                if name != "w34":
                    total.then_inc(c["w_sums"], 1)
                    return
                total.then_inc(c["w_sum"], 1)
                dve.wait_ge(c["w_sum"], 1)
                dve.wait_ge(c["w_sums"], 1)
                dve.tensor_tensor(whole, whole, w4_sum, ALU.subtract).then_inc(c["w_sums"], 1)

            def sum_wa():
                dve.wait_ge(c["loaded_first"], 16 * FIRST)
                for k in range(DT):
                    for j in range(2):
                        dve.tensor_tensor_reduce(products[j][:, k, 0, :], w0_s[:, k, :], arow[:, j, :], 1.0, 0.0,
                                                 ALU.mult, ALU.add, wsum[:, k, j:j + 1]).then_inc(c["wa_sum"], 1)

            def take_wa():
                dve.wait_ge(c["wa_turned"], 1)
                dve.tensor_copy(wa[:, :, :].rearrange("p j c -> p (j c)"), pA[1][:, :]).then_inc(c["wa_ready"], 1)

            def beta_identity():
                dve.wait_ge(c["loaded_first"], 16 * FIRST)
                dve.wait_ge(c["ident_ready"], 1)
                for k in range(NT):
                    dve.tensor_scalar(beta_ident[:, k, :], ident[:, :], beta_c[:, 0:1], None,
                                      ALU.mult).then_inc(c["beta_ready"], 1)

            def degrees():
                dve.wait_ge(c["loaded_first"], 16 * FIRST)
                dve.tensor_reduce(deg[:, 0:NT], adjN[:, :, :], mybir.AxisListType.X, ALU.add).then_inc(c["deg_step"], 1)
                dve.wait_ge(c["deg_step"], 1)
                dve.tensor_scalar(deg[:, NT:2 * NT], deg[:, 0:NT], 1e-38, None, ALU.max).then_inc(c["deg_step"], 1)
                dve.tensor_scalar(deg[:, 2 * NT:3 * NT], deg[:, 0:NT], 0.0, None, ALU.is_gt).then_inc(c["deg_step"], 1)

            def take_dinv():
                dve.wait_ge(c["deg_pow"], 1)
                dve.wait_ge(c["deg_step"], 3)
                dve.tensor_tensor(dinv[:, :], deg[:, 3 * NT:4 * NT], deg[:, 2 * NT:3 * NT],
                                  ALU.mult).then_inc(c["dinv_ready"], 1)

            def sum_biases():
                dve.wait_ge(c["loaded_third"], 16 * THIRD)
                dve.tensor_tensor(bz[:, :], braw[:, 0, :], braw[:, 1, :], ALU.add).then_inc(c["bias_step"], 1)
                dve.tensor_tensor(br[:, :], braw[:, 2, :], braw[:, 1, :], ALU.add).then_inc(c["bias_step"], 1)
                dve.tensor_tensor(bh[:, :], braw[:, 3, :], braw[:, 4, :], ALU.add).then_inc(c["bias_ready"], 1)
                dve.wait_ge(c["bias_step"], 2)
                dve.tensor_scalar(bz[:, :], bz[:, :], 0.5, None, ALU.mult).then_inc(c["bias_ready"], 1)
                dve.tensor_scalar(br[:, :], br[:, :], 0.5, None, ALU.mult).then_inc(c["bias_ready"], 1)

            def matrix_lo(name):
                dve.wait_ge(c["matrix_hi"], made(name))
                hi_part, lo_part = matrix[name]
                bank = matrix_bank[name][:, :]
                if name == "u5":
                    dve.scalar_tensor_tensor(flat(lo_part), bank, 0.5, f32(flat(hi_part)), ALU.mult,
                                             ALU.subtract).then_inc(c["matrix_lo"], 1)
                else:
                    dve.tensor_tensor(flat(lo_part), bank, f32(flat(hi_part)), ALU.subtract).then_inc(c["matrix_lo"], 1)

            def flag_adj_lo():
                dve.wait_ge(c["matrix_lo"], made("adjT"))
                dve.tensor_scalar(flat(Y[1]), f32(flat(adjT[1])), 0.0, None, ALU.not_equal).then_inc(c["lo_flags"], 1)
                dve.wait_ge(c["lo_flags"], 1)
                dve.tensor_reduce(flags[:, :], Y[1][:, :, :], mybir.AxisListType.XY, ALU.max).then_inc(c["lo_flags"], 1)

            def take_flag():
                dve.wait_ge(c["flags_turned"], 1)
                dve.tensor_reduce(flag[:, :], pH[0][0:1, 0:P], mybir.AxisListType.X, ALU.max).then_inc(c["adj_flag"], 1)

            def w0_lo():
                dve.wait_ge(c["direct_hi"], 1)
                dve.tensor_tensor(w0[1][:, :, :], w0_s, f32(w0[0][:, :, :]), ALU.subtract).then_inc(c["direct_lo"], 1)

            def w2_lo():
                dve.wait_ge(c["direct_hi"], 2)
                dve.tensor_tensor(w2[1][:, :, :], w2_s, f32(w2[0][:, :, :]), ALU.subtract).then_inc(c["direct_lo"], 1)

            def lo(o, full, hi):
                return dve.tensor_tensor(o, full, f32(hi), ALU.subtract)

            def statistics(s, rows_of, sums, means, small, n, ready, mean_ready):
                for k in range(NT):
                    dve.bn_stats(sums[:, k, :], rows_of[:, k, :]).then_inc(ready, 1)
                dve.wait_ge(ready, 2 * n + 2)
                dve.memset(scratch[:, 0:1], 0.0)
                for k in range(NT):
                    dve.bn_aggr(means[:, k, :], sums[:, k, :]).then_inc(mean_ready, 1)
                dve.wait_ge(mean_ready, 3 * n + 2)
                dve.tensor_scalar(small[:, 2, :], means[:, :, 0], -1.0, None, ALU.mult).then_inc(mean_ready, 1)

            def stats(g, b, layer):
                s = f[b]
                n = 3 * g + layer
                dve.wait_ge(s["y_ready"], n + 1)
                statistics(s, Y[b], st[b], mv[b], ln[b], n, s["stats_ready"], s["mean_ready"])

            def l0_s(g, b):
                s = f[b]
                first(dve, g, c["wa_ready"], 1)
                dve.wait_ge(s["x_loaded"], 16 * g + 16)
                for k in range(NT):
                    for j in range(2):
                        dve.tensor_tensor_reduce(products[b][:, k, j, :], X0[b][:, k, :], wa[:, j, :], 1.0, 0.0,
                                                 ALU.mult, ALU.add, s12[b][:, k, j:j + 1]).then_inc(s["s_ready"], 1)
                dve.wait_ge(s["s_ready"], 5 * g + 4)
                dve.tensor_scalar(s1x[b][:, :], s12[b][:, :, 0], SLOPE, None, ALU.mult).then_inc(s["s_ready"], 1)

            def l0_mask(g, b):
                s = f[b]
                dve.wait_ge(s["w02_ready"], 2 * g + 2)
                for k in range(NT):
                    dve.scalar_tensor_tensor(E[b][:, k, :], pF[b][:, 0:N], s12[b][:, k, 0:1], W02[b][:, k, :],
                                             ALU.add, ALU.max).then_inc(s["lrelu_ready"], 1)
                dve.wait_ge(c["adj_flag"], 1)
                dve.wait_ge(s["lrelu_ready"], 2 * g + 2)
                for k in range(NT):
                    dve.tensor_tensor_reduce(E2[b][:, k, :], E[b][:, k, :], adjN[:, k, :], 1.0, -3e38, ALU.mult,
                                             ALU.max, nmx[b][:, k:k + 1]).then_inc(s["masked_ready"], 1)
                dve.wait_ge(s["masked_ready"], 2 * g + 2)
                dve.tensor_scalar(nmx[b][:, NT:2 * NT], nmx[b][:, 0:NT], -1.0, None,
                                  ALU.mult).then_inc(s["max_ready"], 1)

            def l0_rinv(g, b):
                s = f[b]
                dve.wait_ge(s["exp_ready"], 2 * g + 2)
                dve.reciprocal(rs[b][:, NT:2 * NT], rs[b][:, 0:NT]).then_inc(s["rinv_ready"], 1)

            def l0_diagonal(g, b):
                s = f[b]
                first(dve, g, c["beta_ready"], 2)
                dve.wait_ge(s["scaled_ready"], 2 * g + 2)
                blocks = flat(W02[b]).rearrange("p (a q) -> p a q", q=P)[:, 0:NT * NT:NT + 1, :]
                dve.tensor_tensor(blocks, blocks, beta_ident[:, :, :], ALU.add).then_inc(s["p_ready"], 1)

            def l0_p_lo(g, b):
                s = f[b]
                dve.wait_ge(s["part_hi"], parted(g, "p"))
                lo(flat(pt[b][1]), pF[b][:, :], flat(pt[b][0])).then_inc(s["part_lo"], 1)

            def l0_u_lo(g, b):
                s = f[b]
                dve.wait_ge(s["part_hi"], parted(g, "u0"))
                lo(flat(yT[b][1]), pF[b][:, :], flat(yT[b][0])).then_inc(s["part_lo"], 1)

            def l0_elu_out(g, b):
                s = f[b]
                dve.wait_ge(s["elu_exp"], g + 1)
                dve.scalar_tensor_tensor(flat(V[b]), pF[b][:, :], 0.0, flat(E[b]), ALU.max,
                                         ALU.add).then_inc(s["elu_ready"], 1)
                dve.wait_ge(s["elu_ready"], g + 1)
                dve.scalar_tensor_tensor(flat(Y[b]), flat(V[b]), -1.0, flat(X0[b]), ALU.add,
                                         ALU.add).then_inc(s["y_ready"], 1)

            def x1T_lo(g, b):
                s = f[b]
                dve.wait_ge(s["part_hi"], parted(g, "xT1"))
                lo(flat(xT[b][1]), pF[b][:, :], flat(xT[b][0])).then_inc(s["part_lo"], 1)

            def l1_y_lo(g, b):
                dve.wait_ge(f[b]["part_hi"], parted(g, "yT"))
                lo(flat(yT[b][1]), pF[b][:, :], flat(yT[b][0])).then_inc(f[b]["part_lo"], 1)

            def l1_mask(g, b):
                s = f[b]
                dve.wait_ge(s["front_psum"], in_bank(g, "rel"))
                dve.tensor_tensor(flat(R[b]), pF[b][:, :], flat(adjN), ALU.mult).then_inc(s["rel_masked"], 1)

            def l1_v_lo(g, b):
                dve.wait_ge(f[b]["vv_hi"], g + 1)
                lo(flat(hs[b][1]), pF[b][:, :], flat(hs[b][0])).then_inc(f[b]["vv_lo"], 1)

            def l1_residual(g, b):
                s = f[b]
                dve.wait_ge(s["front_psum"], in_bank(g, "out1"))
                dve.wait_ge(s["rn_ready"], g + 1)
                for k in range(NT):
                    last = dve.scalar_tensor_tensor(Y[b][:, k, :], pF[b][:, k * D:k * D + D],
                                                    rn[b][:, NT + k:NT + k + 1], X1[b][:, k, :], ALU.mult, ALU.add)
                last.then_inc(s["y_ready"], 1)

            def l2_x_lo(g, b):
                s = f[b]
                dve.wait_ge(s["part_hi"], parted(g, "x2"))
                for k in range(NT):
                    dve.scalar_tensor_tensor(hs[b][1][:, k, :], X2[b][:, k, :], dinv[:, k:k + 1],
                                             f32(hs[b][0][:, k, :]), ALU.mult, ALU.subtract).then_inc(s["part_lo"], 1)

            def l2_u_lo(g, b):
                s = f[b]
                dve.wait_ge(s["part_hi"], parted(g, "u2"))
                lo(flat(yT[b][1]), pF[b][:, :], flat(yT[b][0])).then_inc(s["part_lo"], 1)

            def l2_residual(g, b):
                s = f[b]
                dve.wait_ge(s["front_psum"], in_bank(g, "out2"))
                dve.wait_ge(s["xb_ready"], g + 1)
                for k in range(NT):
                    last = dve.scalar_tensor_tensor(Y[b][:, k, :], pF[b][:, k * D:k * D + D],
                                                    dinv[:, k:k + 1], XB[b][:, k, :], ALU.mult, ALU.add)
                last.then_inc(s["y_ready"], 1)

            def take_x3(g, b):
                s = f[b]
                dve.wait_ge(s["hT_hi"], 3 * g + 1)
                lo(flat(hTs[b][1]), flat(hT[b]), flat(hTs[b][0])).then_inc(s["hT_lo"], 1)

            def a_lo(g, b, t):
                dve.wait_ge(f[b]["a_hi"], 3 * g + t + 1)
                lo(flat(aT[b][1]), pA[b][:, :], flat(aT[b][0])).then_inc(f[b]["a_lo"], 1)

            def reset(g, b, t):
                dve.wait_ge(f[b]["r_ready"], 2 * (3 * g + t + 1))
                dve.scalar_tensor_tensor(flat(rh[b]), flat(tr[b]), 1.0, flat(hT[b]), ALU.add,
                                         ALU.mult).then_inc(f[b]["rh_ready"], 1)

            def rh_lo(g, b, t):
                dve.wait_ge(f[b]["rh_hi"], 3 * g + t + 1)
                lo(flat(rhs[b][1]), flat(rh[b]), flat(rhs[b][0])).then_inc(f[b]["rh_lo"], 1)

            def diff(g, b, t):
                n = 3 * g + t
                dve.wait_ge(f[b]["hv_ready"], 2 * n + 2)
                dve.tensor_tensor(flat(rh[b]), flat(hv[b]), flat(hT[b]), ALU.subtract).then_inc(f[b]["diff_ready"], 1)

            def gated(g, b, t):
                n = 3 * g + t
                dve.wait_ge(f[b]["diff_ready"], n + 1)
                dve.wait_ge(f[b]["z_ready"], 2 * n + 2)
                dve.scalar_tensor_tensor(flat(rh[b]), flat(tz[b]), 1.0, flat(rh[b]), ALU.add,
                                         ALU.mult).then_inc(f[b]["gated_ready"], 1)

            def h_new(g, b, t):
                dve.wait_ge(f[b]["gated_ready"], 3 * g + t + 1)
                dve.scalar_tensor_tensor(flat(hT[b]), flat(rh[b]), 0.5, flat(hT[b]), ALU.mult,
                                         ALU.add).then_inc(f[b]["h_new"], 1)

            def hT_lo(g, b, t):
                dve.wait_ge(f[b]["hT_hi"], 3 * g + t + 2)
                lo(flat(hTs[b][1]), flat(hT[b]), flat(hTs[b][0])).then_inc(f[b]["hT_lo"], 1)

            def hN_lo(g, b, t):
                dve.wait_ge(f[b]["hN_hi"], 3 * g + t + 2)
                lo(flat(hN[b][1]), pA[b][:, :], flat(hN[b][0])).then_inc(f[b]["hN_lo"], 1)

            def residual3(g, b):
                s = f[b]
                dve.wait_ge(s["hN_psum"], 3 * g + 3)
                dve.wait_ge(s["xr_copied"], 16 * g + 16)
                once(dve, s["stored"], 16 * g)
                dve.tensor_tensor(flat(YO[b]), pA[b][:, :], flat(XR[b]), ALU.add).then_inc(s["yo_ready"], 1)

            def stats3(g, b):
                s = f[b]
                dve.wait_ge(s["yo_ready"], g + 1)
                statistics(s, YO[b], st3[b], mv3[b], ln3[b], g, s["stats3"], s["mean3"])

            def first_turns():
                degrees(); sum_wa(); take_dinv(); matrix_lo("adjT"); beta_identity(); flag_adj_lo(); take_wa()
                take_flag(); l0_s(0, 0); l0_s(0, 1); l0_mask(0, 0); l0_mask(0, 1); l0_rinv(0, 0); sum_biases()
                matrix_lo("gqk"); l0_rinv(0, 1); sum_halves("w4"); l0_diagonal(0, 0); sum_halves("w34")
                l0_diagonal(0, 1); sum_halves("w5"); l0_p_lo(0, 0); w0_lo(); l0_p_lo(0, 1); matrix_lo("wv")
                w2_lo(); l0_u_lo(0, 0); matrix_lo("u3"); l0_u_lo(0, 1); matrix_lo("w4"); matrix_lo("w34")
                matrix_lo("w5"); l0_elu_out(0, 0); l0_elu_out(0, 1); stats(0, 0, 0); stats(0, 1, 0); l0_s(1, 0)
                l0_s(1, 1); x1T_lo(0, 0); matrix_lo("u5"); x1T_lo(0, 1); l1_y_lo(0, 0); l1_y_lo(0, 1)
                l1_mask(0, 0); l1_mask(0, 1); l1_v_lo(0, 0); l1_v_lo(0, 1); l1_residual(0, 0); stats(0, 0, 1)
                l1_residual(0, 1); stats(0, 1, 1); l2_x_lo(0, 0); l2_x_lo(0, 1); l2_u_lo(0, 0); l2_u_lo(0, 1)
                l2_residual(0, 0); stats(0, 0, 2); l2_residual(0, 1); stats(0, 1, 2); l0_mask(1, 0)
                l0_mask(1, 1); l0_rinv(1, 0); take_x3(0, 0); l0_diagonal(1, 0); a_lo(0, 0, 0); l0_rinv(1, 1)
                take_x3(0, 1); l0_p_lo(1, 0); l0_diagonal(1, 1); reset(0, 0, 0); l0_u_lo(1, 0); l0_p_lo(1, 1)
                rh_lo(0, 0, 0); l0_elu_out(1, 0); l0_u_lo(1, 1); stats(1, 0, 0); a_lo(0, 1, 0); diff(0, 0, 0)
                gated(0, 0, 0); l0_s(2, 0); h_new(0, 0, 0); l0_elu_out(1, 1); x1T_lo(1, 0); reset(0, 1, 0)
                stats(1, 1, 0); hN_lo(0, 0, 0); hT_lo(0, 0, 0); rh_lo(0, 1, 0); l1_y_lo(1, 0); l0_s(2, 1)
                a_lo(0, 0, 1); diff(0, 1, 0); l1_mask(1, 0); gated(0, 1, 0); x1T_lo(1, 1); h_new(0, 1, 0)
                reset(0, 0, 1); hT_lo(0, 1, 0); l1_v_lo(1, 0); rh_lo(0, 0, 1); hN_lo(0, 1, 0); l1_residual(1, 0)
                stats(1, 0, 1); a_lo(0, 1, 1); diff(0, 0, 1); gated(0, 0, 1); l1_y_lo(1, 1); h_new(0, 0, 1)
                l2_x_lo(1, 0); hT_lo(0, 0, 1); reset(0, 1, 1); l1_mask(1, 1); hN_lo(0, 0, 1); rh_lo(0, 1, 1)
                l2_u_lo(1, 0); a_lo(0, 0, 2); l2_residual(1, 0); stats(1, 0, 2); l1_v_lo(1, 1); l0_mask(2, 0)
                diff(0, 1, 1); l0_rinv(2, 0); gated(0, 1, 1); reset(0, 0, 2); l0_diagonal(2, 0); h_new(0, 1, 1)
                rh_lo(0, 0, 2); hT_lo(0, 1, 1); l0_p_lo(2, 0); hN_lo(0, 1, 1); l1_residual(1, 1); stats(1, 1, 1)
                diff(0, 0, 2); gated(0, 0, 2); l0_u_lo(2, 0); h_new(0, 0, 2); a_lo(0, 1, 2); l2_x_lo(1, 1)
                residual3(0, 0); l0_elu_out(2, 0); reset(0, 1, 2); stats(2, 0, 0); l2_u_lo(1, 1); rh_lo(0, 1, 2)
                take_x3(1, 0); stats3(0, 0); l2_residual(1, 1); stats(1, 1, 2); a_lo(1, 0, 0); l0_mask(2, 1)
                diff(0, 1, 2); reset(1, 0, 0); x1T_lo(2, 0); gated(0, 1, 2); rh_lo(1, 0, 0); l0_rinv(2, 1)
                h_new(0, 1, 2); l0_diagonal(2, 1); l1_y_lo(2, 0); residual3(0, 1); diff(1, 0, 0); l0_p_lo(2, 1)
                l1_mask(2, 0); stats3(0, 1); gated(1, 0, 0); h_new(1, 0, 0); take_x3(1, 1); l0_u_lo(2, 1)
                hT_lo(1, 0, 0); l1_v_lo(2, 0); hN_lo(1, 0, 0); a_lo(1, 1, 0); l0_elu_out(2, 1); stats(2, 1, 0)
                reset(1, 1, 0); l1_residual(2, 0); rh_lo(1, 1, 0); stats(2, 0, 1); a_lo(1, 0, 1); diff(1, 1, 0)
                x1T_lo(2, 1); gated(1, 1, 0); h_new(1, 1, 0); l2_x_lo(2, 0); hT_lo(1, 1, 0); reset(1, 0, 1)
                hN_lo(1, 1, 0); l2_u_lo(2, 0); rh_lo(1, 0, 1); a_lo(1, 1, 1); l2_residual(2, 0); stats(2, 0, 2)
                diff(1, 0, 1)

            def merged(turn, *lags):
                def at(lag, step, *which):
                    if lag in lags:
                        step(turn - lag, *which)

                at(1, l1_y_lo, 1)
                at(2, gated, 0, 1)
                at(2, h_new, 0, 1)
                at(2, hT_lo, 0, 1)
                at(1, l1_mask, 1)
                at(0, l0_s, 0)
                at(2, hN_lo, 0, 1)
                at(2, reset, 1, 1)
                at(0, l0_s, 1)
                at(2, rh_lo, 1, 1)
                at(1, l1_v_lo, 1)
                at(2, a_lo, 0, 2)
                at(0, l0_mask, 0)
                at(2, diff, 1, 1)
                at(2, gated, 1, 1)
                at(0, l0_rinv, 0)
                at(2, h_new, 1, 1)
                at(2, reset, 0, 2)
                at(0, l0_diagonal, 0)
                at(2, hT_lo, 1, 1)
                at(2, rh_lo, 0, 2)
                at(2, hN_lo, 1, 1)
                at(0, l0_p_lo, 0)
                at(1, l1_residual, 1)
                at(1, stats, 1, 1)
                at(2, diff, 0, 2)
                at(2, gated, 0, 2)
                at(0, l0_u_lo, 0)
                at(2, h_new, 0, 2)
                at(2, a_lo, 1, 2)
                at(1, l2_x_lo, 1)
                at(2, residual3, 0)
                at(0, l0_elu_out, 0)
                at(2, stats3, 0)
                at(1, l2_u_lo, 1)
                at(2, reset, 1, 2)
                at(0, stats, 0, 0)
                at(2, rh_lo, 1, 2)
                at(1, l2_residual, 1)
                at(1, take_x3, 0)
                at(1, stats, 1, 2)
                at(1, a_lo, 0, 0)
                at(2, diff, 1, 2)
                at(0, l0_mask, 1)
                at(0, x1T_lo, 0)
                at(2, gated, 1, 2)
                at(0, l0_rinv, 1)
                at(1, reset, 0, 0)
                at(2, h_new, 1, 2)
                at(0, l0_diagonal, 1)
                at(1, rh_lo, 0, 0)
                at(2, residual3, 1)
                at(0, l1_y_lo, 0)
                at(0, l0_p_lo, 1)
                at(2, stats3, 1)
                at(1, diff, 0, 0)
                at(0, l1_mask, 0)
                at(1, gated, 0, 0)
                at(1, h_new, 0, 0)
                at(1, take_x3, 1)
                at(0, l0_u_lo, 1)
                at(1, hT_lo, 0, 0)
                at(1, hN_lo, 0, 0)
                at(0, l1_v_lo, 0)
                at(1, a_lo, 1, 0)
                at(0, l0_elu_out, 1)
                at(0, stats, 1, 0)
                at(1, reset, 1, 0)
                at(0, l1_residual, 0)
                at(1, rh_lo, 1, 0)
                at(0, stats, 0, 1)
                at(1, a_lo, 0, 1)
                at(1, diff, 1, 0)
                at(0, x1T_lo, 1)
                at(1, gated, 1, 0)
                at(1, h_new, 1, 0)
                at(0, l2_x_lo, 0)
                at(1, hT_lo, 1, 0)
                at(1, reset, 0, 1)
                at(1, hN_lo, 1, 0)
                at(0, l2_u_lo, 0)
                at(1, rh_lo, 0, 1)
                at(1, a_lo, 1, 1)
                at(0, l2_residual, 0)
                at(0, stats, 0, 2)
                at(1, diff, 0, 1)

            def last_turns():
                l1_y_lo(G - 1, 1); gated(G - 2, 0, 1); h_new(G - 2, 0, 1); hT_lo(G - 2, 0, 1)
                reset(G - 2, 1, 1); l1_mask(G - 1, 1); rh_lo(G - 2, 1, 1); hN_lo(G - 2, 0, 1); l1_v_lo(G - 1, 1)
                diff(G - 2, 1, 1); a_lo(G - 2, 0, 2); gated(G - 2, 1, 1); h_new(G - 2, 1, 1)
                l1_residual(G - 1, 1); hT_lo(G - 2, 1, 1); hN_lo(G - 2, 1, 1); stats(G - 1, 1, 1)
                reset(G - 2, 0, 2); rh_lo(G - 2, 0, 2); a_lo(G - 2, 1, 2); l2_x_lo(G - 1, 1); diff(G - 2, 0, 2)
                gated(G - 2, 0, 2); h_new(G - 2, 0, 2); reset(G - 2, 1, 2); residual3(G - 2, 0)
                l2_u_lo(G - 1, 1); rh_lo(G - 2, 1, 2); stats3(G - 2, 0); l2_residual(G - 1, 1)
                take_x3(G - 1, 0); stats(G - 1, 1, 2); diff(G - 2, 1, 2); a_lo(G - 1, 0, 0); gated(G - 2, 1, 2)
                h_new(G - 2, 1, 2); reset(G - 1, 0, 0); residual3(G - 2, 1); rh_lo(G - 1, 0, 0)
                stats3(G - 2, 1); diff(G - 1, 0, 0); take_x3(G - 1, 1); gated(G - 1, 0, 0); h_new(G - 1, 0, 0)
                a_lo(G - 1, 1, 0); hT_lo(G - 1, 0, 0); hN_lo(G - 1, 0, 0); reset(G - 1, 1, 0)
                rh_lo(G - 1, 1, 0); a_lo(G - 1, 0, 1); diff(G - 1, 1, 0); gated(G - 1, 1, 0); reset(G - 1, 0, 1)
                h_new(G - 1, 1, 0); rh_lo(G - 1, 0, 1); hT_lo(G - 1, 1, 0); hN_lo(G - 1, 1, 0)
                diff(G - 1, 0, 1); gated(G - 1, 0, 1); h_new(G - 1, 0, 1); a_lo(G - 1, 1, 1); hT_lo(G - 1, 0, 1)
                hN_lo(G - 1, 0, 1); reset(G - 1, 1, 1); rh_lo(G - 1, 1, 1); a_lo(G - 1, 0, 2); diff(G - 1, 1, 1)
                gated(G - 1, 1, 1); h_new(G - 1, 1, 1); reset(G - 1, 0, 2); hT_lo(G - 1, 1, 1)
                hN_lo(G - 1, 1, 1); rh_lo(G - 1, 0, 2); a_lo(G - 1, 1, 2); diff(G - 1, 0, 2); gated(G - 1, 0, 2)
                h_new(G - 1, 0, 2); reset(G - 1, 1, 2); rh_lo(G - 1, 1, 2); residual3(G - 1, 0)
                stats3(G - 1, 0); diff(G - 1, 1, 2); gated(G - 1, 1, 2); h_new(G - 1, 1, 2); residual3(G - 1, 1)
                stats3(G - 1, 1)

            first_turns()
            with dve.Fori(3, G) as i:
                merged(i, 0, 1, 2)
            last_turns()

        @block.gpsimd
        def _(pool):
            pool.memset(ident[:, :], 0.0).then_inc(c["ident_zero"], 1)
            pool.memset(minus_half[:, :], -0.5).then_inc(c["const_ready"], 1)
            pool.memset(eps[:, :], EPS).then_inc(c["const_ready"], 1)
            pool.wait_ge(c["ident_zero"], 1)
            pool.affine_select(out=ident[:, :], in_=ident[:, :], compare_op=ALU.not_equal, fill=1.0, base=0,
                               pattern=[[-1, P]], channel_multiplier=1).then_inc(c["ident_ready"], 1)
            pool.wait_ge(c["const_ready"], 2)

            def lo(o, full, hi):
                return pool.tensor_tensor(o, full, f32(hi), ALU.subtract)

            def degree_power():
                pool.wait_ge(c["deg_step"], 2)
                pool.tensor_tensor(deg[:, 3 * NT:4 * NT], deg[:, NT:2 * NT], minus_half[:, 0:NT],
                                   ALU.pow).then_inc(c["deg_pow"], 1)

            def deviation(means, small, n, mean_ready, ready):
                pool.wait_ge(mean_ready, 3 * n + 3)
                pool.tensor_tensor(small[:, 0, :], means[:, :, 1], eps[:, :], ALU.add).then_inc(ready, 1)
                pool.wait_ge(ready, 3 * n + 1)
                pool.tensor_tensor(small[:, 1, :], small[:, 0, :], minus_half[:, :], ALU.pow).then_inc(ready, 1)
                pool.wait_ge(ready, 3 * n + 2)
                pool.tensor_tensor(small[:, 3, :], small[:, 2, :], small[:, 1, :], ALU.mult).then_inc(ready, 1)

            def rstd_of(g, b, layer):
                deviation(mv[b], ln[b], 3 * g + layer, f[b]["mean_ready"], f[b]["rstd_ready"])

            def rstd3_of(g, b):
                deviation(mv3[b], ln3[b], g, f[b]["mean3"], f[b]["rstd3_ready"])

            def x0_lo(g, b):
                s = f[b]
                pool.wait_ge(s["x0_hi"], g + 1)
                lo(flat(hs[b][1]), flat(X0[b]), flat(hs[b][0])).then_inc(s["x0_lo"], 1)

            def l1_rel_lo(g, b):
                s = f[b]
                pool.wait_ge(s["rel_hi"], g + 1)
                lo(flat(pt[b][1]), flat(R[b]), flat(pt[b][0])).then_inc(s["rel_lo"], 1)

            def take_x3(g, b):
                s = f[b]
                pool.wait_ge(s["hN_hi"], 3 * g + 1)
                lo(flat(hN[b][1]), flat(X3[b]), flat(hN[b][0])).then_inc(s["hN_lo"], 1)

            def rnorm(g, b):
                s = f[b]
                pool.wait_ge(s["norm_ready"], 2 * g + 2)
                pool.tensor_tensor(rn[b][:, NT:2 * NT], rn[b][:, 0:NT], minus_half[:, 0:NT],
                                   ALU.pow).then_inc(s["rn_ready"], 1)

            def add_bias2(g, b):
                s = f[b]
                first(pool, g, c["loaded_third"], 16 * THIRD)
                pool.wait_ge(s["x2_ready"], 2 * g + 2)
                pool.tensor_tensor(flat(XB[b]), flat(X2[b]), bias2_r[:, :], ALU.add).then_inc(s["xb_ready"], 1)

            def first_turns():
                degree_power(); x0_lo(0, 0); x0_lo(0, 1); rstd_of(0, 0, 0); rstd_of(0, 1, 0); l1_rel_lo(0, 0)
                l1_rel_lo(0, 1); rnorm(0, 0); rnorm(0, 1); rstd_of(0, 0, 1); rstd_of(0, 1, 1); add_bias2(0, 0)
                add_bias2(0, 1); x0_lo(1, 0); rstd_of(0, 0, 2); x0_lo(1, 1); rstd_of(0, 1, 2); take_x3(0, 0)
                take_x3(0, 1); rstd_of(1, 0, 0); rstd_of(1, 1, 0); l1_rel_lo(1, 0); rnorm(1, 0)
                rstd_of(1, 0, 1); add_bias2(1, 0); l1_rel_lo(1, 1); x0_lo(2, 0); rstd_of(1, 0, 2); rnorm(1, 1)
                rstd_of(1, 1, 1); add_bias2(1, 1); take_x3(1, 0); rstd_of(2, 0, 0); rstd3_of(0, 0); x0_lo(2, 1)
                rstd_of(1, 1, 2); take_x3(1, 1); rstd3_of(0, 1); l1_rel_lo(2, 0); rnorm(2, 0); rstd_of(2, 1, 0)
                rstd_of(2, 0, 1); add_bias2(2, 0); rstd_of(2, 0, 2)

            def merged(turn, *lags):
                def at(lag, step, *which):
                    if lag in lags:
                        step(turn - lag, *which)

                at(0, x0_lo, 0)
                at(1, l1_rel_lo, 1)
                at(1, rnorm, 1)
                at(1, rstd_of, 1, 1)
                at(1, add_bias2, 1)
                at(2, rstd3_of, 0)
                at(1, take_x3, 0)
                at(0, rstd_of, 0, 0)
                at(0, x0_lo, 1)
                at(1, rstd_of, 1, 2)
                at(2, rstd3_of, 1)
                at(1, take_x3, 1)
                at(0, l1_rel_lo, 0)
                at(0, rnorm, 0)
                at(0, rstd_of, 1, 0)
                at(0, rstd_of, 0, 1)
                at(0, add_bias2, 0)
                at(0, rstd_of, 0, 2)

            def last_turns():
                l1_rel_lo(G - 1, 1); rnorm(G - 1, 1); rstd_of(G - 1, 1, 1); add_bias2(G - 1, 1)
                take_x3(G - 1, 0); rstd3_of(G - 2, 0); rstd_of(G - 1, 1, 2); rstd3_of(G - 2, 1)
                take_x3(G - 1, 1); rstd3_of(G - 1, 0); rstd3_of(G - 1, 1)

            first_turns()
            with pool.Fori(3, G) as i:
                merged(i, 0, 1, 2)
            last_turns()


_INS = ['x', 'adj', 'L0_gnn_W', 'L0_gnn_a', 'L0_gnn_beta', 'L1_gnn_Wq', 'L1_gnn_Wk', 'L1_gnn_Wv', 'L2_gnn_weight',
        'L2_gnn_bias', 'L3_gnn_w3_w', 'L3_gnn_w3_b', 'L3_gnn_u3_w', 'L3_gnn_u3_b', 'L3_gnn_w4_w', 'L3_gnn_w4_b',
        'L3_gnn_w5_w', 'L3_gnn_w5_b', 'L3_gnn_u5_w', 'L3_gnn_u5_b']
_OUTS = [((B, N, D), 'float32')]


def kernel(**inputs):
    import numpy as _np
    import concourse.bacc as _bacc
    from concourse import mybir as _mybir
    from concourse.bass_utils import run_bass_kernel_spmd as _run

    nc = _bacc.Bacc("TRN2", target_bir_lowering=False, num_devices=1)
    arrays, args = {}, []
    for name in _INS:
        a = _np.ascontiguousarray(inputs[name])
        arrays[f"in_{name}_dram"] = a
        args.append(nc.dram_tensor(f"in_{name}_dram", a.shape, _mybir.dt.from_np(a.dtype), kind="ExternalInput").ap())
    for i, (shape, dtype) in enumerate(_OUTS):
        dt = _mybir.dt.from_np(_np.dtype(dtype))
        args.append(nc.dram_tensor(f"out_{i}_dram", shape, dt, kind="ExternalOutput").ap())
    four_layer_gnn_kernel(nc, *args)
    r = _run(nc, [arrays], core_ids=[0])
    return r.results[0]["out_0_dram"]
```
